# Optimizing a Trainium2 kernel written in Bass

```python
import numpy as np
import jax
import jax.numpy as jnp

def _softmax(x, axis=-1):
    return jax.nn.softmax(x, axis=axis)

def _gelu(x):
    return jax.nn.gelu(x, approximate=True)

def _silu(x):
    return jax.nn.silu(x)

def _sigmoid(x):
    return jax.nn.sigmoid(x)

def _layernorm(x, axis=-1, eps=1e-05):
    m = jnp.mean(x, axis=axis, keepdims=True)
    v = jnp.var(x, axis=axis, keepdims=True)
    return (x - m) / jnp.sqrt(v + eps)

def _scatter_add(tgt, idx, src, axis=0):
    return tgt.at[idx].add(src)

def _segment_sum(src, seg, n):
    return jax.ops.segment_sum(src, seg, n)
kernel_name = 'mk_seq_preln_d2_jaxref_r4_0a4b6d'

def setup_inputs(seed: int=0):
    np.random.seed(seed)
    _w = jnp.asarray

    def _L0_attn_setup():
        import jax, jax.numpy as jnp
        import numpy as np
        HEADS = 16
        DIM_HEAD = 64
        SEG = 32
        SCALE = DIM_HEAD ** (-0.5)
        INNER = HEADS * DIM_HEAD

        def elu1(x):
            return jax.nn.elu(x) + 1.0

        def rope(t, pos):
            d = t.shape[-1]
            freqs = 10000.0 ** (-jnp.arange(0, d, 2, dtype=jnp.float32) / d)
            ang = pos[:, None] * freqs
            cos = jnp.repeat(jnp.cos(ang), 2, axis=-1)
            sin = jnp.repeat(jnp.sin(ang), 2, axis=-1)
            t2 = t.reshape(t.shape[:-1] + (d // 2, 2))
            rot = jnp.stack((-t2[..., 1], t2[..., 0]), axis=-1).reshape(t.shape)
            return t * cos + rot * sin

        def _reference_tuple_inner(x, w_qkv, w_out, ln_g, ln_b, mem_beta):
            B, N, D = x.shape
            mu = x.mean(-1, keepdims=True)
            var = x.var(-1, keepdims=True)
            xn = (x - mu) / jnp.sqrt(var + 1e-05) * ln_g + ln_b
            qkv = xn @ w_qkv
            q, k, v = jnp.split(qkv, 3, axis=-1)

            def to_heads(t):
                return t.reshape(B, N, HEADS, DIM_HEAD).transpose(0, 2, 1, 3)
            q, k, v = map(to_heads, (q, k, v))
            next_k, next_v = (k, v)
            pos = jnp.arange(N, dtype=jnp.float32)
            qr, kr = (rope(q, pos), rope(k, pos))
            W = N // SEG

            def to_segs(t):
                return t.reshape(B, HEADS, W, SEG, DIM_HEAD).transpose(2, 0, 1, 3, 4)
            qs, ks, vs, qnope, knope = map(to_segs, (qr, kr, v, q, k))
            mask = jnp.tril(jnp.ones((SEG, SEG), bool))
            beta = jax.nn.sigmoid(mem_beta)
            mem0 = jnp.zeros((B, HEADS, DIM_HEAD, DIM_HEAD), x.dtype)
            z0 = jnp.full((B, HEADS, DIM_HEAD), 1e-06, x.dtype)

            def step(carry, inp):
                mem, z = carry
                q_s, k_s, v_s, qn_s, kn_s = inp
                scores = jnp.einsum('bhnd,bhmd->bhnm', q_s, k_s) * SCALE
                scores = jnp.where(mask, scores, -jnp.inf)
                sdpa = jnp.einsum('bhnm,bhmd->bhnd', jax.nn.softmax(scores, axis=-1), v_s)
                sq = elu1(qn_s)
                num = jnp.einsum('bhnk,bhkv->bhnv', sq, mem)
                den = jnp.einsum('bhnk,bhk->bhn', sq, z)[..., None]
                mem_out = num / (den + 1e-06)
                out = beta * mem_out + (1.0 - beta) * sdpa
                sk = elu1(kn_s)
                prev_v = jnp.einsum('bhnk,bhkv->bhnv', sk, mem) / jnp.einsum('bhnk,bhk->bhn', sk, z)[..., None]
                mem = mem + jnp.einsum('bhnk,bhnv->bhkv', sk, v_s - prev_v)
                z = z + sk.sum(axis=2)
                return ((mem, z), out)
            _, outs = jax.lax.scan(step, (mem0, z0), (qs, ks, vs, qnope, knope))
            o = outs.transpose(1, 0, 3, 2, 4).reshape(B, N, INNER)
            out = o @ w_out
            return (out, next_k, next_v)
        key = jax.random.key(seed)
        k1, k2, k3 = jax.random.split(key, 3)
        B, N, D = (4, 1024, 256)
        x = jax.random.normal(k1, (B, N, D), dtype=jnp.float32)
        w_qkv = jax.random.normal(k2, (D, 3 * INNER), dtype=jnp.float32) * 0.02
        w_out = jax.random.normal(k3, (INNER, D), dtype=jnp.float32) * 0.02
        ln_g = jnp.ones((D,), jnp.float32)
        ln_b = jnp.zeros((D,), jnp.float32)
        mem_beta = jnp.zeros((1, HEADS, 1, 1), jnp.float32)
        return {'x': x, 'w_qkv': w_qkv, 'w_out': w_out, 'ln_g': ln_g, 'ln_b': ln_b, 'mem_beta': mem_beta}
    _L0_attn_in = _L0_attn_setup()

    def _L0_ffn_setup():
        import jax, jax.numpy as jnp
        import numpy as np
        E, H, I = (8, 256, 128)
        NG, TKG, TOPK = (4, 2, 4)
        SCALE = 2.5

        def _mlp(x, wg, wu, wd):
            return jax.nn.silu(x @ wg) * (x @ wu) @ wd
        key = jax.random.key(seed)
        ks = jax.random.split(key, 8)
        s = 0.02
        return {'hidden_states': jax.random.normal(ks[0], (32, 64, H), jnp.float32), 'gate_w': jax.random.normal(ks[1], (E, H), jnp.float32) * np.float32(np.sqrt(2.0 / H)), 'correction_bias': jnp.zeros((E,), jnp.float32), 'Wg': jax.random.normal(ks[2], (E, H, I), jnp.float32) * s, 'Wu': jax.random.normal(ks[3], (E, H, I), jnp.float32) * s, 'Wd': jax.random.normal(ks[4], (E, I, H), jnp.float32) * s, 'Wg_s': jax.random.normal(ks[5], (H, I), jnp.float32) * s, 'Wu_s': jax.random.normal(ks[6], (H, I), jnp.float32) * s, 'Wd_s': jax.random.normal(ks[7], (I, H), jnp.float32) * s}
    _L0_ffn_in = _L0_ffn_setup()

    def _L1_attn_setup():
        import jax, jax.numpy as jnp
        import numpy as np
        BSZ, T, D, H, WIN, N = (2, 512, 256, 16, 128, 64)
        DH = D // H
        DFF = 4 * D

        def _layernorm(x, g, b, eps=1e-05):
            mu = jnp.mean(x, axis=-1, keepdims=True)
            var = jnp.mean((x - mu) ** 2, axis=-1, keepdims=True)
            return (x - mu) * jax.lax.rsqrt(var + eps) * g + b
        key = jax.random.key(seed)
        ks = jax.random.split(key, 16)
        w = lambda k, shape: (jax.random.normal(k, shape) * 0.02).astype(jnp.float32)
        return {'x': jax.random.normal(ks[0], (BSZ, T, D), dtype=jnp.float32), 'ln1_g': jnp.ones((D,), jnp.float32), 'ln1_b': jnp.zeros((D,), jnp.float32), 'WQ': w(ks[1], (D, D)), 'bQ': jnp.zeros((D,), jnp.float32), 'WK': w(ks[2], (D, D)), 'bK': jnp.zeros((D,), jnp.float32), 'WV': w(ks[3], (D, D)), 'bV': jnp.zeros((D,), jnp.float32), 'WO': w(ks[4], (D, D)), 'bO': jnp.zeros((D,), jnp.float32), 'Wg': w(ks[5], (D, D)), 'bg': jnp.zeros((D,), jnp.float32), 'A': jax.random.uniform(ks[6], (N,), jnp.float32, -0.1, 0.1), 'Bw': w(ks[7], (D, N)), 'Cw': w(ks[8], (N, D)), 'ln2_g': jnp.ones((D,), jnp.float32), 'ln2_b': jnp.zeros((D,), jnp.float32), 'W1': w(ks[9], (D, DFF)), 'b1': jnp.zeros((DFF,), jnp.float32), 'W2': w(ks[10], (DFF, D)), 'b2': jnp.zeros((D,), jnp.float32)}
    _L1_attn_in = _L1_attn_setup()

    def _L1_ffn_setup():
        import jax, jax.numpy as jnp
        import numpy as np
        B, S, H, I, E = (2, 1024, 256, 128, 8)
        key = jax.random.key(seed)
        ks = jax.random.split(key, 5)
        scale_h = 1.0 / np.sqrt(H)
        scale_i = 1.0 / np.sqrt(I)
        return {'hidden_states': jax.random.normal(ks[0], (B, S, H), dtype=jnp.float32), 'gate_w': jax.random.normal(ks[1], (E, H), dtype=jnp.float32) * scale_h, 'w_gate': jax.random.normal(ks[2], (E, I, H), dtype=jnp.float32) * scale_h, 'w_up': jax.random.normal(ks[3], (E, I, H), dtype=jnp.float32) * scale_h, 'w_down': jax.random.normal(ks[4], (E, H, I), dtype=jnp.float32) * scale_i}
    _L1_ffn_in = _L1_ffn_setup()
    _d = {'L0_attn_x': _L0_attn_in['x'], 'L0_attn_w_qkv': _L0_attn_in['w_qkv'], 'L0_attn_w_out': _L0_attn_in['w_out'], 'L0_attn_ln_g': _L0_attn_in['ln_g'], 'L0_attn_ln_b': _L0_attn_in['ln_b'], 'L0_attn_mem_beta': _L0_attn_in['mem_beta'], 'L0_ffn_gate_w': _L0_ffn_in['gate_w'], 'L0_ffn_correction_bias': _L0_ffn_in['correction_bias'], 'L0_ffn_Wg': _L0_ffn_in['Wg'], 'L0_ffn_Wu': _L0_ffn_in['Wu'], 'L0_ffn_Wd': _L0_ffn_in['Wd'], 'L0_ffn_Wg_s': _L0_ffn_in['Wg_s'], 'L0_ffn_Wu_s': _L0_ffn_in['Wu_s'], 'L0_ffn_Wd_s': _L0_ffn_in['Wd_s'], 'L1_attn_ln1_g': _L1_attn_in['ln1_g'], 'L1_attn_ln1_b': _L1_attn_in['ln1_b'], 'L1_attn_WQ': _L1_attn_in['WQ'], 'L1_attn_bQ': _L1_attn_in['bQ'], 'L1_attn_WK': _L1_attn_in['WK'], 'L1_attn_bK': _L1_attn_in['bK'], 'L1_attn_WV': _L1_attn_in['WV'], 'L1_attn_bV': _L1_attn_in['bV'], 'L1_attn_WO': _L1_attn_in['WO'], 'L1_attn_bO': _L1_attn_in['bO'], 'L1_attn_Wg': _L1_attn_in['Wg'], 'L1_attn_bg': _L1_attn_in['bg'], 'L1_attn_A': _L1_attn_in['A'], 'L1_attn_Bw': _L1_attn_in['Bw'], 'L1_attn_Cw': _L1_attn_in['Cw'], 'L1_attn_ln2_g': _L1_attn_in['ln2_g'], 'L1_attn_ln2_b': _L1_attn_in['ln2_b'], 'L1_attn_W1': _L1_attn_in['W1'], 'L1_attn_b1': _L1_attn_in['b1'], 'L1_attn_W2': _L1_attn_in['W2'], 'L1_attn_b2': _L1_attn_in['b2'], 'L1_ffn_gate_w': _L1_ffn_in['gate_w'], 'L1_ffn_w_gate': _L1_ffn_in['w_gate'], 'L1_ffn_w_up': _L1_ffn_in['w_up'], 'L1_ffn_w_down': _L1_ffn_in['w_down']}
    _x0 = _d['L0_attn_x']
    _d['L0_attn_x'] = jax.random.normal(jax.random.fold_in(jax.random.key(seed), 1), (16, 512, 256), dtype=_x0.dtype)
    del _x0
    return _d

def reference(L0_attn_x, L0_attn_w_qkv, L0_attn_w_out, L0_attn_ln_g, L0_attn_ln_b, L0_attn_mem_beta, L0_ffn_gate_w, L0_ffn_correction_bias, L0_ffn_Wg, L0_ffn_Wu, L0_ffn_Wd, L0_ffn_Wg_s, L0_ffn_Wu_s, L0_ffn_Wd_s, L1_attn_ln1_g, L1_attn_ln1_b, L1_attn_WQ, L1_attn_bQ, L1_attn_WK, L1_attn_bK, L1_attn_WV, L1_attn_bV, L1_attn_WO, L1_attn_bO, L1_attn_Wg, L1_attn_bg, L1_attn_A, L1_attn_Bw, L1_attn_Cw, L1_attn_ln2_g, L1_attn_ln2_b, L1_attn_W1, L1_attn_b1, L1_attn_W2, L1_attn_b2, L1_ffn_gate_w, L1_ffn_w_gate, L1_ffn_w_up, L1_ffn_w_down):

    def _L0_attn_ref(x, w_qkv, w_out, ln_g, ln_b, mem_beta):
        import jax, jax.numpy as jnp
        import numpy as np
        HEADS = 16
        DIM_HEAD = 64
        SEG = 32
        SCALE = DIM_HEAD ** (-0.5)
        INNER = HEADS * DIM_HEAD

        def elu1(x):
            return jax.nn.elu(x) + 1.0

        def rope(t, pos):
            d = t.shape[-1]
            freqs = 10000.0 ** (-jnp.arange(0, d, 2, dtype=jnp.float32) / d)
            ang = pos[:, None] * freqs
            cos = jnp.repeat(jnp.cos(ang), 2, axis=-1)
            sin = jnp.repeat(jnp.sin(ang), 2, axis=-1)
            t2 = t.reshape(t.shape[:-1] + (d // 2, 2))
            rot = jnp.stack((-t2[..., 1], t2[..., 0]), axis=-1).reshape(t.shape)
            return t * cos + rot * sin

        def _reference_tuple_inner(x, w_qkv, w_out, ln_g, ln_b, mem_beta):
            B, N, D = x.shape
            mu = x.mean(-1, keepdims=True)
            var = x.var(-1, keepdims=True)
            xn = (x - mu) / jnp.sqrt(var + 1e-05) * ln_g + ln_b
            qkv = xn @ w_qkv
            q, k, v = jnp.split(qkv, 3, axis=-1)

            def to_heads(t):
                return t.reshape(B, N, HEADS, DIM_HEAD).transpose(0, 2, 1, 3)
            q, k, v = map(to_heads, (q, k, v))
            next_k, next_v = (k, v)
            pos = jnp.arange(N, dtype=jnp.float32)
            qr, kr = (rope(q, pos), rope(k, pos))
            W = N // SEG

            def to_segs(t):
                return t.reshape(B, HEADS, W, SEG, DIM_HEAD).transpose(2, 0, 1, 3, 4)
            qs, ks, vs, qnope, knope = map(to_segs, (qr, kr, v, q, k))
            mask = jnp.tril(jnp.ones((SEG, SEG), bool))
            beta = jax.nn.sigmoid(mem_beta)
            mem0 = jnp.zeros((B, HEADS, DIM_HEAD, DIM_HEAD), x.dtype)
            z0 = jnp.full((B, HEADS, DIM_HEAD), 1e-06, x.dtype)

            def step(carry, inp):
                mem, z = carry
                q_s, k_s, v_s, qn_s, kn_s = inp
                scores = jnp.einsum('bhnd,bhmd->bhnm', q_s, k_s) * SCALE
                scores = jnp.where(mask, scores, -jnp.inf)
                sdpa = jnp.einsum('bhnm,bhmd->bhnd', jax.nn.softmax(scores, axis=-1), v_s)
                sq = elu1(qn_s)
                num = jnp.einsum('bhnk,bhkv->bhnv', sq, mem)
                den = jnp.einsum('bhnk,bhk->bhn', sq, z)[..., None]
                mem_out = num / (den + 1e-06)
                out = beta * mem_out + (1.0 - beta) * sdpa
                sk = elu1(kn_s)
                prev_v = jnp.einsum('bhnk,bhkv->bhnv', sk, mem) / jnp.einsum('bhnk,bhk->bhn', sk, z)[..., None]
                mem = mem + jnp.einsum('bhnk,bhnv->bhkv', sk, v_s - prev_v)
                z = z + sk.sum(axis=2)
                return ((mem, z), out)
            _, outs = jax.lax.scan(step, (mem0, z0), (qs, ks, vs, qnope, knope))
            o = outs.transpose(1, 0, 3, 2, 4).reshape(B, N, INNER)
            out = o @ w_out
            return (out, next_k, next_v)
        return _reference_tuple_inner(x, w_qkv, w_out, ln_g, ln_b, mem_beta)[0]

    def _L0_ffn_ref(hidden_states, gate_w, correction_bias, Wg, Wu, Wd, Wg_s, Wu_s, Wd_s):
        import jax, jax.numpy as jnp
        import numpy as np
        E, H, I = (8, 256, 128)
        NG, TKG, TOPK = (4, 2, 4)
        SCALE = 2.5

        def _mlp(x, wg, wu, wd):
            return jax.nn.silu(x @ wg) * (x @ wu) @ wd
        B, T, _ = hidden_states.shape
        x = hidden_states.reshape(-1, H)
        N = x.shape[0]
        logits = x @ gate_w.T
        scores = jax.nn.sigmoid(logits)
        scores_c = scores + correction_bias
        grp = scores_c.reshape(N, NG, E // NG)
        group_scores = jnp.sum(jax.lax.top_k(grp, 2)[0], axis=-1)
        grp_idx = jax.lax.top_k(group_scores, TKG)[1]
        group_mask = jnp.zeros_like(group_scores).at[jnp.arange(N)[:, None], grp_idx].set(1.0)
        score_mask = jnp.repeat(group_mask, E // NG, axis=-1) > 0.5
        scores_for_choice = jnp.where(score_mask, scores_c, 0.0)
        topk_idx = jax.lax.top_k(scores_for_choice, TOPK)[1]
        topk_w = jnp.take_along_axis(scores, topk_idx, axis=-1)
        topk_w = topk_w / (jnp.sum(topk_w, axis=-1, keepdims=True) + 1e-20)
        topk_w = topk_w * SCALE
        cw = jnp.sum(jax.nn.one_hot(topk_idx, E, dtype=topk_w.dtype) * topk_w[..., None], axis=1)
        g = jnp.einsum('nh,ehi->eni', x, Wg)
        u = jnp.einsum('nh,ehi->eni', x, Wu)
        y = jnp.einsum('eni,eih->enh', jax.nn.silu(g) * u, Wd)
        routed = jnp.einsum('enh,ne->nh', y, cw)
        out = routed + _mlp(x, Wg_s, Wu_s, Wd_s)
        return out.reshape(B, T, H)

    def _L1_attn_ref(x, ln1_g, ln1_b, WQ, bQ, WK, bK, WV, bV, WO, bO, Wg, bg, A, Bw, Cw, ln2_g, ln2_b, W1, b1, W2, b2):
        import jax, jax.numpy as jnp
        import numpy as np
        BSZ, T, D, H, WIN, N = (2, 512, 256, 16, 128, 64)
        DH = D // H
        DFF = 4 * D

        def _layernorm(x, g, b, eps=1e-05):
            mu = jnp.mean(x, axis=-1, keepdims=True)
            var = jnp.mean((x - mu) ** 2, axis=-1, keepdims=True)
            return (x - mu) * jax.lax.rsqrt(var + eps) * g + b
        B, Tlen, d = x.shape
        h = _layernorm(x, ln1_g, ln1_b)

        def heads(t):
            return t.reshape(B, Tlen, H, DH).transpose(0, 2, 1, 3)
        q = heads(h @ WQ + bQ)
        k = heads(h @ WK + bK)
        v = heads(h @ WV + bV)
        scores = jnp.einsum('bhqd,bhkd->bhqk', q, k) / jnp.sqrt(jnp.float32(DH))
        i = jnp.arange(Tlen)
        diff = i[:, None] - i[None, :]
        allowed = (diff >= 0) & (diff < WIN)
        scores = jnp.where(allowed, scores, -jnp.inf)
        attn = jax.nn.softmax(scores, axis=-1)
        ao = jnp.einsum('bhqk,bhkd->bhqd', attn, v)
        ao = ao.transpose(0, 2, 1, 3).reshape(B, Tlen, d)
        attn_out = ao @ WO + bO
        u = h @ Bw

        def step(s, u_t):
            s = A * s + u_t
            return (s, s)
        _, states = jax.lax.scan(step, jnp.zeros((B, N), x.dtype), jnp.swapaxes(u, 0, 1))
        ssm_out = jnp.swapaxes(states, 0, 1) @ Cw
        g = jax.nn.sigmoid(h @ Wg + bg)
        x1 = x + g * attn_out + (1.0 - g) * ssm_out
        h2 = _layernorm(x1, ln2_g, ln2_b)
        mlp = jax.nn.gelu(h2 @ W1 + b1, approximate=False) @ W2 + b2
        return x1 + mlp

    def _L1_ffn_ref(hidden_states, gate_w, w_gate, w_up, w_down):
        import jax, jax.numpy as jnp
        import numpy as np
        B, S, H, I, E = (2, 1024, 256, 128, 8)
        b, s, h = hidden_states.shape
        x = hidden_states.reshape(-1, h)
        logits = x @ gate_w.T
        top_v = jnp.max(logits, axis=-1)
        sel = jnp.argmax(logits, axis=-1)
        rw = jax.nn.sigmoid(top_v)
        out = jnp.zeros_like(x)
        n_exp = gate_w.shape[0]
        for e in range(n_exp):
            mask = (sel == e).astype(x.dtype)
            xs = x * (rw * mask)[:, None]
            g = xs @ w_gate[e].T
            u = xs @ w_up[e].T
            out = out + u * jax.nn.silu(g) @ w_down[e].T
        return out.reshape(b, s, h)
    x = L0_attn_x
    x = x + _L0_attn_ref(_layernorm(x, axis=-1), L0_attn_w_qkv, L0_attn_w_out, L0_attn_ln_g, L0_attn_ln_b, L0_attn_mem_beta)
    x = x + _L0_ffn_ref(_layernorm(x, axis=-1), L0_ffn_gate_w, L0_ffn_correction_bias, L0_ffn_Wg, L0_ffn_Wu, L0_ffn_Wd, L0_ffn_Wg_s, L0_ffn_Wu_s, L0_ffn_Wd_s)
    x = x + _L1_attn_ref(_layernorm(x, axis=-1), L1_attn_ln1_g, L1_attn_ln1_b, L1_attn_WQ, L1_attn_bQ, L1_attn_WK, L1_attn_bK, L1_attn_WV, L1_attn_bV, L1_attn_WO, L1_attn_bO, L1_attn_Wg, L1_attn_bg, L1_attn_A, L1_attn_Bw, L1_attn_Cw, L1_attn_ln2_g, L1_attn_ln2_b, L1_attn_W1, L1_attn_b1, L1_attn_W2, L1_attn_b2)
    x = x + _L1_ffn_ref(_layernorm(x, axis=-1), L1_ffn_gate_w, L1_ffn_w_gate, L1_ffn_w_up, L1_ffn_w_down)
    return x

_drawn_inputs = setup_inputs


def setup_inputs(seed=0):
    import zlib

    import numpy as np

    out = dict(_drawn_inputs(seed))
    spreads = {'L0_attn_ln_g': (1.0, 0.6),
     'L0_attn_ln_b': (0.0, 0.1),
     'L0_attn_mem_beta': (0.0, 0.8),
     'L0_ffn_correction_bias': (0.0, 0.548),
     'L1_attn_ln1_g': (1.0, 0.6),
     'L1_attn_ln1_b': (0.0, 0.739),
     'L1_attn_bQ': (0.0, 0.8),
     'L1_attn_bK': (0.0, 0.8),
     'L1_attn_bV': (0.0, 0.418),
     'L1_attn_bO': (0.0, 0.1),
     'L1_attn_bg': (0.0, 0.8),
     'L1_attn_ln2_g': (1.0, 0.6),
     'L1_attn_ln2_b': (0.0, 0.499),
     'L1_attn_b1': (0.0, 0.278),
     'L1_attn_b2': (0.0, 0.1)}
    factors = {'L0_ffn_gate_w': 2.944,
     'L0_ffn_Wg_s': 2.696,
     'L0_ffn_Wu_s': 2.711,
     'L0_ffn_Wd_s': 2.752,
     'L1_attn_WQ': 8.0,
     'L1_attn_WK': 8.0,
     'L1_attn_WV': 6.061,
     'L1_attn_WO': 3.006,
     'L1_attn_Wg': 4.401,
     'L1_attn_A': 8.0}
    for name, (base, spread) in spreads.items():
        noise = np.random.default_rng([zlib.crc32(name.encode()), seed]).standard_normal(out[name].shape)
        drawn = base * np.exp(spread * noise) if base else spread * noise
        out[name] = jnp.asarray(drawn.astype(out[name].dtype))
    for name, factor in factors.items():
        out[name] = (out[name] * factor).astype(out[name].dtype)
    return out
```

```python
from contextlib import ExitStack
import concourse.bass as bass
from concourse import mybir


F32 = mybir.dt.float32
F32R = mybir.dt.float32r
BF16 = mybir.dt.bfloat16
ALU = mybir.AluOpType
ACT = mybir.ActivationFunctionType
AX = mybir.AxisListType
P = 128
D = 256
DC = D // P
SEQ = 512
T = SEQ // P
NSEQ = 16
EPS = 1e-5


class Order:

    def __init__(self, eng, sem):
        self.eng, self.sem, self.n, self.base, self.per = eng, sem, 0, 0, 0

    def link(self, ins):
        ins.then_inc(self.sem, 1)
        self.n += 1
        self.eng.wait_ge(self.sem, self.base + self.n)

    def step(self, it):
        if isinstance(it, int) and it == 0:
            self.start = self.n
        elif not self.per:
            self.per = self.n
        if self.per:
            self.base = self.start + it * self.per
        else:
            self.base = self.start
        self.n = 0


def last_step(it):
    return isinstance(it, int) and it == NSEQ - 1


def first_step(it):
    return isinstance(it, int) and it == 0


def steps(eng, body):
    body(0, 0)
    with eng.Fori(0, NSEQ // 2 - 1) as turn:
        body(turn * 2 + 1, 1)
        body(turn * 2 + 2, 0)
    body(NSEQ - 1, 1)


def sequence(v, it):
    return v[bass.ds(it, 1)].rearrange("a p t d -> p (a t) d")


def three(nc, out, w, x, start, stop):
    nc.tensor.matmul(out, w[0], x[0], start=start, stop=False)
    nc.tensor.matmul(out, w[1], x[0], start=False, stop=False)
    return nc.tensor.matmul(out, w[0], x[1], start=False, stop=stop)


def moe_phase(nc, name, src, dst, wg_d, wu_d, wd_d, gate_d, bias_d, lower_d, half_d, ident_d, shared):
    E = wg_d.shape[1]
    E0 = 1 if shared else 0
    NE = E - E0
    NT = 1 if shared else 2
    YB = T * D // SEQ
    BT = T // YB
    AHEAD = 2
    src_v = src.rearrange("(n t p) d -> n p t d", t=T, p=P)
    dst_v = dst.rearrange("(n t p) d -> n p t d", t=T, p=P)
    with ExitStack() as ctx:
        def sb(nm, shape, dt=F32):
            return ctx.enter_context(nc.sbuf_tensor(f"{name}_{nm}", shape, dt))

        def ps(nm, shape):
            return ctx.enter_context(nc.psum_tensor(f"{name}_{nm}", shape, F32))

        def sem(nm):
            return ctx.enter_context(nc.semaphore(f"{name}_{nm}"))

        wgu_raw = sb("wgu_raw", [P, 2, E * DC * P])
        wd_raw = sb("wd_raw", [P, E * D])
        gate = sb("gate", [P, DC, NE])
        wgu_hi = sb("wgu_hi", [P, 2, E * DC * P], F32R)
        wgu_lo = sb("wgu_lo", [P, 2, E * DC * P], F32R)
        wd_hi = sb("wd_hi", [P, E, D], F32R)
        wd_lo = sb("wd_lo", [P, E, D], F32R)
        bias = sb("bias", [P, NE])
        lower = sb("lower", [P, NE, NE])
        half = sb("half", [P, T])
        eps = sb("eps", [P, T])
        ident = sb("ident", [P, P])
        x_in = sb("x_in", [P, T, D])
        acc = sb("acc", [P, T, D])
        xn = sb("xn", [P, T, D])
        xT = sb("xT", [P, DC, SEQ])
        xT_hi = sb("xT_hi", [P, 2, DC, SEQ], F32R)
        xT_lo = sb("xT_lo", [P, 2, DC, SEQ], F32R)
        stats = sb("stats", [P, T, 6])
        mv = sb("mv", [P, T, 2])
        var = sb("var", [P, T])
        rstd = sb("rstd", [P, T])
        carrier = sb("carrier", [P, 1])
        s_sb = sb("s_sb", [P, 2, SEQ])
        h_sb = sb("h_sb", [P, 2, SEQ])
        h_hi = sb("h_hi", [P, 2, SEQ], F32R)
        h_lo = sb("h_lo", [P, 2, SEQ], F32R)
        score = sb("score", [P, T, NE])
        score_c = sb("score_c", [P, T, NE])
        top = sb("top", [P, T])
        rw = sb("rw", [P, T])
        group = sb("group", [P, T, NE // 2])
        wins = sb("wins", [P, T, NE * NE])
        ties = sb("ties", [P, T, NE * NE])
        rank = sb("rank", [P, T, NE])
        total = sb("total", [P, T])
        cw = sb("cw", [P, 2, T, NE])

        xT_ps = ps("xT_ps", [P, DC, SEQ])
        gu_ps = ps("gu_ps", [P, 2, 2, SEQ])
        y_ps = ps("y_ps", [P, T, D])
        logits = xT_ps[:, 0, 0:T * NE].rearrange("p (t e) -> p t e", e=NE)

        loaded = sem("loaded")
        split = sem("split")
        x_loaded = sem("x_loaded")
        var_ready = sem("var_ready")
        rstd_ready = sem("rstd_ready")
        xn_ready = sem("xn_ready")
        xT_in_psum = sem("xT_in_psum")
        xT_ready = sem("xT_ready")
        hi_ready = sem("hi_ready")
        lo_ready = sem("lo_ready")
        logits_ready = sem("logits_ready")
        top_ready = sem("top_ready")
        sig_ready = sem("sig_ready")
        routed = sem("routed")
        gu_ready = sem("gu_ready")
        silu_ready = sem("silu_ready")
        h_ready = sem("h_ready")
        hhi_ready = sem("hhi_ready")
        hlo_ready = sem("hlo_ready")
        y_ready = sem("y_ready")
        acc_done = sem("acc_done")
        stored = sem("stored")
        dve_order = sem("dve_order")
        pool_order = sem("pool_order")
        LOADS = 8 if shared else 7

        def slot(par, e):
            return (par * E + e) % 2

        block = ctx.enter_context(nc.Block())

        @block.sync
        def _(sp):
            sp.dma_start(x_in[:], src_v[0]).then_inc(x_loaded, 16)
            sp.dma_start(wgu_raw[:, 0, :], wg_d.rearrange("p e c i -> p (e c i)")).then_inc(loaded, 16)
            sp.dma_start(wgu_raw[:, 1, :], wu_d.rearrange("p e c i -> p (e c i)")).then_inc(loaded, 16)
            sp.dma_start(wd_raw[:], wd_d.rearrange("p e d -> p (e d)")).then_inc(loaded, 16)
            sp.dma_start(gate[:], gate_d).then_inc(loaded, 16)
            sp.dma_start(lower[:], lower_d).then_inc(loaded, 16)
            sp.dma_start(half[:], half_d).then_inc(loaded, 16)
            sp.dma_start(ident[:], ident_d).then_inc(loaded, 16)
            if shared:
                sp.dma_start(bias[:], bias_d).then_inc(loaded, 16)

            def body(it, par):
                if not last_step(it):
                    sp.wait_ge(acc_done, it * T * E + T)
                    sp.dma_start(x_in[:], sequence(src_v, it + 1)).then_inc(x_loaded, 16)
                sp.wait_ge(acc_done, (it + 1) * T * E)
                sp.dma_start(sequence(dst_v, it), acc[:]).then_inc(stored, 16)

            steps(sp, body)
            sp.wait_ge(stored, 16 * NSEQ)

        @block.gpsimd
        def _(pool):
            order = Order(pool, pool_order)
            pool.wait_ge(loaded, 16 * LOADS)
            order.link(nc.gpsimd.memset(eps[:], EPS))

            def body(it, par):
                order.step(it)
                pool.wait_ge(var_ready, it + 1)
                order.link(nc.gpsimd.tensor_tensor(var[:], mv[:, :, 1], eps[:], ALU.add))
                nc.gpsimd.tensor_tensor(rstd[:], var[:], half[:], ALU.pow).then_inc(rstd_ready, 1)

            steps(pool, body)

        @block.scalar
        def _(act):
            def evacuate(it, k):
                act.wait_ge(xT_in_psum, it * NT + k + 1)
                if k:
                    act.wait_ge(logits_ready, it + 1)
                elif not first_step(it):
                    act.wait_ge(lo_ready, it)
                nc.scalar.copy(xT[:], xT_ps[:]).then_inc(xT_ready, 1)

            def scores(it):
                if shared:
                    act.wait_ge(logits_ready, it + 1)
                    if not first_step(it):
                        act.wait_ge(routed, it)
                    nc.scalar.activation(score[:], logits, ACT.Sigmoid).then_inc(sig_ready, 1)
                else:
                    act.wait_ge(top_ready, it + 1)
                    nc.scalar.activation(rw[:], top[:], ACT.Sigmoid).then_inc(sig_ready, 1)

            def hi_copy(it, par):
                act.wait_ge(xT_ready, (it + 1) * NT)
                if not (isinstance(it, int) and it < 2):
                    act.wait_ge(gu_ready, (it - 1) * E)
                nc.scalar.copy(xT_hi[:, par], xT[:]).then_inc(hi_ready, 1)

            def silu(it, par, e):
                k = slot(par, e)
                act.wait_ge(gu_ready, it * E + e + 1)
                if not (first_step(it) and e < 2):
                    act.wait_ge(h_ready, it * E + e - 1)
                nc.scalar.activation(s_sb[:, k, :], gu_ps[:, k, 0, :], ACT.Silu).then_inc(silu_ready, 1)

            def h_hi_copy(it, par, e):
                k = slot(par, e)
                act.wait_ge(h_ready, it * E + e + 1)
                if not (first_step(it) and e < 2):
                    act.wait_ge(y_ready, (it * E + e - 1) * YB)
                nc.scalar.copy(h_hi[:, k, :], h_sb[:, k, :]).then_inc(hhi_ready, 1)

            act.wait_ge(loaded, 16 * LOADS)
            nc.scalar.copy(wgu_hi[:], wgu_raw[:])
            nc.scalar.copy(wd_hi[:].rearrange("p e d -> p (e d)"), wd_raw[:]).then_inc(split, 1)
            evacuate(0, 0)
            scores(0)
            if not shared:
                evacuate(0, 1)
            hi_copy(0, 0)

            def body(it, par):
                for e in range(E):
                    silu(it, par, e)
                    h_hi_copy(it, par, e)
                    if not last_step(it):
                        if e == 3:
                            evacuate(it + 1, 0)
                        if e == (4 if shared else 5):
                            scores(it + 1)
                        if e == 5:
                            if not shared:
                                evacuate(it + 1, 1)
                            hi_copy(it + 1, 1 - par)

            steps(act, body)

        @block.vector
        def _(dve):
            order = Order(dve, dve_order)
            link = order.link
            nc.vector.memset(carrier[:], 0.0)

            def stats_of(it):
                dve.wait_ge(x_loaded, (it + 1) * 16)
                for t in range(T):
                    last = nc.vector.bn_stats(stats[:, t, :], x_in[:, t, :])
                link(last)
                nc.vector.memset(carrier[:], 0.0)
                for t in range(T):
                    last = nc.vector.bn_aggr(mv[:, t, :], stats[:, t, :])
                last.then_inc(var_ready, 1)

            def normalise(it):
                dve.wait_ge(rstd_ready, it + 1)
                if not first_step(it):
                    dve.wait_ge(xT_in_psum, it * NT)
                for t in range(T):
                    last = nc.vector.tensor_scalar(xn[:, t, :], x_in[:, t, :], mv[:, t, 0:1], rstd[:, t:t + 1], ALU.subtract, ALU.mult)
                last.then_inc(xn_ready, 1)

            def ranks(a, n):
                for t in range(T):
                    me = a[:, t, 0:n].unsqueeze(2).to_broadcast([P, n, n])
                    other = a[:, t, 0:n].unsqueeze(1).to_broadcast([P, n, n])
                    nc.vector.tensor_tensor(wins[:, t, 0:n * n].rearrange("p (a b) -> p a b", b=n), other, me, ALU.is_gt)
                    last = nc.vector.tensor_tensor(ties[:, t, 0:n * n].rearrange("p (a b) -> p a b", b=n), other, me, ALU.is_equal)
                link(last)
                for t in range(T):
                    q = ties[:, t, 0:n * n].rearrange("p (a b) -> p a b", b=n)
                    last = nc.vector.tensor_tensor(q, q, lower[:, 0:n, 0:n], ALU.mult)
                link(last)
                w = wins[:, :, 0:n * n]
                link(nc.vector.tensor_tensor(w, w, ties[:, :, 0:n * n], ALU.add))
                link(nc.vector.tensor_reduce(rank[:, :, 0:n], w.rearrange("p t (a b) -> p t a b", b=n), AX.X, ALU.add))

            def route_top4(it, par):
                dve.wait_ge(sig_ready, it + 1)
                link(nc.vector.tensor_tensor(score_c[:], score[:], bias[:, :].unsqueeze(1).to_broadcast([P, T, NE]), ALU.add))
                pair = score_c[:].rearrange("p t (g k) -> p t g k", k=2)
                link(nc.vector.tensor_tensor(group[:], pair[:, :, :, 0], pair[:, :, :, 1], ALU.add))
                ranks(group, NE // 2)
                link(nc.vector.tensor_scalar(group[:], rank[:, :, 0:NE // 2], 2.0, None, ALU.is_lt))
                for k in range(2):
                    last = nc.vector.tensor_tensor(pair[:, :, :, k], pair[:, :, :, k], group[:], ALU.mult)
                link(last)
                ranks(score_c, NE)
                link(nc.vector.scalar_tensor_tensor(cw[:, par], rank[:], 4.0, score[:], ALU.is_lt, ALU.mult))
                link(nc.vector.tensor_reduce(total[:], cw[:, par], AX.X, ALU.add))
                link(nc.vector.tensor_scalar(total[:], total[:], 1e-20, None, ALU.add))
                link(nc.vector.reciprocal(total[:], total[:]))
                nc.vector.scalar_tensor_tensor(cw[:, par], cw[:, par], 2.5, total[:].unsqueeze(2).to_broadcast([P, T, NE]), ALU.mult, ALU.mult).then_inc(routed, 1)

            def route_top1(it, par):
                dve.wait_ge(logits_ready, it + 1)
                link(nc.vector.tensor_copy(score[:], logits))
                nc.vector.tensor_reduce(top[:], score[:], AX.X, ALU.max).then_inc(top_ready, 1)
                ranks(score, NE)
                link(nc.vector.tensor_scalar(cw[:, par], rank[:], 1.0, None, ALU.is_lt))

            def scale(it):
                dve.wait_ge(sig_ready, it + 1)
                dve.wait_ge(xT_in_psum, it * NT + 1)
                for t in range(T):
                    last = nc.vector.tensor_scalar(xn[:, t, :], xn[:, t, :], rw[:, t:t + 1], None, ALU.mult)
                last.then_inc(xn_ready, 1)

            def lo_sub(it, par):
                dve.wait_ge(hi_ready, it + 1)
                nc.vector.tensor_tensor(xT_lo[:, par], xT[:], xT_hi[:, par].bitcast(F32), ALU.subtract).then_inc(lo_ready, 1)

            def times_up(it, par, e):
                k = slot(par, e)
                dve.wait_ge(silu_ready, it * E + e + 1)
                if not (first_step(it) and e < 2):
                    dve.wait_ge(hhi_ready, it * E + e - 1)
                    dve.wait_ge(hlo_ready, it * E + e - 1)
                nc.vector.tensor_tensor(h_sb[:, k, :], s_sb[:, k, :], gu_ps[:, k, 1, :], ALU.mult).then_inc(h_ready, 1)

            def h_lo_sub(it, par, e):
                k = slot(par, e)
                dve.wait_ge(hhi_ready, it * E + e + 1)
                if not (first_step(it) and e < 2):
                    dve.wait_ge(y_ready, (it * E + e - 1) * YB)
                nc.vector.tensor_tensor(h_lo[:, k, :], h_sb[:, k, :], h_hi[:, k, :].bitcast(F32), ALU.subtract).then_inc(hlo_ready, 1)

            def accumulate(it, par, e):
                for t in range(T):
                    if t % BT == 0:
                        dve.wait_ge(y_ready, (it * E + e) * YB + t // BT + 1)
                    if e == 0 and t == 0 and not first_step(it):
                        dve.wait_ge(stored, it * 16)
                    if e and t == 0:
                        dve.wait_ge(acc_done, (it * E + e) * T)
                    into = x_in[:, t, :] if e == 0 else acc[:, t, :]
                    if e < E0:
                        nc.vector.tensor_tensor(acc[:, t, :], y_ps[:, t, :], into, ALU.add).then_inc(acc_done, 1)
                    else:
                        nc.vector.scalar_tensor_tensor(acc[:, t, :], y_ps[:, t, :], cw[:, par, t, e - E0:e - E0 + 1], into, ALU.mult, ALU.add).then_inc(acc_done, 1)

            stats_of(0)
            normalise(0)
            dve.wait_ge(split, 1)
            nc.vector.tensor_tensor(wgu_lo[:], wgu_raw[:], wgu_hi[:].bitcast(F32), ALU.subtract)
            nc.vector.tensor_tensor(wd_lo[:].rearrange("p e d -> p (e d)"), wd_raw[:], wd_hi[:].bitcast(F32).rearrange("p e d -> p (e d)"), ALU.subtract).then_inc(split, 1)
            if shared:
                route_top4(0, 0)
            else:
                route_top1(0, 0)
                scale(0)
            lo_sub(0, 0)

            def body(it, par):
                order.step(it)
                for e in range(E):
                    times_up(it, par, e)
                    if e:
                        accumulate(it, par, e - 1)
                    h_lo_sub(it, par, e)
                    if not last_step(it):
                        if e == 1:
                            stats_of(it + 1)
                        if e == 2:
                            normalise(it + 1)
                        if e == 5:
                            if shared:
                                route_top4(it + 1, 1 - par)
                            else:
                                route_top1(it + 1, 1 - par)
                                scale(it + 1)
                        if e == 6:
                            lo_sub(it + 1, 1 - par)
                accumulate(it, par, E - 1)

            steps(dve, body)

        @block.tensor
        def _(pe):
            wgu = [w[:].rearrange("p u (e c i) -> p u e c i", e=E, c=DC) for w in (wgu_hi, wgu_lo)]

            def transposes(it, k):
                pe.wait_ge(xn_ready, it * NT + k + 1)
                if k:
                    pe.wait_ge(top_ready, it + 1)
                elif not first_step(it):
                    pe.wait_ge(xT_ready, it * NT)
                    if shared:
                        pe.wait_ge(sig_ready, it)
                for t in range(T):
                    for c in range(DC):
                        last = nc.tensor.transpose(xT_ps[:, c, t * P:(t + 1) * P], xn[:, t, c * P:(c + 1) * P], ident[:])
                last.then_inc(xT_in_psum, 1)

            def router(it):
                pe.wait_ge(xT_ready, it * NT + 1)
                for t in range(T):
                    for c in range(DC):
                        last = nc.tensor.matmul(logits[:, t, :], xT[:, c, t * P:(t + 1) * P], gate[:, c, :], start=(c == 0), stop=(c == DC - 1))
                last.then_inc(logits_ready, 1)

            def gate_up(it, par, e):
                k = slot(par, e)
                if e == 0:
                    pe.wait_ge(lo_ready, it + 1)
                if not (first_step(it) and e < 2):
                    pe.wait_ge(h_ready, it * E + e - 1)
                for u in range(2):
                    for c in range(DC):
                        last = three(nc, gu_ps[:, k, u, :], [w[:, u, e, c, :] for w in wgu], (xT_hi[:, par, c, :], xT_lo[:, par, c, :]), c == 0, c == DC - 1)
                last.then_inc(gu_ready, 1)

            def down(it, par, e):
                k = slot(par, e)
                pe.wait_ge(hlo_ready, it * E + e + 1)
                for t in range(T):
                    if t % BT == 0 and not (first_step(it) and e == 0):
                        pe.wait_ge(acc_done, (it * E + e - 1) * T + t + BT)
                    tok = slice(t * P, (t + 1) * P)
                    last = three(nc, y_ps[:, t, :], (h_hi[:, k, tok], h_lo[:, k, tok]), (wd_hi[:, e, :], wd_lo[:, e, :]), True, True)
                    if t % BT == BT - 1:
                        last.then_inc(y_ready, 1)

            pe.wait_ge(loaded, 16 * LOADS)
            transposes(0, 0)
            router(0)
            if not shared:
                transposes(0, 1)
            pe.wait_ge(split, 2)
            for e in range(AHEAD):
                gate_up(0, 0, e)

            def body(it, par):
                for e in range(E):
                    if not last_step(it):
                        if e == 3:
                            transposes(it + 1, 0)
                        if e == 4:
                            router(it + 1)
                        if e == 6 and not shared:
                            transposes(it + 1, 1)
                    down(it, par, e)
                    if e + AHEAD < E:
                        gate_up(it, par, e + AHEAD)
                    elif not last_step(it):
                        gate_up(it + 1, 1 - par, e + AHEAD - E)

            steps(pe, body)


HEADS = 16
DH = 64
SEG = 32
SEGS = SEQ // SEG
SPT = P // SEG
PAIRS = HEADS // 2
GROUPS = 2
PU = PAIRS // GROUPS
HU = 2 * PU
GD = HU * DH
NORM = DH ** -0.5


def after(eng, sem, value):
    if not (isinstance(value, int) and value <= 0):
        eng.wait_ge(sem, value)


def attn0_phase(nc, x, out, wqk_d, wv_d, wo_d, lng_d, lnb_d, beta_rows_d, beta_heads_d, cos_d, sin_d, mask_d, sel_d, selbc_d, eps4_d, half_d, ident_d):
    x_v = x.rearrange("(n t p) d -> n p t d", t=T, p=P)
    out_v = out.rearrange("(n t p) d -> n p t d", t=T, p=P)
    with ExitStack() as ctx:
        def sb(nm, shape, dt=F32, c=ctx):
            return c.enter_context(nc.sbuf_tensor(f"a_{nm}", shape, dt))

        def ps(nm, shape):
            return ctx.enter_context(nc.psum_tensor(f"a_{nm}", shape, F32))

        def sem(nm):
            return ctx.enter_context(nc.semaphore(f"a_{nm}"))

        NQK = 2 * PAIRS * DC * P
        NV = DC * HEADS * DH
        NO = PAIRS * D
        wqk = [sb(f"wqk_{h}", [P, 2, PAIRS, DC, P], F32R) for h in ("hi", "lo")]
        wv = [sb(f"wv_{h}", [P, DC, HEADS * DH], F32R) for h in ("hi", "lo")]
        wo = [sb(f"wo_{h}", [P, PAIRS, D], F32R) for h in ("hi", "lo")]
        selbc = sb("selbc", [8, 2, P], F32R)
        loaded = sem("loaded")
        hi_split = sem("hi_split")
        lo_split = sem("lo_split")

        with ExitStack() as c1:
            wqk_raw = sb("wqk_raw", [P, NQK], c=c1)
            wv_raw = sb("wv_raw", [P, NV], c=c1)
            wo_raw = sb("wo_raw", [P, NO], c=c1)
            selbc_raw = sb("selbc_raw", [8, 2 * P], c=c1)
            block = c1.enter_context(nc.Block())
            flat = [(w[0][:].rearrange(r), w[1][:].rearrange(r), raw[:]) for w, raw, r in (
                (wqk, wqk_raw, "p a b c i -> p (a b c i)"), (wv, wv_raw, "p c i -> p (c i)"), (wo, wo_raw, "p j d -> p (j d)"))]

            @block.sync
            def _(sp):
                sp.dma_start(wqk_raw[:], wqk_d).then_inc(loaded, 16)
                sp.dma_start(wv_raw[:], wv_d).then_inc(loaded, 16)
                sp.dma_start(wo_raw[:], wo_d).then_inc(loaded, 16)
                sp.dma_start(selbc_raw[:], selbc_d).then_inc(loaded, 16)

            @block.scalar
            def _(act):
                act.wait_ge(loaded, 64)
                for hi, lo, raw in flat:
                    nc.scalar.copy(hi, raw).then_inc(hi_split, 1)

            @block.vector
            def _(dve):
                dve.wait_ge(loaded, 64)
                nc.vector.tensor_copy(selbc[:].rearrange("k a p -> k (a p)"), selbc_raw[:])
                for n, (hi, lo, raw) in enumerate(flat):
                    dve.wait_ge(hi_split, n + 1)
                    nc.vector.tensor_tensor(lo, raw, hi.bitcast(F32), ALU.subtract).then_inc(lo_split, 1)

        lng = sb("lng", [P, DC])
        lnb = sb("lnb", [P, DC])
        beta_rows = sb("beta_rows", [P, PAIRS])
        keep = sb("keep", [P, HEADS])
        cos = sb("cos", [P, SEQ])
        sin = sb("sin", [P, SEQ])
        mask = sb("mask", [P, SEG])
        sel = sb("sel", [P, 2, 4])
        eps4 = sb("eps4", [4, 1])
        half = sb("half", [P, T])
        eps = sb("eps", [P, T])
        ident = sb("ident", [P, P])
        ones = sb("ones", [P, SEGS])
        carrier = sb("carrier", [P, 1])

        x_ln = sb("x_ln", [P, T, D])
        x_res = sb("x_res", [P, T, D])
        acc = sb("acc", [P, T, D])
        xT = sb("xT", [P, DC, SEQ])
        xT_hi = sb("xT_hi", [P, DC, SEQ], F32R)
        xT_lo = sb("xT_lo", [P, DC, SEQ], F32R)
        stats = sb("stats", [P, T, 6])
        mv = sb("mv", [P, T, 2])
        lnt = sb("lnt", [P, 4, T])
        rstd = sb("rstd", [P, T])

        raw = sb("raw", [P, 2, SEQ])
        expo = sb("expo", [P, 2, SEQ])
        swap = sb("swap", [P, 2, SEQ])
        rope = sb("rope", [P, 2, SEQ])
        sT = sb("sT", [P, 2, SEQ])
        prod = sb("prod", [P, 2, SEQ])
        zin = sb("zin", [P, SEGS])
        z = sb("z", [P, SEGS])
        den = sb("den", [4, SEQ])
        den_r = sb("den_r", [P, SEQ // SEG])
        rec_r = sb("rec_r", [P, SEQ // SEG])
        rec_hi = sb("rec_hi", [P, SEQ // SEG], F32R)
        rec_lo = sb("rec_lo", [P, SEQ // SEG], F32R)
        rec8 = sb("rec8", [8, SEQ], F32R)

        sqn = sb("sqn", [P, GROUPS, PU, SEQ])
        skn = sb("skn", [P, GROUPS, PU, SEQ])
        sk = sb("sk", [P, GROUPS, T, GD])
        v = sb("v", [P, GROUPS, T, GD])
        s_all = sb("s_all", [P, GROUPS, T, HU * SEG])
        prob = sb("prob", [P, HU, SEG])
        smax = sb("smax", [P, HU])
        ssum = sb("ssum", [P, HU])
        pT = sb("pT", [P, HU, P])
        u = sb("u", [P, GD])
        mem = sb("mem", [P, PU, P])
        o_hi = sb("o_hi", [P, PU, P], F32R)
        o_lo = sb("o_lo", [P, PU, P], F32R)

        qk_ps = ps("qk_ps", [P, 2, SEQ])
        a_ps = ps("a_ps", [P, SEQ])
        b_ps = ps("b_ps", [P, SEQ])
        o_ps = ps("o_ps", [P, PU, P])
        prev_ps = ps("prev_ps", [P, GD])
        d_ps = ps("d_ps", [P, PU, P])
        y_ps = ps("y_ps", [P, SEQ])

        const_in = sem("const_in")
        setup = sem("setup")
        xln_in = sem("xln_in")
        xres_in = sem("xres_in")
        var_ready = sem("var_ready")
        rstd_ready = sem("rstd_ready")
        xn_ready = sem("xn_ready")
        xT_in_psum = sem("xT_in_psum")
        xT_ready = sem("xT_ready")
        xhi_ready = sem("xhi_ready")
        xlo_ready = sem("xlo_ready")
        qk_ready = sem("qk_ready")
        raw_ready = sem("raw_ready")
        exp_ready = sem("exp_ready")
        swapped = sem("swapped")
        v_in_psum = sem("v_in_psum")
        v_ready = sem("v_ready")
        s_ready = sem("s_ready")
        z_ready = sem("z_ready")
        prod_ready = sem("prod_ready")
        sk_in_psum = sem("sk_in_psum")
        sk_ready = sem("sk_ready")
        den_in_psum = sem("den_in_psum")
        den_ready = sem("den_ready")
        den_spread = sem("den_spread")
        rec_ready = sem("rec_ready")
        rec_rows = sem("rec_rows")
        bc_ready = sem("bc_ready")
        norm_done = sem("norm_done")
        sin_part = sem("sin_part")
        rope_ready = sem("rope_ready")
        sc_in_psum = sem("sc_in_psum")
        sc_ready = sem("sc_ready")
        sub_ready = sem("sub_ready")
        p_ready = sem("p_ready")
        pT_ready = sem("pT_ready")
        sdpa_done = sem("sdpa_done")
        prev_ready = sem("prev_ready")
        u_ready = sem("u_ready")
        d_ready = sem("d_ready")
        mem_ready = sem("mem_ready")
        o_ready = sem("o_ready")
        ohi_ready = sem("ohi_ready")
        olo_ready = sem("olo_ready")
        y_ready = sem("y_ready")
        acc_done = sem("acc_done")
        stored = sem("stored")
        dve_order = sem("dve_order")
        pool_order = sem("pool_order")

        NU = SEGS - 2
        NM = SEGS - 1
        CONSTS = 13
        block = ctx.enter_context(nc.Block())

        def units(eng, body):
            body(0)
            with eng.Fori(1, NSEQ - 1) as it:
                body(it)
            body(NSEQ - 1)

        def slots(it):
            for g in range(GROUPS):
                for t in range(T):
                    Z = (it * GROUPS + g) * T + t
                    it1, g1 = (it, 1) if g == 0 else (it + 1, 0)
                    yield g, t, Z, (None if g and last_step(it) else (it1, g1, t, Z + T))

        def buffers_free(j, Y):
            return Y - j - PU

        @block.sync
        def _(sp):
            for dst, src in ((lng, lng_d), (lnb, lnb_d), (cos, cos_d), (sin, sin_d), (mask, mask_d), (sel, sel_d), (eps4, eps4_d), (half, half_d), (ident, ident_d)):
                sp.dma_start(dst[:], src).then_inc(const_in, 16)
            sp.dma_start(beta_rows[0:64, :], beta_rows_d).then_inc(const_in, 16)
            sp.dma_start(keep[:], beta_heads_d).then_inc(const_in, 16)
            sp.dma_start(x_ln[:], x_v[0]).then_inc(xln_in, 16)
            sp.dma_start(x_res[:], x_v[0]).then_inc(xres_in, 16)

            def part1(it, g, j, Y):
                sp.wait_ge(raw_ready, Y + 1)
                for h in range(2):
                    for a in range(2):
                        to, fr = 64 * h + 32 * a, 64 * h + 32 * (1 - a)
                        sp.dma_start(swap[to:to + 32], raw[fr:fr + 32]).then_inc(swapped, 16)
                sp.wait_ge(den_ready, Y + 1)
                sp.dma_start(den_r[:], den[:].rearrange("r (c k) -> r c k", k=16)).then_inc(den_spread, 16)
                sp.wait_ge(rec_ready, Y + 1)
                sp.dma_start(rec8[0:4].bitcast(F32).rearrange("r (c k) -> r c k", k=16), rec_hi[:].bitcast(F32)).then_inc(rec_rows, 16)
                sp.dma_start(rec8[4:8].bitcast(F32).rearrange("r (c k) -> r c k", k=16), rec_lo[:].bitcast(F32)).then_inc(rec_rows, 16)

            def store(it, t, Z):
                sp.wait_ge(acc_done, Z)
                sp.dma_start(out_v[bass.ds(it, 1), :, t].rearrange("a p d -> p (a d)"), acc[:, t]).then_inc(stored, 16)

            for j in range(PU):
                part1(0, 0, j, j)

            def body(it):
                before = None if first_step(it) else sp.snap(it - 1)
                for g, t, Z, nxt in slots(it):
                    if nxt:
                        part1(*nxt)
                    if g == 0 and t == 0 and not last_step(it):
                        sp.wait_ge(xT_in_psum, it + 1)
                        sp.dma_start(x_ln[:], sequence(x_v, it + 1)).then_inc(xln_in, 16)
                    if g == 1 and t == 1 and not last_step(it):
                        sp.wait_ge(acc_done, it * 2 * T + T)
                        sp.dma_start(x_res[:], sequence(x_v, it + 1)).then_inc(xres_in, 16)
                    if g == 1 and t:
                        store(it, t - 1, Z)
                    if g == 0 and t == 0 and not first_step(it):
                        store(before, T - 1, Z)

            units(sp, body)
            sp.wait_ge(acc_done, NSEQ * 2 * T)
            sp.dma_start(out_v[NSEQ - 1, :, T - 1], acc[:, T - 1]).then_inc(stored, 16)
            sp.wait_ge(stored, 16 * NSEQ * T)

        @block.gpsimd
        def _(pool):
            order = Order(pool, pool_order)
            pool.wait_ge(const_in, 16 * 11)
            order.link(nc.gpsimd.memset(eps[:], EPS))

            def inverse_deviation(it):
                pool.wait_ge(var_ready, it + 1)
                order.link(nc.gpsimd.tensor_tensor(lnt[:, 0], mv[:, :, 1], eps[:], ALU.add))
                order.link(nc.gpsimd.tensor_tensor(lnt[:, 1], lnt[:, 0], half[:], ALU.pow))
                order.link(nc.gpsimd.tensor_tensor(lnt[:, 2], lnt[:, 1], lnt[:, 1], ALU.mult))
                order.link(nc.gpsimd.tensor_tensor(lnt[:, 0], lnt[:, 2], mv[:, :, 1], ALU.mult))
                order.link(nc.gpsimd.tensor_tensor(lnt[:, 2], lnt[:, 0], eps[:], ALU.add))
                order.link(nc.gpsimd.tensor_tensor(lnt[:, 3], lnt[:, 2], half[:], ALU.pow))
                nc.gpsimd.tensor_tensor(rstd[:], lnt[:, 1], lnt[:, 3], ALU.mult).then_inc(rstd_ready, 1)

            def part1(it, g, j, Y):
                pool.wait_ge(swapped, 64 * (Y + 1))
                nc.gpsimd.tensor_tensor(swap[:], swap[:], sin[:].unsqueeze(1).to_broadcast([P, 2, SEQ]), ALU.mult).then_inc(sin_part, 1)
                pool.wait_ge(z_ready, Y + 1)
                after(pool, den_in_psum, Y)
                four = lambda a: a[:].rearrange("p a (w k) -> p a w k", k=SEG)
                nc.gpsimd.tensor_tensor(four(prod), four(sT), z[:].unsqueeze(1).unsqueeze(3).to_broadcast([P, 2, SEGS, SEG]), ALU.mult).then_inc(prod_ready, 1)

            inverse_deviation(0)
            for j in range(PU):
                part1(0, 0, j, j)

            def body(it):
                order.step(it)
                for g, t, Z, nxt in slots(it):
                    if g == 0 and t == 3 and not last_step(it):
                        inverse_deviation(it + 1)
                    if nxt:
                        part1(*nxt)

            units(pool, body)

        @block.scalar
        def _(act):
            act.wait_ge(const_in, 16 * 11)
            nc.scalar.activation(beta_rows[0:64, :], beta_rows[0:64, :], ACT.Sigmoid).then_inc(setup, 1)
            nc.scalar.activation(keep[:], keep[:], ACT.Sigmoid).then_inc(setup, 1)

            def x_hi(it):
                act.wait_ge(xT_ready, it + 1)
                after(act, v_in_psum, it * 2 * PU)
                nc.scalar.copy(xT_hi[:], xT[:]).then_inc(xhi_ready, 1)

            def project(it, g, j, Y):
                act.wait_ge(qk_ready, Y + 1)
                after(act, rope_ready, Y)
                after(act, s_ready, Y)
                nc.scalar.copy(raw[:], qk_ps[:]).then_inc(raw_ready, 1)
                nc.scalar.activation(expo[:], qk_ps[:], ACT.Exp).then_inc(exp_ready, 1)

            def values(it, g, j, Y):
                act.wait_ge(v_in_psum, Y + 1)
                after(act, y_ready, buffers_free(j, Y))
                nc.scalar.copy(v[:, g, j], b_ps[:]).then_inc(v_ready, 1)

            def keys(it, g, j, Y):
                act.wait_ge(sk_in_psum, Y + 1)
                nc.scalar.copy(sk[:, g, :, j * P:(j + 1) * P], b_ps[:].rearrange("p (t i) -> p t i", t=T)).then_inc(sk_ready, 1)

            def denominators(it, g, j, Y):
                act.wait_ge(den_in_psum, Y + 1)
                after(act, den_spread, 16 * Y)
                nc.scalar.activation(den[:], a_ps[0:4, :], ACT.Identity, bias=eps4[:]).then_inc(den_ready, 1)

            x_hi(0)
            for j in range(PU):
                for f in (project, values, keys, denominators):
                    f(0, 0, j, j)

            def body(it):
                for g, t, Z, nxt in slots(it):
                    act.wait_ge(sub_ready, Z + 1)
                    after(act, pT_ready, Z)
                    nc.scalar.activation(prob[:], s_all[:, g, t].rearrange("p (h k) -> p h k", k=SEG), ACT.Exp).then_inc(p_ready, 1)
                    if nxt:
                        if g == 1 and t == 0:
                            x_hi(it + 1)
                        for f in (project, values, keys, denominators):
                            f(*nxt)
                    act.wait_ge(o_ready, Z + 1)
                    after(act, y_ready, Z)
                    nc.scalar.copy(o_hi[:], o_ps[:]).then_inc(ohi_ready, 1)

            units(act, body)

        @block.vector
        def _(dve):
            order = Order(dve, dve_order)
            link = order.link
            nc.vector.memset(carrier[:], 0.0)
            nc.vector.memset(zin[:], 1e-6)
            nc.vector.memset(ones[:], 1.0)
            nc.vector.memset(beta_rows[64:128, :], 1.0)
            nc.vector.memset(mem[:].rearrange("p j e -> p (j e)"), 0.0)
            nc.vector.memset(pT[:].rearrange("p h q -> p (h q)"), 0.0)
            dve.wait_ge(setup, 2)
            link(nc.vector.tensor_scalar(keep[:], keep[:], -1.0, 1.0, ALU.mult, ALU.add))

            def norm(it):
                dve.wait_ge(xln_in, 16 * (it + 1))
                for t in range(T):
                    last = nc.vector.bn_stats(stats[:, t], x_ln[:, t])
                link(last)
                nc.vector.memset(carrier[:], 0.0)
                for t in range(T):
                    last = nc.vector.bn_aggr(mv[:, t], stats[:, t])
                last.then_inc(var_ready, 1)

            def norm2(it):
                dve.wait_ge(rstd_ready, it + 1)
                for t in range(T):
                    last = nc.vector.tensor_scalar(x_ln[:, t], x_ln[:, t], mv[:, t, 0:1], rstd[:, t:t + 1], ALU.subtract, ALU.mult)
                last.then_inc(xn_ready, 1)

            def x_affine(it):
                dve.wait_ge(xT_in_psum, it + 1)
                for c in range(DC):
                    last = nc.vector.tensor_scalar(xT[:, c], qk_ps[:, c], lng[:, c:c + 1], lnb[:, c:c + 1], ALU.mult, ALU.add)
                last.then_inc(xT_ready, 1)
                dve.wait_ge(xhi_ready, it + 1)
                nc.vector.tensor_tensor(xT_lo[:], xT[:], xT_hi[:].bitcast(F32), ALU.subtract).then_inc(xlo_ready, 1)

            def elu(it, g, j, Y):
                dve.wait_ge(exp_ready, Y + 1)
                link(nc.vector.tensor_scalar(expo[:], expo[:], 1.0, None, ALU.min))
                after(dve, sk_in_psum, Y)
                after(dve, prod_ready, Y)
                nc.vector.scalar_tensor_tensor(sT[:], raw[:], 1.0, expo[:], ALU.add, ALU.max).then_inc(s_ready, 1)

            def rope_cos(it, g, j, Y):
                after(dve, sc_in_psum, Y)
                dve.wait_ge(raw_ready, Y + 1)
                link(nc.vector.tensor_tensor(rope[:], raw[:], cos[:].unsqueeze(1).to_broadcast([P, 2, SEQ]), ALU.mult))

            def memory_z(it, g, j, Y):
                dve.wait_ge(s_ready, Y + 1)
                link(nc.vector.tensor_reduce(zin[:, 1:SEGS], sT[:, 1, 0:(SEGS - 1) * SEG].rearrange("p (w k) -> p w k", k=SEG), AX.X, ALU.add))
                after(dve, prod_ready, Y)
                nc.vector.tensor_tensor_scan(z[:], ones[:], zin[:], 0.0, ALU.mult, ALU.add).then_inc(z_ready, 1)

            def rope_sum(it, g, j, Y):
                dve.wait_ge(sin_part, Y + 1)
                nc.vector.tensor_tensor(rope[:], rope[:], swap[:], ALU.add).then_inc(rope_ready, 1)

            def scores(it, g, j, Y):
                dve.wait_ge(sc_in_psum, Y + 1)
                for h in range(2):
                    k = slice((2 * j + h) * SEG, (2 * j + h + 1) * SEG)
                    last = nc.vector.scalar_tensor_tensor(
                        s_all[:, g, :, k], (a_ps, b_ps)[h][:, 0:T * SEG].rearrange("p (t k) -> p t k", t=T), NORM,
                        mask[:].unsqueeze(1).to_broadcast([P, T, SEG]), ALU.mult, ALU.add)
                last.then_inc(sc_ready, 1)

            def inverses(it, g, j, Y):
                p = g * PU + j
                dve.wait_ge(den_spread, 16 * (Y + 1))
                after(dve, rec_rows, 32 * Y)
                link(nc.vector.reciprocal(rec_r[:], den_r[:]))
                link(nc.vector.tensor_scalar(rec_r[:], rec_r[:], beta_rows[:, p:p + 1], None, ALU.mult))
                link(nc.vector.tensor_copy(rec_hi[:], rec_r[:]))
                nc.vector.tensor_tensor(rec_lo[:], rec_r[:], rec_hi[:].bitcast(F32), ALU.subtract).then_inc(rec_ready, 1)

            def normalise(it, g, j, Y):
                dve.wait_ge(bc_ready, Y + 1)
                after(dve, y_ready, buffers_free(j, Y))
                nc.vector.tensor_tensor(sqn[:, g, j], sT[:, 0], a_ps[:], ALU.mult)
                nc.vector.tensor_tensor(skn[:, g, j], sT[:, 1], b_ps[:], ALU.mult).then_inc(norm_done, 1)

            def softmax(g, t, Z):
                s = s_all[:, g, t].rearrange("p (h k) -> p h k", k=SEG)
                if t == 0:
                    dve.wait_ge(sc_ready, Z + T)
                link(nc.vector.tensor_reduce(smax[:], s, AX.X, ALU.max))
                nc.vector.tensor_tensor(s, s, smax[:].unsqueeze(2).to_broadcast([P, HU, SEG]), ALU.subtract).then_inc(sub_ready, 1)

            def softmax2(g, t, Z):
                dve.wait_ge(p_ready, Z + 1)
                link(nc.vector.tensor_reduce(ssum[:], prob[:], AX.X, ALU.add))
                link(nc.vector.reciprocal(ssum[:], ssum[:]))
                link(nc.vector.tensor_tensor(ssum[:], ssum[:], keep[:, g * HU:(g + 1) * HU], ALU.mult))
                link(nc.vector.tensor_tensor(prob[:], prob[:], ssum[:].unsqueeze(2).to_broadcast([P, HU, SEG]), ALU.mult))
                after(dve, sdpa_done, Z)
                for s in range(SPT):
                    q = slice(s * SEG, (s + 1) * SEG)
                    last = nc.vector.transpose(pT[q, :, q], prob[q])
                last.then_inc(pT_ready, 1)

            def make_u(g, t, s, U):
                w = t * SPT + s
                q = slice(s * SEG, (s + 1) * SEG)
                if 1 <= w < SEGS - 1:
                    dve.wait_ge(prev_ready, U * NU + w)
                    nc.vector.tensor_tensor(u[q], v[q, g, t], prev_ps[q], ALU.subtract).then_inc(u_ready, 1)

            def update(g, t, s, U):
                w = t * SPT + s
                if w < SEGS - 1:
                    dve.wait_ge(d_ready, U * NM + w + 1)
                    if w:
                        dve.wait_ge(mem_ready, U * NM + w)
                    for h in range(2):
                        d = slice(h * DH, (h + 1) * DH)
                        if w:
                            last = nc.vector.tensor_tensor(mem[d, :, d], mem[d, :, d], d_ps[d, :, d], ALU.add)
                        else:
                            last = nc.vector.tensor_copy(mem[d, :, d], d_ps[d, :, d])
                    last.then_inc(mem_ready, 1)

            def o_low(Z):
                dve.wait_ge(ohi_ready, Z + 1)
                nc.vector.tensor_tensor(o_lo[:], o_ps[:], o_hi[:].bitcast(F32), ALU.subtract).then_inc(olo_ready, 1)

            def add_y(it, g, t, Z):
                dve.wait_ge(y_ready, Z + 1)
                if g == 0:
                    dve.wait_ge(xres_in, 16 * (it + 1))
                    after(dve, stored, (it - 1) * 16 * T + 16 * (t + 1))
                else:
                    dve.wait_ge(acc_done, Z - T + 1)
                nc.vector.tensor_tensor(acc[:, t], y_ps[:, 0:D], (acc if g else x_res)[:, t], ALU.add).then_inc(acc_done, 1)

            norm(0)
            norm2(0)
            x_affine(0)
            for j in range(PU):
                for f in (elu, memory_z, rope_cos, rope_sum, scores, inverses, normalise):
                    f(0, 0, j, j)

            def body(it):
                order.step(it)
                for g, t, Z, nxt in slots(it):
                    U = it * GROUPS + g
                    do = lambda f: nxt and f(*nxt)
                    softmax(g, t, Z)
                    softmax2(g, t, Z)
                    if g == 1 and t == 0 and nxt:
                        x_affine(it + 1)
                    do(elu)
                    make_u(g, t, 0, U)
                    do(memory_z)
                    update(g, t, 0, U)
                    if t:
                        add_y(it, g, t - 1, Z - 1)
                    elif g:
                        add_y(it, 0, T - 1, Z - 1)
                    elif not first_step(it):
                        add_y(it - 1, 1, T - 1, Z - 1)
                    do(rope_cos)
                    make_u(g, t, 1, U)
                    update(g, t, 1, U)
                    do(rope_sum)
                    make_u(g, t, 2, U)
                    do(inverses)
                    update(g, t, 2, U)
                    do(scores)
                    make_u(g, t, 3, U)
                    update(g, t, 3, U)
                    o_low(Z)
                    do(normalise)
                    if g == 0 and not last_step(it):
                        if t == 2:
                            norm(it + 1)
                        if t == 3:
                            norm2(it + 1)
                if last_step(it):
                    add_y(it, 1, T - 1, Z)

            units(dve, body)

        @block.tensor
        def _(pe):
            pe.wait_ge(const_in, 16 * 11)
            pe.wait_ge(lo_split, 3)

            def x_transposes(it):
                pe.wait_ge(xn_ready, it + 1)
                after(pe, exp_ready, it * 2 * PU)
                for t in range(T):
                    for c in range(DC):
                        last = nc.tensor.transpose(qk_ps[:, c, t * P:(t + 1) * P], x_ln[:, t, c * P:(c + 1) * P], ident[:])
                last.then_inc(xT_in_psum, 1)

            def project(it, g, j, Y):
                if g == 0 and j == 0:
                    pe.wait_ge(xlo_ready, it + 1)
                after(pe, exp_ready, Y)
                p = g * PU + j
                for a in range(2):
                    for c in range(DC):
                        last = three(nc, qk_ps[:, a], [w[:, a, p, c] for w in wqk], (xT_hi[:, c], xT_lo[:, c]), c == 0, c == DC - 1)
                last.then_inc(qk_ready, 1)

            def values(it, g, j, Y):
                after(pe, norm_done, Y)
                tok = slice(j * P, (j + 1) * P)
                for c in range(DC):
                    last = three(nc, b_ps[:], (xT_hi[:, c, tok], xT_lo[:, c, tok]), [w[:, c, g * GD:(g + 1) * GD] for w in wv], c == 0, c == DC - 1)
                last.then_inc(v_in_psum, 1)

            def keys(it, g, j, Y):
                pe.wait_ge(s_ready, Y + 1)
                pe.wait_ge(v_ready, Y + 1)
                for t in range(T):
                    last = nc.tensor.transpose(b_ps[:, t * P:(t + 1) * P], sT[:, 1, t * P:(t + 1) * P], ident[:])
                last.then_inc(sk_in_psum, 1)

            def denominators(it, g, j, Y):
                pe.wait_ge(prod_ready, Y + 1)
                after(pe, norm_done, Y)
                for a in range(2):
                    last = nc.tensor.matmul(a_ps[0:4, :], sel[:, a, :], prod[:, a, :], start=(a == 0), stop=(a == 1))
                last.then_inc(den_in_psum, 1)

            def scores(it, g, j, Y, tiles):
                if 0 in tiles:
                    pe.wait_ge(rope_ready, Y + 1)
                    pe.wait_ge(sk_ready, Y + 1)
                    pe.wait_ge(den_ready, Y + 1)
                    nc.tensor.matmul(b_ps[0:SEG, 0:2], ident[:, 0:SEG], ident[:, 0:2], start=True, stop=True)
                for t in tiles:
                    for s in range(SPT):
                        tok = slice(t * P + s * SEG, t * P + (s + 1) * SEG)
                        for h in range(2):
                            d = slice(h * DH, (h + 1) * DH)
                            last = nc.tensor.matmul((a_ps, b_ps)[h][s * SEG:(s + 1) * SEG, t * SEG:(t + 1) * SEG], rope[d, 0, tok], rope[d, 1, tok], start=True, stop=True)
                if T - 1 in tiles:
                    last.then_inc(sc_in_psum, 1)

            def broadcast(it, g, j, Y):
                pe.wait_ge(rec_rows, 32 * (Y + 1))
                pe.wait_ge(sc_ready, Y + 1)
                pe.wait_ge(den_ready, Y + 1)
                nc.tensor.matmul(a_ps[:], selbc[:, 0, :], rec8[:], start=True, stop=True)
                nc.tensor.matmul(b_ps[:], selbc[:, 1, :], rec8[:], start=True, stop=True).then_inc(bc_ready, 1)

            def sdpa(g, t, Z):
                pe.wait_ge(pT_ready, Z + 1)
                after(pe, olo_ready, Z)
                if t == 0:
                    pe.wait_ge(norm_done, Z + T)
                for h in range(HU):
                    e = slice((h % 2) * DH, (h % 2 + 1) * DH)
                    last = nc.tensor.matmul(o_ps[e, h // 2, :], v[:, g, t, h * DH:(h + 1) * DH], pT[:, h, :], start=(h < 2), stop=False, skip_group_check=True)
                last.then_inc(sdpa_done, 1)

            def recall(g, t, s, U):
                w = t * SPT + s
                if w == 0:
                    return
                pe.wait_ge(mem_ready, U * NM + w)
                tok = slice(w * SEG, (w + 1) * SEG)
                q = slice(s * SEG, (s + 1) * SEG)
                if w < SEGS - 1:
                    after(pe, u_ready, U * NU + w - 1)
                    for j in range(PU):
                        last = nc.tensor.matmul(prev_ps[q, j * P:(j + 1) * P], skn[:, g, j, tok], mem[:, j, :], start=True, stop=True)
                    last.then_inc(prev_ready, 1)
                for j in range(PU):
                    last = nc.tensor.matmul(o_ps[:, j, q], mem[:, j, :], sqn[:, g, j, tok], start=False, stop=True, skip_group_check=True)
                if s == SPT - 1:
                    last.then_inc(o_ready, 1)

            def store(g, t, s, U, Z):
                w = t * SPT + s
                q = slice(s * SEG, (s + 1) * SEG)
                if w < SEGS - 1:
                    if w:
                        pe.wait_ge(u_ready, U * NU + w)
                    after(pe, mem_ready, U * NM + w)
                    for j in range(PU):
                        e = slice(j * P, (j + 1) * P)
                        last = nc.tensor.matmul(d_ps[:, j, :], sk[q, g, t, e], u[q, e] if w else v[q, g, t, e], start=True, stop=True)
                    last.then_inc(d_ready, 1)

            def project_out(g, t, Z):
                pe.wait_ge(olo_ready, Z + 1)
                after(pe, acc_done, Z)
                for j in range(PU):
                    last = three(nc, y_ps[:, 0:D], (o_hi[:, j], o_lo[:, j]), [w[:, g * PU + j] for w in wo], j == 0, j == PU - 1)
                last.then_inc(y_ready, 1)

            x_transposes(0)
            for j in range(PU):
                for f in (project, values, keys, denominators):
                    f(0, 0, j, j)
                scores(0, 0, j, j, range(T))
                broadcast(0, 0, j, j)

            def body(it):
                for g, t, Z, nxt in slots(it):
                    U = it * GROUPS + g
                    do = lambda f, *a: nxt and f(*nxt, *a)
                    if g == 1 and t == 0 and nxt:
                        x_transposes(it + 1)
                    do(project)
                    sdpa(g, t, Z)
                    recall(g, t, 0, U)
                    do(values)
                    store(g, t, 0, U, Z)
                    if t:
                        project_out(g, t - 1, Z - 1)
                    elif g:
                        project_out(0, T - 1, Z - 1)
                    elif not first_step(it):
                        project_out(1, T - 1, Z - 1)
                    recall(g, t, 1, U)
                    do(keys)
                    store(g, t, 1, U, Z)
                    do(denominators)
                    recall(g, t, 2, U)
                    do(scores, range(T // 2))
                    store(g, t, 2, U, Z)
                    do(scores, range(T // 2, T))
                    recall(g, t, 3, U)
                    store(g, t, 3, U, Z)
                    do(broadcast)
                if last_step(it):
                    project_out(1, T - 1, Z)

            units(pe, body)


H1 = 16
DH1 = D // H1
VE = DH1 + 1
NS = T * H1 // 2
KB = 2 * P
STATE = 64
DFF = 4 * D
MF = DFF // P
LAG_T, LAG_P = 2, 3


def attn1_phase(nc, x, out, wqk_d, wvg_d, bw_d, cw_d, wo_d, w1_d, w2_d, cols_d, rows_d, b1_d, a_d, window_d, half_d, ident_d):
    x_v = x.rearrange("(n t p) d -> n p t d", t=T, p=P)
    out_v = out.rearrange("(n t p) d -> n p t d", t=T, p=P)
    with ExitStack() as ctx:
        def sb(nm, shape, dt=F32, c=ctx):
            return c.enter_context(nc.sbuf_tensor(f"c_{nm}", shape, dt))

        def ps(nm, shape):
            return ctx.enter_context(nc.psum_tensor(f"c_{nm}", shape, F32))

        def sem(nm):
            return ctx.enter_context(nc.semaphore(f"c_{nm}"))

        def halves(nm, shape):
            return [sb(f"{nm}_{h}", shape, F32R) for h in ("hi", "lo")]

        wqk = halves("wqk", [P, DC, 2 * D])
        wvg = halves("wvg", [P, DC, 2 * D])
        bw = halves("bw", [P, DC, P])
        cw = halves("cw", [P, D])
        wo = halves("wo", [P, DC, D])
        w1 = halves("w1", [P, DC, DFF])
        w2 = halves("w2", [P, MF, D])
        loaded = sem("loaded")
        hi_split = sem("hi_split")
        lo_split = sem("lo_split")

        with ExitStack() as c1:
            block = c1.enter_context(nc.Block())
            parts = []
            for n, (w, src) in enumerate(((wqk, wqk_d), (wvg, wvg_d), (bw, bw_d), (cw, cw_d), (wo, wo_d), (w1, w1_d), (w2, w2_d))):
                hi, lo = [h[:] if len(h.shape) == 2 else h[:].rearrange("p c i -> p (c i)") for h in w]
                parts.append((hi, lo, sb(f"raw{n}", [P, src.shape[1]], c=c1), src))

            @block.sync
            def _(sp):
                for hi, lo, raw, src in parts:
                    sp.dma_start(raw[:], src).then_inc(loaded, 16)

            @block.scalar
            def _(act):
                act.wait_ge(loaded, 16 * len(parts))
                for hi, lo, raw, src in parts:
                    nc.scalar.copy(hi, raw[:]).then_inc(hi_split, 1)

            @block.vector
            def _(dve):
                for n, (hi, lo, raw, src) in enumerate(parts):
                    dve.wait_ge(hi_split, n + 1)
                    nc.vector.tensor_tensor(lo, raw[:], hi.bitcast(F32), ALU.subtract).then_inc(lo_split, 1)

        cols = sb("cols", [P, 14])
        rows = sb("rows", [P, 4, D])
        b1 = sb("b1", [P, MF])
        a = sb("a", [P, 1])
        half = sb("half", [P, T])
        eps = sb("eps", [P, T])
        ident = sb("ident", [P, P])
        identb = sb("identb", [P, P], BF16)
        window = sb("window", [P, KB])
        maskb = sb("maskb", [P, KB], BF16)
        carrier = sb("carrier", [P, 1])
        ln1_g, ln1_b, bq, bk, head_mask, ln2_g, ln2_b = (cols[:, n * 2:n * 2 + 2] for n in range(7))
        kbias = sb("kbias", [P, 2, DC])

        x_in = sb("x_in", [P, T, D])
        hn = sb("hn", [P, T, D])
        y = sb("y", [P, T, D])
        xb = sb("xb", [P, T, D])
        stats = sb("stats", [P, T, 6])
        mv = sb("mv", [P, T, 2])
        lnt = sb("lnt", [P, 5, T])
        hT = sb("hT", [P, DC, SEQ])
        hT_hl = halves("hT", [P, DC, SEQ])
        qT = sb("qT", [P, DC, SEQ])
        kz = sb("kz", [P, 2, DC, SEQ])
        v = sb("v", [P, T, H1, VE])
        gate = sb("gate", [P, T, D])
        state = sb("state", [P, SEQ])
        state_hl = sb("state_hl", [P, SEQ], F32R)
        nmax = sb("nmax", [P, 4, 2])
        prob = sb("prob", [P, 4, 2, KB])
        pT = sb("pT", [P, 2, 2, 2, P])
        osum = sb("osum", [P, H1])
        ao = sb("ao", [P, D])
        aoT_hl = halves("aoT", [P, DC, P])
        t1 = sb("t1", [P, D])
        x1 = sb("x1", [P, T, D])
        res = sb("res", [P, T, D])
        stats2 = sb("stats2", [P, T, 6])
        mv2 = sb("mv2", [P, T, 2])
        lnt2 = sb("lnt2", [P, 2, T])
        h2T = sb("h2T", [P, DC, SEQ])
        h2T_hl = halves("h2T", [P, DC, SEQ])
        ff = sb("ff", [P, 2, SEQ])
        ff_hl = halves("ff", [P, MF, SEQ])
        result = sb("result", [P, 2, D])

        s_ps = ps("s_ps", [P, 2, 2, KB])
        t_ps = ps("t_ps", [P, 2, 2, 2, P])
        o_ps = ps("o_ps", [P, 512])
        ab_ps = ps("ab_ps", [P, 2, SEQ])
        c_ps = ps("c_ps", [P, 2, D])
        o17 = o_ps[:, 0:H1 * VE].rearrange("p (h e) -> p h e", e=VE)

        const_in = sem("const_in")
        const_ready = sem("const_ready")
        x_loaded = sem("x_loaded")
        var_ready = sem("var_ready")
        rstd_ready = sem("rstd_ready")
        hn_ready = sem("hn_ready")
        hT_in_psum = sem("hT_in_psum")
        hT_ready = sem("hT_ready")
        hhi_ready = sem("hhi_ready")
        hlo_ready = sem("hlo_ready")
        q_in_psum = sem("q_in_psum")
        q_ready = sem("q_ready")
        k_in_psum = sem("k_in_psum")
        k_ready = sem("k_ready")
        vg_in_psum = sem("vg_in_psum")
        vg_ready = sem("vg_ready")
        gate_ready = sem("gate_ready")
        in_in_psum = sem("in_in_psum")
        state_ready = sem("state_ready")
        statehi_ready = sem("statehi_ready")
        statelo_ready = sem("statelo_ready")
        s_ready = sem("s_ready")
        max_ready = sem("max_ready")
        exp_ready = sem("exp_ready")
        t_ready = sem("t_ready")
        pT_ready = sem("pT_ready")
        pv_done = sem("pv_done")
        ao_ready = sem("ao_ready")
        aoT_in_psum = sem("aoT_in_psum")
        aohi_ready = sem("aohi_ready")
        aolo_ready = sem("aolo_ready")
        mix_in_psum = sem("mix_in_psum")
        x1_done = sem("x1_done")
        xb_ready = sem("xb_ready")
        var2_ready = sem("var2_ready")
        rstd2_ready = sem("rstd2_ready")
        h2n_ready = sem("h2n_ready")
        h2T_in_psum = sem("h2T_in_psum")
        h2T_ready = sem("h2T_ready")
        h2hi_ready = sem("h2hi_ready")
        h2lo_ready = sem("h2lo_ready")
        ff_in_psum = sem("ff_in_psum")
        ff_ready = sem("ff_ready")
        ffhi_ready = sem("ffhi_ready")
        fflo_ready = sem("fflo_ready")
        y_in_psum = sem("y_in_psum")
        result_ready = sem("result_ready")
        slot_free = [sem(f"slot_free{n}") for n in range(2)]
        dve_order = sem("dve_order")
        pool_order = sem("pool_order")
        CONSTS = 7

        block = ctx.enter_context(nc.Block())

        def bodies(eng, body):
            body(0)
            with eng.Fori(1, NSEQ - 1) as it:
                body(it)
            body(NSEQ - 1)

        def keys_of(i):
            return slice(0 if i else P, KB)

        def blocks_of(i):
            return range(0 if i else 1, 2)

        @block.sync
        def _(sp):
            for dst, src in ((cols, cols_d), (rows, rows_d), (b1, b1_d), (a, a_d), (half, half_d), (ident, ident_d), (window, window_d)):
                sp.dma_start(dst[:], src).then_inc(const_in, 16)
            sp.dma_start(x_in[:], x_v[0]).then_inc(x_loaded, 16)

            def load(it):
                sp.wait_ge(xb_ready, it)
                sp.dma_start(x_in[:], sequence(x_v, it)).then_inc(x_loaded, 16)

            def body(it):
                before = None if first_step(it) else sp.snap(it - 1)
                if not last_step(it):
                    load(it + 1)
                if not first_step(it):
                    for t in range(T):
                        store(before, t, it * T - T + t + 1)
            
            def store(it, t, count):
                sp.wait_ge(result_ready, count)
                sp.dma_start(out_v[bass.ds(it, 1), :, t].rearrange("a p d -> p (a d)"), result[:, t % 2]).then_inc(slot_free[t % 2], 16)

            bodies(sp, body)
            for t in range(T):
                store(NSEQ - 1, t, (NSEQ - 1) * T + t + 1)
            for n in range(2):
                sp.wait_ge(slot_free[n], 16 * (NSEQ * T // 2 + 1))

        @block.gpsimd
        def _(pool):
            order = Order(pool, pool_order)
            pool.wait_ge(const_in, 16 * CONSTS)
            order.link(nc.gpsimd.memset(eps[:], EPS))

            def inverse_deviations(it):
                pool.wait_ge(var_ready, it + 1)
                order.link(nc.gpsimd.tensor_tensor(lnt[:, 0], mv[:, :, 1], eps[:], ALU.add))
                order.link(nc.gpsimd.tensor_tensor(lnt[:, 1], lnt[:, 0], half[:], ALU.pow))
                order.link(nc.gpsimd.tensor_tensor(lnt[:, 2], lnt[:, 1], lnt[:, 1], ALU.mult))
                order.link(nc.gpsimd.tensor_tensor(lnt[:, 0], lnt[:, 2], mv[:, :, 1], ALU.mult))
                order.link(nc.gpsimd.tensor_tensor(lnt[:, 2], lnt[:, 0], eps[:], ALU.add))
                order.link(nc.gpsimd.tensor_tensor(lnt[:, 3], lnt[:, 2], half[:], ALU.pow))
                nc.gpsimd.tensor_tensor(lnt[:, 4], lnt[:, 1], lnt[:, 3], ALU.mult).then_inc(rstd_ready, 1)

            def inverse_deviation2(it):
                pool.wait_ge(var2_ready, it + 1)
                order.link(nc.gpsimd.tensor_tensor(lnt2[:, 0], mv2[:, :, 1], eps[:], ALU.add))
                nc.gpsimd.tensor_tensor(lnt2[:, 1], lnt2[:, 0], half[:], ALU.pow).then_inc(rstd2_ready, 1)

            inverse_deviations(0)

            def body(it):
                order.step(it)
                if not last_step(it):
                    inverse_deviations(it + 1)
                inverse_deviation2(it)

            bodies(pool, body)

        @block.scalar
        def _(act):
            act.wait_ge(const_in, 16 * CONSTS)
            act.wait_ge(const_ready, 1)

            def h_hi(it):
                act.wait_ge(hT_ready, it + 1)
                after(act, in_in_psum, it)
                nc.scalar.copy(hT_hl[0][:], hT[:]).then_inc(hhi_ready, 1)

            def keys(it):
                for c in range(DC):
                    act.wait_ge(k_in_psum, it * DC + c + 1)
                    if c == 0:
                        after(act, pv_done, it * NS)
                    for m in range(2):
                        last = nc.scalar.activation(kz[:, m, c], ab_ps[:, c], ACT.Identity, bias=kbias[:, m, c:c + 1], scale=head_mask[:, m:m + 1])
                    last.then_inc(k_ready, 1)

            def gates(it):
                act.wait_ge(vg_ready, (it + 1) * T)
                nc.scalar.activation(gate[:], gate[:], ACT.Tanh, scale=0.5).then_inc(gate_ready, 1)

            def state_hi(it):
                act.wait_ge(state_ready, it + 1)
                after(act, mix_in_psum, it * T)
                nc.scalar.copy(state_hl[:], state[:]).then_inc(statehi_ready, 1)

            def exp(it, n):
                i = n // (H1 // 2)
                G = it * NS + n
                act.wait_ge(max_ready, G + 1)
                after(act, t_ready, G - 3)
                for h in range(2):
                    last = nc.scalar.activation(prob[:, n % 4, h, keys_of(i)], s_ps[:, n % 2, h, keys_of(i)], ACT.Exp, bias=nmax[:, n % 4, h:h + 1])
                last.then_inc(exp_ready, 1)

            def pT_copy(it, n):
                i = n // (H1 // 2)
                b = blocks_of(i)
                G = it * NS + n
                act.wait_ge(t_ready, G + 1)
                after(act, pv_done, G - 1)
                nc.scalar.copy(pT[:, n % 2, :, b[0]:2], t_ps[:, n % 2, :, b[0]:2]).then_inc(pT_ready, 1)

            def ao_hi(it, t):
                act.wait_ge(aoT_in_psum, it * T + t + 1)
                after(act, mix_in_psum, it * T + t)
                nc.scalar.copy(aoT_hl[0][:].rearrange("p c q -> p (c q)"), c_ps[:, 0, :]).then_inc(aohi_ready, 1)

            def h2_hi(it):
                act.wait_ge(h2T_ready, it + 1)
                after(act, ff_in_psum, it * MF)
                nc.scalar.copy(h2T_hl[0][:], h2T[:]).then_inc(h2hi_ready, 1)

            def gelu(it, m):
                act.wait_ge(ff_in_psum, it * MF + m + 1)
                after(act, fflo_ready, it * MF + m - 1)
                nc.scalar.activation(ff[:, m % 2], ab_ps[:, m % 2], ACT.Gelu, bias=b1[:, m:m + 1]).then_inc(ff_ready, 1)

            def ff_hi(it, m):
                act.wait_ge(ff_ready, it * MF + m + 1)
                after(act, y_in_psum, it * T)
                nc.scalar.copy(ff_hl[0][:, m], ff[:, m % 2]).then_inc(ffhi_ready, 1)

            h_hi(0)
            keys(0)

            def body(it):
                gates(it)
                for n in range(NS + LAG_T):
                    if n < NS:
                        exp(it, n)
                    if n >= LAG_T:
                        pT_copy(it, n - LAG_T)
                    if n == 10:
                        state_hi(it)
                    if n >= 13 and (n - 13) % 8 == 0:
                        ao_hi(it, (n - 13) // 8)
                if not last_step(it):
                    h_hi(it + 1)
                ao_hi(it, T - 1)
                if not last_step(it):
                    keys(it + 1)
                h2_hi(it)
                for m in range(MF):
                    gelu(it, m)
                    if m:
                        ff_hi(it, m - 1)
                ff_hi(it, MF - 1)

            bodies(act, body)

        @block.vector
        def _(dve):
            order = Order(dve, dve_order)
            link = order.link
            for n in range(2):
                nc.vector.memset(result[:, n], 0.0).then_inc(slot_free[n], 16)
            nc.vector.memset(v[:].rearrange("p t h e -> p (t h e)"), 1.0)
            dve.wait_ge(const_in, 16 * CONSTS)
            nc.vector.tensor_copy(identb[:], ident[:])
            nc.vector.tensor_copy(maskb[:], window[:])
            for m in range(2):
                last = nc.vector.tensor_scalar(kbias[:, m], bk, head_mask[:, m:m + 1], None, ALU.mult)
            last.then_inc(const_ready, 1)

            def norm(it):
                dve.wait_ge(x_loaded, 16 * (it + 1))
                for t in range(T):
                    last = nc.vector.bn_stats(stats[:, t], x_in[:, t])
                link(last)
                nc.vector.memset(carrier[:], 0.0)
                for t in range(T):
                    last = nc.vector.bn_aggr(mv[:, t], stats[:, t])
                last.then_inc(var_ready, 1)

            def hn_of(it):
                dve.wait_ge(rstd_ready, it + 1)
                after(dve, hT_in_psum, it)
                for t in range(T):
                    last = nc.vector.tensor_scalar(hn[:, t], x_in[:, t], mv[:, t, 0:1], lnt[:, 4, t:t + 1], ALU.subtract, ALU.mult)
                last.then_inc(hn_ready, 1)

            def y_of(it):
                for t in range(T):
                    nc.vector.tensor_scalar(y[:, t], x_in[:, t], mv[:, t, 0:1], lnt[:, 1, t:t + 1], ALU.subtract, ALU.mult)
                    last = nc.vector.tensor_tensor(xb[:, t], x_in[:, t], rows[:, 3], ALU.add)
                last.then_inc(xb_ready, 1)

            def affine(it, src, dst, g, b, waits, done):
                dve.wait_ge(waits, it + 1)
                for c in range(DC):
                    last = nc.vector.tensor_scalar(dst[:, c], src[c], g[:, c:c + 1], b[:, c:c + 1], ALU.mult, ALU.add)
                last.then_inc(done, 1)

            def h_lo(it):
                dve.wait_ge(hhi_ready, it + 1)
                nc.vector.tensor_tensor(hT_hl[1][:], hT[:], hT_hl[0][:].bitcast(F32), ALU.subtract).then_inc(hlo_ready, 1)

            def queries(it):
                for c in range(DC):
                    dve.wait_ge(q_in_psum, it * DC + c + 1)
                    if c == 0:
                        after(dve, pv_done, it * NS)
                    nc.vector.tensor_scalar(qT[:, c], ab_ps[:, c], bq[:, c:c + 1], DH1 ** -0.5, ALU.add, ALU.mult).then_inc(q_ready, 1)

            def values_gates(it, t):
                dve.wait_ge(vg_in_psum, it * T + t + 1)
                if t == 0:
                    after(dve, pv_done, it * NS)
                heads = lambda ap: ap.rearrange("p (h e) -> p h e", e=DH1)
                nc.vector.tensor_tensor(v[:, t, :, 0:DH1], heads(ab_ps[:, t % 2, 0:D]), heads(rows[:, 0]), ALU.add)
                nc.vector.tensor_tensor(gate[:, t], ab_ps[:, t % 2, D:2 * D], rows[:, 1], ALU.add).then_inc(vg_ready, 1)

            def scan(it):
                dve.wait_ge(in_in_psum, it + 1)
                after(dve, statelo_ready, it)
                nc.vector.tensor_tensor_scan(state[:], a[:].to_broadcast([P, SEQ]), c_ps[:].rearrange("p a d -> p (a d)"), 0.0, ALU.mult, ALU.add).then_inc(state_ready, 1)

            def state_lo(it):
                dve.wait_ge(statehi_ready, it + 1)
                up = slice(STATE, P)
                nc.vector.tensor_tensor(state_hl[up], state[up], state_hl[up].bitcast(F32), ALU.subtract).then_inc(statelo_ready, 1)

            def maxima(it, n):
                i = n // (H1 // 2)
                G = it * NS + n
                dve.wait_ge(s_ready, G + 1)
                after(dve, exp_ready, G - 3)
                nc.vector.tensor_reduce(nmax[:, n % 4], s_ps[:, n % 2, :, keys_of(i)], AX.X, ALU.max, negate=True).then_inc(max_ready, 1)

            def ao_of(it, t):
                dve.wait_ge(pv_done, it * NS + (t + 1) * (H1 // 2))
                link(nc.vector.reciprocal(osum[:], o17[:, :, DH1]))
                after(dve, aoT_in_psum, it * T + t)
                nc.vector.tensor_tensor(ao[:].rearrange("p (h e) -> p h e", e=DH1), o17[:, :, 0:DH1], osum[:].unsqueeze(2).to_broadcast([P, H1, DH1]), ALU.mult).then_inc(ao_ready, 1)

            def ao_lo(it, t):
                dve.wait_ge(aohi_ready, it * T + t + 1)
                nc.vector.tensor_tensor(aoT_hl[1][:].rearrange("p c q -> p (c q)"), c_ps[:, 0, :], aoT_hl[0][:].rearrange("p c q -> p (c q)").bitcast(F32), ALU.subtract).then_inc(aolo_ready, 1)

            def mix(it, t):
                dve.wait_ge(mix_in_psum, it * T + t + 1)
                if t == 0:
                    dve.wait_ge(gate_ready, it + 1)
                    dve.wait_ge(xb_ready, it + 1)
                    after(dve, result_ready, it * T)
                    after(dve, h2n_ready, it)
                link(nc.vector.tensor_tensor(t1[:], c_ps[:, 1], rows[:, 2], ALU.add))
                link(nc.vector.tensor_tensor(t1[:], t1[:], c_ps[:, 0], ALU.subtract))
                link(nc.vector.scalar_tensor_tensor(t1[:], gate[:, t], 1.0, t1[:], ALU.add, ALU.mult))
                link(nc.vector.scalar_tensor_tensor(t1[:], t1[:], 0.5, c_ps[:, 0], ALU.mult, ALU.add))
                nc.vector.tensor_tensor(x1[:, t], t1[:], y[:, t], ALU.add).then_inc(x1_done, 1)
                dve.wait_ge(x1_done, it * T + t + 1)
                nc.vector.bn_stats(stats2[:, t], x1[:, t])
                link(nc.vector.tensor_tensor(res[:, t], x1[:, t], xb[:, t], ALU.add))

            def norm2(it):
                nc.vector.memset(carrier[:], 0.0)
                for t in range(T):
                    last = nc.vector.bn_aggr(mv2[:, t], stats2[:, t])
                last.then_inc(var2_ready, 1)

            def h2n_of(it):
                dve.wait_ge(rstd2_ready, it + 1)
                for t in range(T):
                    last = nc.vector.tensor_scalar(x1[:, t], x1[:, t], mv2[:, t, 0:1], lnt2[:, 1, t:t + 1], ALU.subtract, ALU.mult)
                last.then_inc(h2n_ready, 1)

            def h2_lo(it):
                dve.wait_ge(h2hi_ready, it + 1)
                nc.vector.tensor_tensor(h2T_hl[1][:], h2T[:], h2T_hl[0][:].bitcast(F32), ALU.subtract).then_inc(h2lo_ready, 1)

            def ff_lo(it, m):
                dve.wait_ge(ffhi_ready, it * MF + m + 1)
                nc.vector.tensor_tensor(ff_hl[1][:, m], ff[:, m % 2], ff_hl[0][:, m].bitcast(F32), ALU.subtract).then_inc(fflo_ready, 1)

            def result_of(it, t):
                dve.wait_ge(y_in_psum, it * T + t + 1)
                dve.wait_ge(slot_free[t % 2], 16 * (it * T // 2 + t // 2 + 1))
                nc.vector.tensor_tensor(result[:, t % 2], ab_ps[:, t % 2, 0:D], res[:, t], ALU.add).then_inc(result_ready, 1)

            ab = [ab_ps[:, c] for c in range(DC)]
            sab = [s_ps[:, c].rearrange("p h k -> p (h k)") for c in range(DC)]
            norm(0)
            hn_of(0)
            affine(0, ab, hT, ln1_g, ln1_b, hT_in_psum, hT_ready)
            h_lo(0)
            queries(0)
            for t in range(T):
                values_gates(0, t)
            scan(0)
            y_of(0)

            def body(it):
                order.step(it)
                for n in range(NS):
                    maxima(it, n)
                    if n == 11:
                        state_lo(it)
                    if not first_step(it) and n in (3, 5, 7, 9):
                        result_of(it - 1, (n - 3) // 2)
                    if n >= 11 and (n - 11) % 8 == 0:
                        ao_of(it, (n - 11) // 8)
                    if n >= 13 and (n - 13) % 8 == 0:
                        ao_lo(it, (n - 13) // 8)
                    if n >= 15 and (n - 15) % 8 == 0:
                        mix(it, (n - 15) // 8)
                    if not last_step(it):
                        if n == 20:
                            norm(it + 1)
                        if n == 24:
                            hn_of(it + 1)
                ao_of(it, T - 1)
                if not last_step(it):
                    affine(it + 1, ab, hT, ln1_g, ln1_b, hT_in_psum, hT_ready)
                ao_lo(it, T - 1)
                if not last_step(it):
                    h_lo(it + 1)
                mix(it, T - 1)
                norm2(it)
                if not last_step(it):
                    queries(it + 1)
                    values_gates(it + 1, 0)
                    values_gates(it + 1, 1)
                h2n_of(it)
                if not last_step(it):
                    y_of(it + 1)
                    values_gates(it + 1, 2)
                affine(it, sab, h2T, ln2_g, ln2_b, h2T_in_psum, h2T_ready)
                h2_lo(it)
                if not last_step(it):
                    values_gates(it + 1, 3)
                    scan(it + 1)
                for m in range(MF):
                    ff_lo(it, m)

            bodies(dve, body)
            for t in range(T):
                result_of(NSEQ - 1, t)

        @block.tensor
        def _(pe):
            pe.wait_ge(const_in, 16 * CONSTS)
            pe.wait_ge(const_ready, 1)
            pe.wait_ge(lo_split, 7)

            def transpose_tiles(src, dst):
                for t in range(T):
                    for c in range(DC):
                        last = nc.tensor.transpose(dst[c][:, t * P:(t + 1) * P], src[:, t, c * P:(c + 1) * P], ident[:])
                return last

            ab = [ab_ps[:, c] for c in range(DC)]
            sab = [s_ps[:, c].rearrange("p h k -> p (h k)") for c in range(DC)]

            def h_transposes(it):
                pe.wait_ge(hn_ready, it + 1)
                after(pe, result_ready, (it - 1) * T)
                transpose_tiles(hn, ab).then_inc(hT_in_psum, 1)

            def feature_major(w, cols_, x_hl, out_):
                for c in range(DC):
                    last = three(nc, out_, [h[:, c, cols_] for h in w], [h[:, c] for h in x_hl], c == 0, c == DC - 1)
                return last

            def queries(it, m):
                pe.wait_ge(hlo_ready, it + 1)
                feature_major(wqk, slice(m * P, (m + 1) * P), hT_hl, ab_ps[:, m]).then_inc(q_in_psum, 1)

            def keys(it, m):
                pe.wait_ge(q_ready, it * DC + m + 1)
                feature_major(wqk, slice(D + m * P, D + (m + 1) * P), hT_hl, ab_ps[:, m]).then_inc(k_in_psum, 1)

            def values_gates(it, t):
                if t < 2:
                    pe.wait_ge(k_ready, it * DC + t + 1)
                else:
                    pe.wait_ge(vg_ready, it * T + t - 1)
                tok = slice(t * P, (t + 1) * P)
                for c in range(DC):
                    last = three(nc, ab_ps[:, t % 2], [h[:, c, tok] for h in hT_hl], [w[:, c] for w in wvg], c == 0, c == DC - 1)
                last.then_inc(vg_in_psum, 1)

            def state_input(it):
                after(pe, x1_done, it * T)
                feature_major(bw, slice(0, P), hT_hl, c_ps[:].rearrange("p a d -> p (a d)")).then_inc(in_in_psum, 1)

            def scores(it, n):
                i, j = divmod(n, H1 // 2)
                G = it * NS + n
                if n == 0:
                    pe.wait_ge(k_ready, (it + 1) * DC)
                    after(pe, h2T_ready, it)
                after(pe, exp_ready, G - 1)
                rows_, c = slice((j % 4) * 32, (j % 4 + 1) * 32), j // 4
                keys_ = slice(max(i - 1, 0) * P, (i + 1) * P)
                for h in range(2):
                    o = s_ps[:, n % 2, h, keys_of(i)]
                    nc.tensor.matmul(o, identb[:], maskb[:, keys_of(i)], start=True, stop=False)
                    last = nc.tensor.matmul(o, qT[rows_, c, i * P:(i + 1) * P], kz[rows_, h, c, keys_], start=False, stop=True)
                last.then_inc(s_ready, 1)

            def transposes(it, n):
                i = n // (H1 // 2)
                G = it * NS + n
                pe.wait_ge(exp_ready, G + 1)
                after(pe, pT_ready, G - 1)
                for h in range(2):
                    for b in blocks_of(i):
                        last = nc.tensor.transpose(t_ps[:, n % 2, h, b], prob[:, n % 4, h, b * P:(b + 1) * P], ident[:])
                last.then_inc(t_ready, 1)

            def values(it, n):
                i, j = divmod(n, H1 // 2)
                G = it * NS + n
                pe.wait_ge(pT_ready, G + 1)
                if n == 0:
                    pe.wait_ge(vg_ready, (it + 1) * T)
                if j == 0:
                    after(pe, ao_ready, it * T + i)
                for h in range(2):
                    for b in blocks_of(i):
                        last = nc.tensor.matmul(o17[:, 2 * j + h], pT[:, n % 2, h, b], v[:, i - 1 + b, 2 * j + h], start=(b == blocks_of(i)[0]), stop=(b == 1))
                last.then_inc(pv_done, 1)

            def ao_transposes(it, t):
                pe.wait_ge(ao_ready, it * T + t + 1)
                if t:
                    pe.wait_ge(x1_done, it * T + t)
                else:
                    pe.wait_ge(state_ready, it + 1)
                for c in range(DC):
                    last = nc.tensor.transpose(c_ps[:, 0, c * P:(c + 1) * P], ao[:, c * P:(c + 1) * P], ident[:])
                last.then_inc(aoT_in_psum, 1)

            def mix(it, t):
                pe.wait_ge(aolo_ready, it * T + t + 1)
                if t == 0:
                    pe.wait_ge(statelo_ready, it + 1)
                tok = slice(t * P, (t + 1) * P)
                nc.tensor.matmul(c_ps[:, 0], state_hl[:, tok], cw[0][:], start=True, stop=False)
                nc.tensor.matmul(c_ps[:, 0], state_hl[0:STATE, tok], cw[1][0:STATE], start=False, stop=True)
                for c in range(DC):
                    last = three(nc, c_ps[:, 1], [h[:, c] for h in aoT_hl], [w[:, c] for w in wo], c == 0, c == DC - 1)
                last.then_inc(mix_in_psum, 1)

            def h2_transposes(it):
                pe.wait_ge(h2n_ready, it + 1)
                pe.wait_ge(exp_ready, (it + 1) * NS)
                transpose_tiles(x1, sab).then_inc(h2T_in_psum, 1)

            def mlp1(it, m):
                if m == 0:
                    pe.wait_ge(h2lo_ready, it + 1)
                if m < 2:
                    pe.wait_ge(vg_ready, (it + 2) * T if not last_step(it) else NSEQ * T)
                else:
                    pe.wait_ge(ff_ready, it * MF + m - 1)
                feature_major(w1, slice(m * P, (m + 1) * P), h2T_hl, ab_ps[:, m % 2]).then_inc(ff_in_psum, 1)

            def mlp2(it, t):
                if t == 0:
                    pe.wait_ge(fflo_ready, (it + 1) * MF)
                if t >= 2:
                    pe.wait_ge(result_ready, it * T + t - 1)
                tok = slice(t * P, (t + 1) * P)
                for m in range(MF):
                    last = three(nc, ab_ps[:, t % 2, 0:D], [h[:, m, tok] for h in ff_hl], [w[:, m] for w in w2], m == 0, m == MF - 1)
                last.then_inc(y_in_psum, 1)

            h_transposes(0)
            for m in range(DC):
                queries(0, m)
            for m in range(DC):
                keys(0, m)
            for t in range(T):
                values_gates(0, t)
            state_input(0)

            def body(it):
                for n in range(NS + LAG_P):
                    if n < NS:
                        scores(it, n)
                    if LAG_T <= n < NS + LAG_T:
                        transposes(it, n - LAG_T)
                    if n >= LAG_P:
                        values(it, n - LAG_P)
                    if not first_step(it) and n in (2, 4, 6, 8):
                        mlp2(it - 1, (n - 2) // 2)
                    if n >= 12 and (n - 12) % 8 == 0:
                        ao_transposes(it, (n - 12) // 8)
                    if n >= 14 and (n - 14) % 8 == 0:
                        mix(it, (n - 14) // 8)
                if not last_step(it):
                    h_transposes(it + 1)
                ao_transposes(it, T - 1)
                if not last_step(it):
                    queries(it + 1, 0)
                mix(it, T - 1)
                if not last_step(it):
                    queries(it + 1, 1)
                    keys(it + 1, 0)
                    keys(it + 1, 1)
                    values_gates(it + 1, 0)
                    values_gates(it + 1, 1)
                h2_transposes(it)
                if not last_step(it):
                    values_gates(it + 1, 2)
                    values_gates(it + 1, 3)
                    state_input(it + 1)
                for m in range(MF):
                    mlp1(it, m)

            bodies(pe, body)
            for t in range(T):
                mlp2(NSEQ - 1, t)


def network(nc, x, attn0, ffn0, attn1, ffn1, out):
    between = [nc.dram_tensor(f"after_{name}", [NSEQ * SEQ, D], F32, kind="Internal").ap() for name in ("attn0", "ffn0", "attn1")]
    attn0_phase(nc, x, between[0], **attn0)
    moe_phase(nc, "b", between[0], between[1], shared=True, **ffn0)
    attn1_phase(nc, between[1], between[2], **attn1)
    moe_phase(nc, "d", between[2], out, shared=False, bias_d=None, **ffn1)




def by_chunks(w):
    import numpy as np
    return np.reshape(w, (DC, P, -1)).transpose(1, 0, 2).reshape(P, -1)


def experts_by_chunks(w):
    import numpy as np
    return np.reshape(w, (w.shape[0], DC, P, P)).transpose(2, 0, 1, 3)


def common_tables():
    import numpy as np
    return dict(half_d=np.full((P, T), -0.5, np.float32), ident_d=np.eye(P, dtype=np.float32))


def attn0_layout(w_qkv, w_out, ln_g, ln_b, mem_beta):
    import numpy as np
    f32 = np.float32
    inner = HEADS * DH
    evens_first = np.concatenate([np.arange(0, DH, 2), np.arange(1, DH, 2)])
    qk = w_qkv[:, :2 * inner].reshape(DC, P, 2, PAIRS, 2, DH)[..., evens_first].transpose(1, 2, 3, 0, 4, 5).reshape(P, -1)
    beta = mem_beta.reshape(PAIRS, 2)
    freqs = (f32(10000.0) ** (-np.arange(0, DH, 2, dtype=f32) / f32(DH))).astype(f32)
    angles = (np.arange(SEQ, dtype=f32)[None, :] * freqs[:, None]).astype(f32)
    sines = np.sin(angles).astype(f32)
    part = np.arange(P)
    head = part // DH
    sel = np.zeros((P, 2, 4), f32)
    selbc = np.zeros((8, 2, P), f32)
    for a in range(2):
        sel[part, a, 2 * a + head] = 1
        for half in range(2):
            selbc[4 * half + 2 * a + head, a, part] = 1
    return dict(
        wqk_d=qk, wv_d=by_chunks(w_qkv[:, 2 * inner:]), wo_d=w_out.reshape(PAIRS, P, D).transpose(1, 0, 2).reshape(P, -1),
        lng_d=ln_g.reshape(DC, P).T, lnb_d=ln_b.reshape(DC, P).T,
        beta_rows_d=np.repeat(beta.T, SEQ // 16, axis=0), beta_heads_d=np.broadcast_to(beta.reshape(1, HEADS), (P, HEADS)),
        cos_d=np.tile(np.cos(angles), (4, 1)).astype(f32), sin_d=np.concatenate([-sines, sines, -sines, sines]),
        mask_d=np.where(np.arange(SEG)[None, :] <= part[:, None] % SEG, 0, -1e30).astype(f32),
        sel_d=sel, selbc_d=selbc.reshape(8, -1), eps4_d=np.array([[1e-6], [1e-6], [0], [0]], f32), **common_tables())


def ffn0_layout(gate_w, correction_bias, Wg, Wu, Wd, Wg_s, Wu_s, Wd_s):
    import numpy as np
    E = gate_w.shape[0]
    wg, wu, wd = (np.concatenate([s[None], w]) for s, w in ((Wg_s, Wg), (Wu_s, Wu), (Wd_s, Wd)))
    return dict(wg_d=experts_by_chunks(wg), wu_d=experts_by_chunks(wu), wd_d=wd.transpose(1, 0, 2),
                bias_d=np.broadcast_to(correction_bias, (P, E)), **router_layout(gate_w), **common_tables())


def ffn1_layout(gate_w, w_gate, w_up, w_down):
    wg, wu, wd = (w.transpose(0, 2, 1) for w in (w_gate, w_up, w_down))
    return dict(wg_d=experts_by_chunks(wg), wu_d=experts_by_chunks(wu), wd_d=wd.transpose(1, 0, 2), **router_layout(gate_w), **common_tables())


def router_layout(gate_w):
    import numpy as np
    E = gate_w.shape[0]
    lower = np.arange(E)[None, :] < np.arange(E)[:, None]
    return dict(gate_d=by_chunks(gate_w.T).reshape(P, DC, E), lower_d=np.broadcast_to(lower.astype(np.float32), (P, E, E)))


def attn1_layout(ln1_g, ln1_b, WQ, bQ, WK, bK, WV, bV, WO, bO, Wg, bg, A, Bw, Cw, ln2_g, ln2_b, W1, b1, W2, b2):
    import numpy as np
    f32 = np.float32
    by_feature = lambda a: a.reshape(DC, P).T
    odd = (np.arange(P) // DH1) % 2
    head_masks = np.stack([1 - odd, odd], 1).astype(f32)
    q, k = np.arange(P)[:, None], np.arange(P)[None, :]
    window = np.concatenate([np.where(k > q, 0, -1e30), np.where(k <= q, 0, -1e30)], 1).astype(f32)
    return dict(
        wqk_d=by_chunks(np.concatenate([WQ, WK], 1)), wvg_d=by_chunks(np.concatenate([WV, Wg], 1)),
        bw_d=by_chunks(np.concatenate([Bw, Bw], 1)), cw_d=np.concatenate([Cw, Cw]), wo_d=by_chunks(WO), w1_d=by_chunks(W1),
        w2_d=W2.reshape(MF, P, D).transpose(1, 0, 2).reshape(P, -1),
        cols_d=np.concatenate([by_feature(ln1_g), by_feature(ln1_b), by_feature(bQ), by_feature(bK), head_masks, by_feature(ln2_g), by_feature(ln2_b)], 1),
        rows_d=np.broadcast_to(np.stack([bV, bg, bO, b2]), (P, 4, D)), b1_d=b1.reshape(MF, P).T, a_d=np.concatenate([A, A])[:, None],
        window_d=window, **common_tables())


def kernel(**inputs):
    import numpy as np
    import concourse.bacc as bacc
    from concourse.bass_utils import run_bass_kernel_spmd

    arrays = {name: np.asarray(a) for name, a in inputs.items()}

    def of(prefix):
        return {name[len(prefix):]: a for name, a in arrays.items() if name.startswith(prefix)}

    x = arrays.pop("L0_attn_x")
    layouts = dict(attn0=attn0_layout(**of("L0_attn_")), ffn0=ffn0_layout(**of("L0_ffn_")),
                   attn1=attn1_layout(**of("L1_attn_")), ffn1=ffn1_layout(**of("L1_ffn_")))

    nc = bacc.Bacc("TRN2", target_bir_lowering=False, num_devices=1)
    feeds = {}

    def feed(name, a):
        feeds[name] = np.ascontiguousarray(a)
        return nc.dram_tensor(name, feeds[name].shape, mybir.dt.from_np(feeds[name].dtype), kind="ExternalInput").ap()

    x_d = feed("x", x.reshape(NSEQ * SEQ, D))
    args = {block: {name: feed(f"{block}_{name}", a) for name, a in layout.items()} for block, layout in layouts.items()}
    out = nc.dram_tensor("out_0_dram", (NSEQ * SEQ, D), F32, kind="ExternalOutput").ap()
    network(nc, x_d, out=out, **args)
    result = run_bass_kernel_spmd(nc, [feeds], core_ids=[0])
    return result.results[0]["out_0_dram"].reshape(x.shape)
```

```python
from contextlib import ExitStack
import concourse.bass as bass
from concourse import mybir


F32 = mybir.dt.float32
F32R = mybir.dt.float32r
BF16 = mybir.dt.bfloat16
ALU = mybir.AluOpType
ACT = mybir.ActivationFunctionType
AX = mybir.AxisListType
P = 128
D = 256
DC = D // P
SEQ = 512
T = SEQ // P
NSEQ = 16
EPS = 1e-5


class Order:

    def __init__(self, eng, sem):
        self.eng, self.sem, self.n, self.base, self.per = eng, sem, 0, 0, 0

    def link(self, ins):
        ins.then_inc(self.sem, 1)
        self.n += 1
        self.eng.wait_ge(self.sem, self.base + self.n)

    def step(self, it):
        if isinstance(it, int) and it == 0:
            self.start = self.n
        elif not self.per:
            self.per = self.n
        if self.per:
            self.base = self.start + it * self.per
        else:
            self.base = self.start
        self.n = 0


def last_step(it):
    return isinstance(it, int) and it == NSEQ - 1


def first_step(it):
    return isinstance(it, int) and it == 0


def steps(eng, body):
    body(0, 0)
    with eng.Fori(0, NSEQ // 2 - 1) as turn:
        body(turn * 2 + 1, 1)
        body(turn * 2 + 2, 0)
    body(NSEQ - 1, 1)


def sequence(v, it):
    return v[bass.ds(it, 1)].rearrange("a p t d -> p (a t) d")


def three(nc, out, w, x, start, stop, **options):
    nc.tensor.matmul(out, w[0], x[0], start=start, stop=False, **options)
    nc.tensor.matmul(out, w[1], x[0], start=False, stop=False, **options)
    return nc.tensor.matmul(out, w[0], x[1], start=False, stop=stop, **options)


def moe_phase(nc, name, src, dst, wg_d, wu_d, wd_d, gate_d, bias_d, lower_d, half_d, ident_d, shared):
    E = wg_d.shape[1]
    E0 = 1 if shared else 0
    NE = E - E0
    NT = 1 if shared else 2
    YB = T * D // SEQ
    BT = T // YB
    AHEAD = 2
    src_v = src.rearrange("(n t p) d -> n p t d", t=T, p=P)
    dst_v = dst.rearrange("(n t p) d -> n p t d", t=T, p=P)
    with ExitStack() as ctx:
        def sb(nm, shape, dt=F32):
            return ctx.enter_context(nc.sbuf_tensor(f"{name}_{nm}", shape, dt))

        def ps(nm, shape):
            return ctx.enter_context(nc.psum_tensor(f"{name}_{nm}", shape, F32))

        def sem(nm):
            return ctx.enter_context(nc.semaphore(f"{name}_{nm}"))

        wgu_raw = sb("wgu_raw", [P, 2, E * DC * P])
        wd_raw = sb("wd_raw", [P, E * D])
        gate = sb("gate", [P, DC, NE])
        wgu_hi = sb("wgu_hi", [P, 2, E * DC * P], F32R)
        wgu_lo = sb("wgu_lo", [P, 2, E * DC * P], F32R)
        wd_hi = sb("wd_hi", [P, E, D], F32R)
        wd_lo = sb("wd_lo", [P, E, D], F32R)
        bias = sb("bias", [P, NE])
        lower = sb("lower", [P, NE, NE])
        half = sb("half", [P, T])
        eps = sb("eps", [P, T])
        ident = sb("ident", [P, P])
        x_in = sb("x_in", [P, T, D])
        acc = sb("acc", [P, T, D])
        xn = sb("xn", [P, T, D])
        xT = sb("xT", [P, DC, SEQ])
        xT_hi = sb("xT_hi", [P, 2, DC, SEQ], F32R)
        xT_lo = sb("xT_lo", [P, 2, DC, SEQ], F32R)
        stats = sb("stats", [P, T, 6])
        mv = sb("mv", [P, T, 2])
        var = sb("var", [P, T])
        rstd = sb("rstd", [P, T])
        carrier = sb("carrier", [P, 1])
        s_sb = sb("s_sb", [P, 2, SEQ])
        h_sb = sb("h_sb", [P, 2, SEQ])
        h_hi = sb("h_hi", [P, 2, SEQ], F32R)
        h_lo = sb("h_lo", [P, 2, SEQ], F32R)
        score = sb("score", [P, T, NE])
        score_c = sb("score_c", [P, T, NE])
        top = sb("top", [P, T])
        rw = sb("rw", [P, T])
        group = sb("group", [P, T, NE // 2])
        wins = sb("wins", [P, T, NE * NE])
        ties = sb("ties", [P, T, NE * NE])
        rank = sb("rank", [P, T, NE])
        total = sb("total", [P, T])
        cw = sb("cw", [P, 2, T, NE])

        xT_ps = ps("xT_ps", [P, DC, SEQ])
        gu_ps = ps("gu_ps", [P, 2, 2, SEQ])
        y_ps = ps("y_ps", [P, T, D])
        logits = xT_ps[:, 0, 0:T * NE].rearrange("p (t e) -> p t e", e=NE)

        loaded = sem("loaded")
        split = sem("split")
        x_loaded = sem("x_loaded")
        var_ready = sem("var_ready")
        rstd_ready = sem("rstd_ready")
        xn_ready = sem("xn_ready")
        xT_in_psum = sem("xT_in_psum")
        xT_ready = sem("xT_ready")
        hi_ready = sem("hi_ready")
        lo_ready = sem("lo_ready")
        logits_ready = sem("logits_ready")
        top_ready = sem("top_ready")
        sig_ready = sem("sig_ready")
        routed = sem("routed")
        gu_ready = sem("gu_ready")
        silu_ready = sem("silu_ready")
        h_ready = sem("h_ready")
        hhi_ready = sem("hhi_ready")
        hlo_ready = sem("hlo_ready")
        y_ready = sem("y_ready")
        acc_done = sem("acc_done")
        stored = sem("stored")
        dve_order = sem("dve_order")
        pool_order = sem("pool_order")
        LOADS = 8 if shared else 7

        def slot(par, e):
            return (par * E + e) % 2

        block = ctx.enter_context(nc.Block())

        @block.sync
        def _(sp):
            sp.dma_start(x_in[:], src_v[0]).then_inc(x_loaded, 16)
            sp.dma_start(wgu_raw[:, 0, :], wg_d.rearrange("p e c i -> p (e c i)")).then_inc(loaded, 16)
            sp.dma_start(wgu_raw[:, 1, :], wu_d.rearrange("p e c i -> p (e c i)")).then_inc(loaded, 16)
            sp.dma_start(wd_raw[:], wd_d.rearrange("p e d -> p (e d)")).then_inc(loaded, 16)
            sp.dma_start(gate[:], gate_d).then_inc(loaded, 16)
            sp.dma_start(lower[:], lower_d).then_inc(loaded, 16)
            sp.dma_start(half[:], half_d).then_inc(loaded, 16)
            sp.dma_start(ident[:], ident_d).then_inc(loaded, 16)
            if shared:
                sp.dma_start(bias[:], bias_d).then_inc(loaded, 16)

            def body(it, par):
                if not last_step(it):
                    sp.wait_ge(acc_done, it * T * E + T)
                    sp.dma_start(x_in[:], sequence(src_v, it + 1)).then_inc(x_loaded, 16)
                sp.wait_ge(acc_done, (it + 1) * T * E)
                sp.dma_start(sequence(dst_v, it), acc[:]).then_inc(stored, 16)

            steps(sp, body)
            sp.wait_ge(stored, 16 * NSEQ)

        @block.gpsimd
        def _(pool):
            order = Order(pool, pool_order)
            pool.wait_ge(loaded, 16 * LOADS)
            order.link(nc.gpsimd.memset(eps[:], EPS))

            def body(it, par):
                order.step(it)
                pool.wait_ge(var_ready, it + 1)
                order.link(nc.gpsimd.tensor_tensor(var[:], mv[:, :, 1], eps[:], ALU.add))
                nc.gpsimd.tensor_tensor(rstd[:], var[:], half[:], ALU.pow).then_inc(rstd_ready, 1)

            steps(pool, body)

        @block.scalar
        def _(act):
            def evacuate(it, k):
                act.wait_ge(xT_in_psum, it * NT + k + 1)
                if k:
                    act.wait_ge(logits_ready, it + 1)
                elif not first_step(it):
                    act.wait_ge(lo_ready, it)
                nc.scalar.copy(xT[:], xT_ps[:]).then_inc(xT_ready, 1)

            def scores(it):
                if shared:
                    act.wait_ge(logits_ready, it + 1)
                    if not first_step(it):
                        act.wait_ge(routed, it)
                    nc.scalar.activation(score[:], logits, ACT.Sigmoid).then_inc(sig_ready, 1)
                else:
                    act.wait_ge(top_ready, it + 1)
                    nc.scalar.activation(rw[:], top[:], ACT.Sigmoid).then_inc(sig_ready, 1)

            def hi_copy(it, par):
                act.wait_ge(xT_ready, (it + 1) * NT)
                if not (isinstance(it, int) and it < 2):
                    act.wait_ge(gu_ready, (it - 1) * E)
                nc.scalar.copy(xT_hi[:, par], xT[:]).then_inc(hi_ready, 1)

            def silu(it, par, e):
                k = slot(par, e)
                act.wait_ge(gu_ready, it * E + e + 1)
                if not (first_step(it) and e < 2):
                    act.wait_ge(h_ready, it * E + e - 1)
                nc.scalar.activation(s_sb[:, k, :], gu_ps[:, k, 0, :], ACT.Silu).then_inc(silu_ready, 1)

            def h_hi_copy(it, par, e):
                k = slot(par, e)
                act.wait_ge(h_ready, it * E + e + 1)
                if not (first_step(it) and e < 2):
                    act.wait_ge(y_ready, (it * E + e - 1) * YB)
                nc.scalar.copy(h_hi[:, k, :], h_sb[:, k, :]).then_inc(hhi_ready, 1)

            act.wait_ge(loaded, 16 * LOADS)
            nc.scalar.copy(wgu_hi[:], wgu_raw[:])
            nc.scalar.copy(wd_hi[:].rearrange("p e d -> p (e d)"), wd_raw[:]).then_inc(split, 1)
            evacuate(0, 0)
            scores(0)
            if not shared:
                evacuate(0, 1)
            hi_copy(0, 0)

            def body(it, par):
                for e in range(E):
                    silu(it, par, e)
                    h_hi_copy(it, par, e)
                    if not last_step(it):
                        if e == 3:
                            evacuate(it + 1, 0)
                        if e == (4 if shared else 5):
                            scores(it + 1)
                        if e == 5:
                            if not shared:
                                evacuate(it + 1, 1)
                            hi_copy(it + 1, 1 - par)

            steps(act, body)

        @block.vector
        def _(dve):
            order = Order(dve, dve_order)
            link = order.link
            nc.vector.memset(carrier[:], 0.0)

            def stats_of(it):
                dve.wait_ge(x_loaded, (it + 1) * 16)
                for t in range(T):
                    last = nc.vector.bn_stats(stats[:, t, :], x_in[:, t, :])
                link(last)
                nc.vector.memset(carrier[:], 0.0)
                for t in range(T):
                    last = nc.vector.bn_aggr(mv[:, t, :], stats[:, t, :])
                last.then_inc(var_ready, 1)

            def normalise(it):
                dve.wait_ge(rstd_ready, it + 1)
                if not first_step(it):
                    dve.wait_ge(xT_in_psum, it * NT)
                for t in range(T):
                    last = nc.vector.tensor_scalar(xn[:, t, :], x_in[:, t, :], mv[:, t, 0:1], rstd[:, t:t + 1], ALU.subtract, ALU.mult)
                last.then_inc(xn_ready, 1)

            def ranks(a, n):
                for t in range(T):
                    me = a[:, t, 0:n].unsqueeze(2).to_broadcast([P, n, n])
                    other = a[:, t, 0:n].unsqueeze(1).to_broadcast([P, n, n])
                    nc.vector.tensor_tensor(wins[:, t, 0:n * n].rearrange("p (a b) -> p a b", b=n), other, me, ALU.is_gt)
                    last = nc.vector.tensor_tensor(ties[:, t, 0:n * n].rearrange("p (a b) -> p a b", b=n), other, me, ALU.is_equal)
                link(last)
                for t in range(T):
                    q = ties[:, t, 0:n * n].rearrange("p (a b) -> p a b", b=n)
                    last = nc.vector.tensor_tensor(q, q, lower[:, 0:n, 0:n], ALU.mult)
                link(last)
                w = wins[:, :, 0:n * n]
                link(nc.vector.tensor_tensor(w, w, ties[:, :, 0:n * n], ALU.add))
                link(nc.vector.tensor_reduce(rank[:, :, 0:n], w.rearrange("p t (a b) -> p t a b", b=n), AX.X, ALU.add))

            def route_top4(it, par):
                dve.wait_ge(sig_ready, it + 1)
                link(nc.vector.tensor_tensor(score_c[:], score[:], bias[:, :].unsqueeze(1).to_broadcast([P, T, NE]), ALU.add))
                pair = score_c[:].rearrange("p t (g k) -> p t g k", k=2)
                link(nc.vector.tensor_tensor(group[:], pair[:, :, :, 0], pair[:, :, :, 1], ALU.add))
                ranks(group, NE // 2)
                link(nc.vector.tensor_scalar(group[:], rank[:, :, 0:NE // 2], 2.0, None, ALU.is_lt))
                for k in range(2):
                    last = nc.vector.tensor_tensor(pair[:, :, :, k], pair[:, :, :, k], group[:], ALU.mult)
                link(last)
                ranks(score_c, NE)
                link(nc.vector.scalar_tensor_tensor(cw[:, par], rank[:], 4.0, score[:], ALU.is_lt, ALU.mult))
                link(nc.vector.tensor_reduce(total[:], cw[:, par], AX.X, ALU.add))
                link(nc.vector.tensor_scalar(total[:], total[:], 1e-20, None, ALU.add))
                link(nc.vector.reciprocal(total[:], total[:]))
                nc.vector.scalar_tensor_tensor(cw[:, par], cw[:, par], 2.5, total[:].unsqueeze(2).to_broadcast([P, T, NE]), ALU.mult, ALU.mult).then_inc(routed, 1)

            def route_top1(it, par):
                dve.wait_ge(logits_ready, it + 1)
                link(nc.vector.tensor_copy(score[:], logits))
                nc.vector.tensor_reduce(top[:], score[:], AX.X, ALU.max).then_inc(top_ready, 1)
                ranks(score, NE)
                link(nc.vector.tensor_scalar(cw[:, par], rank[:], 1.0, None, ALU.is_lt))

            def scale(it):
                dve.wait_ge(sig_ready, it + 1)
                dve.wait_ge(xT_in_psum, it * NT + 1)
                for t in range(T):
                    last = nc.vector.tensor_scalar(xn[:, t, :], xn[:, t, :], rw[:, t:t + 1], None, ALU.mult)
                last.then_inc(xn_ready, 1)

            def lo_sub(it, par):
                dve.wait_ge(hi_ready, it + 1)
                nc.vector.tensor_tensor(xT_lo[:, par], xT[:], xT_hi[:, par].bitcast(F32), ALU.subtract).then_inc(lo_ready, 1)

            def times_up(it, par, e):
                k = slot(par, e)
                dve.wait_ge(silu_ready, it * E + e + 1)
                if not (first_step(it) and e < 2):
                    dve.wait_ge(hhi_ready, it * E + e - 1)
                    dve.wait_ge(hlo_ready, it * E + e - 1)
                nc.vector.tensor_tensor(h_sb[:, k, :], s_sb[:, k, :], gu_ps[:, k, 1, :], ALU.mult).then_inc(h_ready, 1)

            def h_lo_sub(it, par, e):
                k = slot(par, e)
                dve.wait_ge(hhi_ready, it * E + e + 1)
                if not (first_step(it) and e < 2):
                    dve.wait_ge(y_ready, (it * E + e - 1) * YB)
                nc.vector.tensor_tensor(h_lo[:, k, :], h_sb[:, k, :], h_hi[:, k, :].bitcast(F32), ALU.subtract).then_inc(hlo_ready, 1)

            def accumulate(it, par, e):
                for t in range(T):
                    if t % BT == 0:
                        dve.wait_ge(y_ready, (it * E + e) * YB + t // BT + 1)
                    if e == 0 and t == 0 and not first_step(it):
                        dve.wait_ge(stored, it * 16)
                    if e and t == 0:
                        dve.wait_ge(acc_done, (it * E + e) * T)
                    into = x_in[:, t, :] if e == 0 else acc[:, t, :]
                    if e < E0:
                        nc.vector.tensor_tensor(acc[:, t, :], y_ps[:, t, :], into, ALU.add).then_inc(acc_done, 1)
                    else:
                        nc.vector.scalar_tensor_tensor(acc[:, t, :], y_ps[:, t, :], cw[:, par, t, e - E0:e - E0 + 1], into, ALU.mult, ALU.add).then_inc(acc_done, 1)

            stats_of(0)
            normalise(0)
            dve.wait_ge(split, 1)
            nc.vector.tensor_tensor(wgu_lo[:], wgu_raw[:], wgu_hi[:].bitcast(F32), ALU.subtract)
            nc.vector.tensor_tensor(wd_lo[:].rearrange("p e d -> p (e d)"), wd_raw[:], wd_hi[:].bitcast(F32).rearrange("p e d -> p (e d)"), ALU.subtract).then_inc(split, 1)
            if shared:
                route_top4(0, 0)
            else:
                route_top1(0, 0)
                scale(0)
            lo_sub(0, 0)

            def body(it, par):
                order.step(it)
                for e in range(E):
                    times_up(it, par, e)
                    if e:
                        accumulate(it, par, e - 1)
                    h_lo_sub(it, par, e)
                    if not last_step(it):
                        if e == 1:
                            stats_of(it + 1)
                        if e == 2:
                            normalise(it + 1)
                        if e == 5:
                            if shared:
                                route_top4(it + 1, 1 - par)
                            else:
                                route_top1(it + 1, 1 - par)
                                scale(it + 1)
                        if e == 6:
                            lo_sub(it + 1, 1 - par)
                accumulate(it, par, E - 1)

            steps(dve, body)

        @block.tensor
        def _(pe):
            wgu = [w[:].rearrange("p u (e c i) -> p u e c i", e=E, c=DC) for w in (wgu_hi, wgu_lo)]

            def transposes(it, k):
                pe.wait_ge(xn_ready, it * NT + k + 1)
                if k:
                    pe.wait_ge(top_ready, it + 1)
                elif not first_step(it):
                    pe.wait_ge(xT_ready, it * NT)
                    if shared:
                        pe.wait_ge(sig_ready, it)
                for t in range(T):
                    for c in range(DC):
                        last = nc.tensor.transpose(xT_ps[:, c, t * P:(t + 1) * P], xn[:, t, c * P:(c + 1) * P], ident[:])
                last.then_inc(xT_in_psum, 1)

            def router(it):
                pe.wait_ge(xT_ready, it * NT + 1)
                for t in range(T):
                    for c in range(DC):
                        last = nc.tensor.matmul(logits[:, t, :], xT[:, c, t * P:(t + 1) * P], gate[:, c, :], start=(c == 0), stop=(c == DC - 1))
                last.then_inc(logits_ready, 1)

            def gate_up(it, par, e):
                k = slot(par, e)
                if e == 0:
                    pe.wait_ge(lo_ready, it + 1)
                if not (first_step(it) and e < 2):
                    pe.wait_ge(h_ready, it * E + e - 1)
                for u in range(2):
                    for c in range(DC):
                        last = three(nc, gu_ps[:, k, u, :], [w[:, u, e, c, :] for w in wgu], (xT_hi[:, par, c, :], xT_lo[:, par, c, :]), c == 0, c == DC - 1)
                last.then_inc(gu_ready, 1)

            def down(it, par, e):
                k = slot(par, e)
                pe.wait_ge(hlo_ready, it * E + e + 1)
                for t in range(T):
                    if t % BT == 0 and not (first_step(it) and e == 0):
                        pe.wait_ge(acc_done, (it * E + e - 1) * T + t + BT)
                    tok = slice(t * P, (t + 1) * P)
                    last = three(nc, y_ps[:, t, :], (h_hi[:, k, tok], h_lo[:, k, tok]), (wd_hi[:, e, :], wd_lo[:, e, :]), True, True)
                    if t % BT == BT - 1:
                        last.then_inc(y_ready, 1)

            pe.wait_ge(loaded, 16 * LOADS)
            transposes(0, 0)
            router(0)
            if not shared:
                transposes(0, 1)
            pe.wait_ge(split, 2)
            for e in range(AHEAD):
                gate_up(0, 0, e)

            def body(it, par):
                for e in range(E):
                    if not last_step(it):
                        if e == 3:
                            transposes(it + 1, 0)
                        if e == 4:
                            router(it + 1)
                        if e == 6 and not shared:
                            transposes(it + 1, 1)
                    down(it, par, e)
                    if e + AHEAD < E:
                        gate_up(it, par, e + AHEAD)
                    elif not last_step(it):
                        gate_up(it + 1, 1 - par, e + AHEAD - E)

            steps(pe, body)


HEADS = 16
DH = 64
SEG = 32
SEGS = SEQ // SEG
SPT = P // SEG
PAIRS = HEADS // 2
GROUPS = 2
PU = PAIRS // GROUPS
HU = 2 * PU
GD = HU * DH
NORM = DH ** -0.5


def after(eng, sem, value):
    if not (isinstance(value, int) and value <= 0):
        eng.wait_ge(sem, value)


def attn0_phase(nc, x, out, wqk_d, wv_d, wo_d, lng_d, lnb_d, beta_rows_d, beta_heads_d, cos_d, sin_d, mask_d, sel_d, selbc_d, eps4_d, half_d, ident_d):
    x_v = x.rearrange("(n t p) d -> n p t d", t=T, p=P)
    out_v = out.rearrange("(n t p) d -> n p t d", t=T, p=P)
    sems = []
    with ExitStack() as ctx:
        def sb(nm, shape, dt=F32, c=ctx):
            return c.enter_context(nc.sbuf_tensor(f"a_{nm}", shape, dt))

        def ps(nm, shape):
            return ctx.enter_context(nc.psum_tensor(f"a_{nm}", shape, F32))

        def sem(nm):
            sems.append(nc.alloc_semaphore(f"a_{nm}"))
            return sems[-1]

        NQK = 2 * PAIRS * DC * P
        NV = DC * HEADS * DH
        NO = PAIRS * D
        wqk = [sb(f"wqk_{h}", [P, 2, PAIRS, DC, P], F32R) for h in ("hi", "lo")]
        wv = [sb(f"wv_{h}", [P, DC, HEADS * DH], F32R) for h in ("hi", "lo")]
        wo = [sb(f"wo_{h}", [P, PAIRS, D], F32R) for h in ("hi", "lo")]
        selbc = sb("selbc", [8, 2, P], F32R)
        loaded = sem("loaded")
        hi_split = sem("hi_split")
        lo_split = sem("lo_split")

        with ExitStack() as c1:
            wqk_raw = sb("wqk_raw", [P, NQK], c=c1)
            wv_raw = sb("wv_raw", [P, NV], c=c1)
            wo_raw = sb("wo_raw", [P, NO], c=c1)
            selbc_raw = sb("selbc_raw", [8, 2 * P], c=c1)
            block = c1.enter_context(nc.Block())
            flat = [(w[0][:].rearrange(r), w[1][:].rearrange(r), raw[:]) for w, raw, r in (
                (wqk, wqk_raw, "p a b c i -> p (a b c i)"), (wv, wv_raw, "p c i -> p (c i)"), (wo, wo_raw, "p j d -> p (j d)"))]

            @block.sync
            def _(sp):
                sp.dma_start(wqk_raw[:], wqk_d).then_inc(loaded, 16)
                sp.dma_start(wv_raw[:], wv_d).then_inc(loaded, 16)
                sp.dma_start(wo_raw[:], wo_d).then_inc(loaded, 16)
                sp.dma_start(selbc_raw[:], selbc_d).then_inc(loaded, 16)

            @block.scalar
            def _(act):
                act.wait_ge(loaded, 64)
                for hi, lo, raw in flat:
                    nc.scalar.copy(hi, raw).then_inc(hi_split, 1)

            @block.vector
            def _(dve):
                dve.wait_ge(loaded, 64)
                nc.vector.tensor_copy(selbc[:].rearrange("k a p -> k (a p)"), selbc_raw[:])
                for n, (hi, lo, raw) in enumerate(flat):
                    dve.wait_ge(hi_split, n + 1)
                    nc.vector.tensor_tensor(lo, raw, hi.bitcast(F32), ALU.subtract).then_inc(lo_split, 1)

        lng = sb("lng", [P, DC])
        lnb = sb("lnb", [P, DC])
        beta_rows = sb("beta_rows", [P, PAIRS])
        keep = sb("keep", [P, HEADS])
        cos = sb("cos", [P, SEQ])
        sin = sb("sin", [P, SEQ])
        mask = sb("mask", [P, SEG])
        sel = sb("sel", [P, 2, 4])
        eps4 = sb("eps4", [4, 1])
        half = sb("half", [P, T])
        eps = sb("eps", [P, T])
        ident = sb("ident", [P, P])
        ones = sb("ones", [P, SEGS])
        carrier = sb("carrier", [P, 1])

        x_ln = sb("x_ln", [P, T, D])
        x_res = sb("x_res", [P, T, D])
        acc = sb("acc", [P, T, D])
        xT = sb("xT", [P, DC, SEQ])
        xT_hi = sb("xT_hi", [P, DC, SEQ], F32R)
        xT_lo = sb("xT_lo", [P, DC, SEQ], F32R)
        stats = sb("stats", [P, T, 6])
        mv = sb("mv", [P, T, 2])
        lnt = sb("lnt", [P, 4, T])
        rstd = sb("rstd", [P, T])

        raw = sb("raw", [P, 2, SEQ])
        expo = sb("expo", [P, 2, SEQ])
        swap = sb("swap", [P, 2, SEQ])
        rope = sb("rope", [P, 2, SEQ])
        sT = sb("sT", [P, 2, SEQ])
        prod = sb("prod", [P, 2, SEQ])
        zin = sb("zin", [P, SEGS])
        z = sb("z", [P, SEGS])
        den = sb("den", [4, SEQ])
        den_r = sb("den_r", [P, SEQ // SEG])
        rec_r = sb("rec_r", [P, SEQ // SEG])
        rec_hi = sb("rec_hi", [P, SEQ // SEG], F32R)
        rec_lo = sb("rec_lo", [P, SEQ // SEG], F32R)
        rec8 = sb("rec8", [8, SEQ], F32R)

        sqn = sb("sqn", [P, GROUPS, PU, SEQ])
        skn = sb("skn", [P, GROUPS, PU, SEQ])
        sk = sb("sk", [P, GROUPS, T, GD])
        v = sb("v", [P, GROUPS, T, GD])
        s_all = sb("s_all", [P, GROUPS, T, HU * SEG])
        prob = sb("prob", [P, HU, SEG])
        smax = sb("smax", [P, HU])
        ssum = sb("ssum", [P, HU])
        pT = sb("pT", [P, HU, P])
        u = sb("u", [P, GD])
        mem = sb("mem", [P, PU, P])
        o_hi = sb("o_hi", [P, PU, P], F32R)
        o_lo = sb("o_lo", [P, PU, P], F32R)

        qk_ps = ps("qk_ps", [P, 2, SEQ])
        a_ps = ps("a_ps", [P, SEQ])
        b_ps = ps("b_ps", [P, SEQ])
        o_ps = ps("o_ps", [P, PU, P])
        prev_ps = ps("prev_ps", [P, GD])
        d_ps = ps("d_ps", [P, PU, P])
        y_ps = ps("y_ps", [P, SEQ])

        const_in = sem("const_in")
        setup = sem("setup")
        xln_in = sem("xln_in")
        xres_in = sem("xres_in")
        var_ready = sem("var_ready")
        rstd_ready = sem("rstd_ready")
        xn_ready = sem("xn_ready")
        xT_in_psum = sem("xT_in_psum")
        xT_ready = sem("xT_ready")
        xhi_ready = sem("xhi_ready")
        xlo_ready = sem("xlo_ready")
        qk_ready = sem("qk_ready")
        raw_ready = sem("raw_ready")
        exp_ready = sem("exp_ready")
        swapped = sem("swapped")
        v_in_psum = sem("v_in_psum")
        v_ready = sem("v_ready")
        s_ready = sem("s_ready")
        z_ready = sem("z_ready")
        prod_ready = sem("prod_ready")
        sk_in_psum = sem("sk_in_psum")
        sk_ready = sem("sk_ready")
        den_in_psum = sem("den_in_psum")
        den_ready = sem("den_ready")
        den_spread = sem("den_spread")
        rec_ready = sem("rec_ready")
        rec_rows = sem("rec_rows")
        bc_ready = sem("bc_ready")
        norm_done = sem("norm_done")
        sin_part = sem("sin_part")
        rope_ready = sem("rope_ready")
        sc_in_psum = sem("sc_in_psum")
        sc_ready = sem("sc_ready")
        sub_ready = sem("sub_ready")
        p_ready = sem("p_ready")
        pT_ready = sem("pT_ready")
        sdpa_done = sem("sdpa_done")
        prev_ready = sem("prev_ready")
        u_ready = sem("u_ready")
        d_ready = sem("d_ready")
        mem_ready = sem("mem_ready")
        o_ready = sem("o_ready")
        ohi_ready = sem("ohi_ready")
        olo_ready = sem("olo_ready")
        y_ready = sem("y_ready")
        acc_done = sem("acc_done")
        stored = sem("stored")
        dve_order = sem("dve_order")
        pool_order = sem("pool_order")

        NU = SEGS - 2
        NM = SEGS - 1
        CONSTS = 13
        block = ctx.enter_context(nc.Block())

        def units(eng, body):
            body(0)
            with eng.Fori(1, NSEQ - 1) as it:
                body(it)
            body(NSEQ - 1)

        def slots(it):
            for g in range(GROUPS):
                for t in range(T):
                    Z = (it * GROUPS + g) * T + t
                    it1, g1 = (it, 1) if g == 0 else (it + 1, 0)
                    yield g, t, Z, (None if g and last_step(it) else (it1, g1, t, Z + T))

        def buffers_free(j, Y):
            return Y - j - PU

        @block.sync
        def _(sp):
            for dst, src in ((lng, lng_d), (lnb, lnb_d), (cos, cos_d), (sin, sin_d), (mask, mask_d), (sel, sel_d), (eps4, eps4_d), (half, half_d), (ident, ident_d)):
                sp.dma_start(dst[:], src).then_inc(const_in, 16)
            sp.dma_start(beta_rows[0:64, :], beta_rows_d).then_inc(const_in, 16)
            sp.dma_start(keep[:], beta_heads_d).then_inc(const_in, 16)
            sp.dma_start(x_ln[:], x_v[0]).then_inc(xln_in, 16)
            sp.dma_start(x_res[:], x_v[0]).then_inc(xres_in, 16)

            def part1(it, g, j, Y):
                sp.wait_ge(raw_ready, Y + 1)
                for h in range(2):
                    for a in range(2):
                        to, fr = 64 * h + 32 * a, 64 * h + 32 * (1 - a)
                        sp.dma_start(swap[to:to + 32], raw[fr:fr + 32]).then_inc(swapped, 16)
                sp.wait_ge(den_ready, Y + 1)
                sp.dma_start(den_r[:], den[:].rearrange("r (c k) -> r c k", k=16)).then_inc(den_spread, 16)
                sp.wait_ge(rec_ready, Y + 1)
                sp.dma_start(rec8[0:4].bitcast(F32).rearrange("r (c k) -> r c k", k=16), rec_hi[:].bitcast(F32)).then_inc(rec_rows, 16)
                sp.dma_start(rec8[4:8].bitcast(F32).rearrange("r (c k) -> r c k", k=16), rec_lo[:].bitcast(F32)).then_inc(rec_rows, 16)

            def store(it, t, Z):
                sp.wait_ge(acc_done, Z)
                sp.dma_start(out_v[bass.ds(it, 1), :, t].rearrange("a p d -> p (a d)"), acc[:, t]).then_inc(stored, 16)

            for j in range(PU):
                part1(0, 0, j, j)

            def body(it):
                before = None if first_step(it) else sp.snap(it - 1)
                for g, t, Z, nxt in slots(it):
                    if nxt:
                        part1(*nxt)
                    if g == 0 and t == 0 and not last_step(it):
                        sp.wait_ge(xT_in_psum, it + 1)
                        sp.dma_start(x_ln[:], sequence(x_v, it + 1)).then_inc(xln_in, 16)
                    if g == 1 and t == 1 and not last_step(it):
                        sp.wait_ge(acc_done, it * 2 * T + T)
                        sp.dma_start(x_res[:], sequence(x_v, it + 1)).then_inc(xres_in, 16)
                    if g == 1 and t:
                        store(it, t - 1, Z)
                    if g == 0 and t == 0 and not first_step(it):
                        store(before, T - 1, Z)

            units(sp, body)
            sp.wait_ge(acc_done, NSEQ * 2 * T)
            sp.dma_start(out_v[NSEQ - 1, :, T - 1], acc[:, T - 1]).then_inc(stored, 16)
            sp.wait_ge(stored, 16 * NSEQ * T)

        @block.gpsimd
        def _(pool):
            order = Order(pool, pool_order)
            pool.wait_ge(const_in, 16 * 11)
            order.link(nc.gpsimd.memset(eps[:], EPS))

            def inverse_deviation(it):
                pool.wait_ge(var_ready, it + 1)
                order.link(nc.gpsimd.tensor_tensor(lnt[:, 0], mv[:, :, 1], eps[:], ALU.add))
                order.link(nc.gpsimd.tensor_tensor(lnt[:, 1], lnt[:, 0], half[:], ALU.pow))
                order.link(nc.gpsimd.tensor_tensor(lnt[:, 2], lnt[:, 1], lnt[:, 1], ALU.mult))
                order.link(nc.gpsimd.tensor_tensor(lnt[:, 0], lnt[:, 2], mv[:, :, 1], ALU.mult))
                order.link(nc.gpsimd.tensor_tensor(lnt[:, 2], lnt[:, 0], eps[:], ALU.add))
                order.link(nc.gpsimd.tensor_tensor(lnt[:, 3], lnt[:, 2], half[:], ALU.pow))
                nc.gpsimd.tensor_tensor(rstd[:], lnt[:, 1], lnt[:, 3], ALU.mult).then_inc(rstd_ready, 1)

            def part1(it, g, j, Y):
                pool.wait_ge(swapped, 64 * (Y + 1))
                nc.gpsimd.tensor_tensor(swap[:], swap[:], sin[:].unsqueeze(1).to_broadcast([P, 2, SEQ]), ALU.mult).then_inc(sin_part, 1)
                pool.wait_ge(z_ready, Y + 1)
                after(pool, den_in_psum, Y)
                four = lambda a: a[:].rearrange("p a (w k) -> p a w k", k=SEG)
                nc.gpsimd.tensor_tensor(four(prod), four(sT), z[:].unsqueeze(1).unsqueeze(3).to_broadcast([P, 2, SEGS, SEG]), ALU.mult).then_inc(prod_ready, 1)

            inverse_deviation(0)
            for j in range(PU):
                part1(0, 0, j, j)

            def body(it):
                order.step(it)
                for g, t, Z, nxt in slots(it):
                    if g == 0 and t == 3 and not last_step(it):
                        inverse_deviation(it + 1)
                    if nxt:
                        part1(*nxt)

            units(pool, body)

        @block.scalar
        def _(act):
            act.wait_ge(const_in, 16 * 11)
            nc.scalar.activation(beta_rows[0:64, :], beta_rows[0:64, :], ACT.Sigmoid).then_inc(setup, 1)
            nc.scalar.activation(keep[:], keep[:], ACT.Sigmoid).then_inc(setup, 1)

            def x_hi(it):
                act.wait_ge(xT_ready, it + 1)
                after(act, v_in_psum, it * 2 * PU)
                nc.scalar.copy(xT_hi[:], xT[:]).then_inc(xhi_ready, 1)

            def project(it, g, j, Y):
                act.wait_ge(qk_ready, Y + 1)
                after(act, rope_ready, Y)
                after(act, s_ready, Y)
                nc.scalar.copy(raw[:], qk_ps[:]).then_inc(raw_ready, 1)
                nc.scalar.activation(expo[:], qk_ps[:], ACT.Exp).then_inc(exp_ready, 1)

            def values(it, g, j, Y):
                act.wait_ge(v_in_psum, Y + 1)
                after(act, y_ready, buffers_free(j, Y))
                nc.scalar.copy(v[:, g, j], b_ps[:]).then_inc(v_ready, 1)

            def keys(it, g, j, Y):
                act.wait_ge(sk_in_psum, Y + 1)
                nc.scalar.copy(sk[:, g, :, j * P:(j + 1) * P], b_ps[:].rearrange("p (t i) -> p t i", t=T)).then_inc(sk_ready, 1)

            def denominators(it, g, j, Y):
                act.wait_ge(den_in_psum, Y + 1)
                after(act, den_spread, 16 * Y)
                nc.scalar.activation(den[:], a_ps[0:4, :], ACT.Identity, bias=eps4[:]).then_inc(den_ready, 1)

            x_hi(0)
            for j in range(PU):
                for f in (project, values, keys, denominators):
                    f(0, 0, j, j)

            def body(it):
                for g, t, Z, nxt in slots(it):
                    act.wait_ge(sub_ready, Z + 1)
                    after(act, pT_ready, Z)
                    nc.scalar.activation(prob[:], s_all[:, g, t].rearrange("p (h k) -> p h k", k=SEG), ACT.Exp).then_inc(p_ready, 1)
                    if nxt:
                        if g == 1 and t == 0:
                            x_hi(it + 1)
                        for f in (project, values, keys, denominators):
                            f(*nxt)
                    act.wait_ge(o_ready, Z + 1)
                    after(act, y_ready, Z)
                    nc.scalar.copy(o_hi[:], o_ps[:]).then_inc(ohi_ready, 1)

            units(act, body)

        @block.vector
        def _(dve):
            order = Order(dve, dve_order)
            link = order.link
            nc.vector.memset(carrier[:], 0.0)
            nc.vector.memset(zin[:], 1e-6)
            nc.vector.memset(ones[:], 1.0)
            nc.vector.memset(beta_rows[64:128, :], 1.0)
            nc.vector.memset(mem[:].rearrange("p j e -> p (j e)"), 0.0)
            nc.vector.memset(pT[:].rearrange("p h q -> p (h q)"), 0.0)
            dve.wait_ge(setup, 2)
            link(nc.vector.tensor_scalar(keep[:], keep[:], -1.0, 1.0, ALU.mult, ALU.add))

            def norm(it):
                dve.wait_ge(xln_in, 16 * (it + 1))
                for t in range(T):
                    last = nc.vector.bn_stats(stats[:, t], x_ln[:, t])
                link(last)
                nc.vector.memset(carrier[:], 0.0)
                for t in range(T):
                    last = nc.vector.bn_aggr(mv[:, t], stats[:, t])
                last.then_inc(var_ready, 1)

            def norm2(it):
                dve.wait_ge(rstd_ready, it + 1)
                for t in range(T):
                    last = nc.vector.tensor_scalar(x_ln[:, t], x_ln[:, t], mv[:, t, 0:1], rstd[:, t:t + 1], ALU.subtract, ALU.mult)
                last.then_inc(xn_ready, 1)

            def x_affine(it):
                dve.wait_ge(xT_in_psum, it + 1)
                for c in range(DC):
                    last = nc.vector.tensor_scalar(xT[:, c], qk_ps[:, c], lng[:, c:c + 1], lnb[:, c:c + 1], ALU.mult, ALU.add)
                last.then_inc(xT_ready, 1)
                dve.wait_ge(xhi_ready, it + 1)
                nc.vector.tensor_tensor(xT_lo[:], xT[:], xT_hi[:].bitcast(F32), ALU.subtract).then_inc(xlo_ready, 1)

            def elu(it, g, j, Y):
                dve.wait_ge(exp_ready, Y + 1)
                link(nc.vector.tensor_scalar(expo[:], expo[:], 1.0, None, ALU.min))
                after(dve, sk_in_psum, Y)
                after(dve, prod_ready, Y)
                nc.vector.scalar_tensor_tensor(sT[:], raw[:], 1.0, expo[:], ALU.add, ALU.max).then_inc(s_ready, 1)

            def rope_cos(it, g, j, Y):
                after(dve, sc_in_psum, Y)
                dve.wait_ge(raw_ready, Y + 1)
                link(nc.vector.tensor_tensor(rope[:], raw[:], cos[:].unsqueeze(1).to_broadcast([P, 2, SEQ]), ALU.mult))

            def memory_z(it, g, j, Y):
                dve.wait_ge(s_ready, Y + 1)
                link(nc.vector.tensor_reduce(zin[:, 1:SEGS], sT[:, 1, 0:(SEGS - 1) * SEG].rearrange("p (w k) -> p w k", k=SEG), AX.X, ALU.add))
                after(dve, prod_ready, Y)
                nc.vector.tensor_tensor_scan(z[:], ones[:], zin[:], 0.0, ALU.mult, ALU.add).then_inc(z_ready, 1)

            def rope_sum(it, g, j, Y):
                dve.wait_ge(sin_part, Y + 1)
                nc.vector.tensor_tensor(rope[:], rope[:], swap[:], ALU.add).then_inc(rope_ready, 1)

            def scores(it, g, j, Y):
                dve.wait_ge(sc_in_psum, Y + 1)
                for h in range(2):
                    k = slice((2 * j + h) * SEG, (2 * j + h + 1) * SEG)
                    last = nc.vector.scalar_tensor_tensor(
                        s_all[:, g, :, k], (a_ps, b_ps)[h][:, 0:T * SEG].rearrange("p (t k) -> p t k", t=T), NORM,
                        mask[:].unsqueeze(1).to_broadcast([P, T, SEG]), ALU.mult, ALU.add)
                last.then_inc(sc_ready, 1)

            def inverses(it, g, j, Y):
                p = g * PU + j
                dve.wait_ge(den_spread, 16 * (Y + 1))
                after(dve, rec_rows, 32 * Y)
                link(nc.vector.reciprocal(rec_r[:], den_r[:]))
                link(nc.vector.tensor_scalar(rec_r[:], rec_r[:], beta_rows[:, p:p + 1], None, ALU.mult))
                link(nc.vector.tensor_copy(rec_hi[:], rec_r[:]))
                nc.vector.tensor_tensor(rec_lo[:], rec_r[:], rec_hi[:].bitcast(F32), ALU.subtract).then_inc(rec_ready, 1)

            def normalise(it, g, j, Y):
                dve.wait_ge(bc_ready, Y + 1)
                after(dve, y_ready, buffers_free(j, Y))
                nc.vector.tensor_tensor(sqn[:, g, j], sT[:, 0], a_ps[:], ALU.mult)
                nc.vector.tensor_tensor(skn[:, g, j], sT[:, 1], b_ps[:], ALU.mult).then_inc(norm_done, 1)

            def softmax(g, t, Z):
                s = s_all[:, g, t].rearrange("p (h k) -> p h k", k=SEG)
                if t == 0:
                    dve.wait_ge(sc_ready, Z + T)
                link(nc.vector.tensor_reduce(smax[:], s, AX.X, ALU.max))
                nc.vector.tensor_tensor(s, s, smax[:].unsqueeze(2).to_broadcast([P, HU, SEG]), ALU.subtract).then_inc(sub_ready, 1)

            def softmax2(g, t, Z):
                dve.wait_ge(p_ready, Z + 1)
                link(nc.vector.tensor_reduce(ssum[:], prob[:], AX.X, ALU.add))
                link(nc.vector.reciprocal(ssum[:], ssum[:]))
                link(nc.vector.tensor_tensor(ssum[:], ssum[:], keep[:, g * HU:(g + 1) * HU], ALU.mult))
                link(nc.vector.tensor_tensor(prob[:], prob[:], ssum[:].unsqueeze(2).to_broadcast([P, HU, SEG]), ALU.mult))
                after(dve, sdpa_done, Z)
                for s in range(SPT):
                    q = slice(s * SEG, (s + 1) * SEG)
                    last = nc.vector.transpose(pT[q, :, q], prob[q])
                last.then_inc(pT_ready, 1)

            def make_u(g, t, s, U):
                w = t * SPT + s
                q = slice(s * SEG, (s + 1) * SEG)
                if 1 <= w < SEGS - 1:
                    dve.wait_ge(prev_ready, U * NU + w)
                    nc.vector.tensor_tensor(u[q], v[q, g, t], prev_ps[q], ALU.subtract).then_inc(u_ready, 1)

            def update(g, t, s, U):
                w = t * SPT + s
                if w < SEGS - 1:
                    dve.wait_ge(d_ready, U * NM + w + 1)
                    if w:
                        dve.wait_ge(mem_ready, U * NM + w)
                    for h in range(2):
                        d = slice(h * DH, (h + 1) * DH)
                        if w:
                            last = nc.vector.tensor_tensor(mem[d, :, d], mem[d, :, d], d_ps[d, :, d], ALU.add)
                        else:
                            last = nc.vector.tensor_copy(mem[d, :, d], d_ps[d, :, d])
                    last.then_inc(mem_ready, 1)

            def o_low(Z):
                dve.wait_ge(ohi_ready, Z + 1)
                nc.vector.tensor_tensor(o_lo[:], o_ps[:], o_hi[:].bitcast(F32), ALU.subtract).then_inc(olo_ready, 1)

            def add_y(it, g, t, Z):
                dve.wait_ge(y_ready, Z + 1)
                if g == 0:
                    dve.wait_ge(xres_in, 16 * (it + 1))
                    after(dve, stored, (it - 1) * 16 * T + 16 * (t + 1))
                else:
                    dve.wait_ge(acc_done, Z - T + 1)
                nc.vector.tensor_tensor(acc[:, t], y_ps[:, 0:D], (acc if g else x_res)[:, t], ALU.add).then_inc(acc_done, 1)

            norm(0)
            norm2(0)
            x_affine(0)
            for j in range(PU):
                for f in (elu, memory_z, rope_cos, rope_sum, scores, inverses, normalise):
                    f(0, 0, j, j)

            def body(it):
                order.step(it)
                for g, t, Z, nxt in slots(it):
                    U = it * GROUPS + g
                    do = lambda f: nxt and f(*nxt)
                    softmax(g, t, Z)
                    softmax2(g, t, Z)
                    if g == 1 and t == 0 and nxt:
                        x_affine(it + 1)
                    do(elu)
                    make_u(g, t, 0, U)
                    do(memory_z)
                    update(g, t, 0, U)
                    if t:
                        add_y(it, g, t - 1, Z - 1)
                    elif g:
                        add_y(it, 0, T - 1, Z - 1)
                    elif not first_step(it):
                        add_y(it - 1, 1, T - 1, Z - 1)
                    do(rope_cos)
                    make_u(g, t, 1, U)
                    update(g, t, 1, U)
                    do(rope_sum)
                    make_u(g, t, 2, U)
                    do(inverses)
                    update(g, t, 2, U)
                    do(scores)
                    make_u(g, t, 3, U)
                    update(g, t, 3, U)
                    o_low(Z)
                    do(normalise)
                    if g == 0 and not last_step(it):
                        if t == 2:
                            norm(it + 1)
                        if t == 3:
                            norm2(it + 1)
                if last_step(it):
                    add_y(it, 1, T - 1, Z)

            units(dve, body)

        @block.tensor
        def _(pe):
            pe.wait_ge(const_in, 16 * 11)
            pe.wait_ge(lo_split, 3)

            def x_transposes(it):
                pe.wait_ge(xn_ready, it + 1)
                after(pe, exp_ready, it * 2 * PU)
                for t in range(T):
                    for c in range(DC):
                        last = nc.tensor.transpose(qk_ps[:, c, t * P:(t + 1) * P], x_ln[:, t, c * P:(c + 1) * P], ident[:])
                last.then_inc(xT_in_psum, 1)

            def project(it, g, j, Y):
                if g == 0 and j == 0:
                    pe.wait_ge(xlo_ready, it + 1)
                after(pe, exp_ready, Y)
                p = g * PU + j
                for a in range(2):
                    for c in range(DC):
                        last = three(nc, qk_ps[:, a], [w[:, a, p, c] for w in wqk], (xT_hi[:, c], xT_lo[:, c]), c == 0, c == DC - 1)
                last.then_inc(qk_ready, 1)

            def values(it, g, j, Y):
                after(pe, norm_done, Y)
                tok = slice(j * P, (j + 1) * P)
                for c in range(DC):
                    last = three(nc, b_ps[:], (xT_hi[:, c, tok], xT_lo[:, c, tok]), [w[:, c, g * GD:(g + 1) * GD] for w in wv], c == 0, c == DC - 1)
                last.then_inc(v_in_psum, 1)

            def keys(it, g, j, Y):
                pe.wait_ge(s_ready, Y + 1)
                pe.wait_ge(v_ready, Y + 1)
                for t in range(T):
                    last = nc.tensor.transpose(b_ps[:, t * P:(t + 1) * P], sT[:, 1, t * P:(t + 1) * P], ident[:])
                last.then_inc(sk_in_psum, 1)

            def denominators(it, g, j, Y):
                pe.wait_ge(prod_ready, Y + 1)
                after(pe, norm_done, Y)
                for a in range(2):
                    last = nc.tensor.matmul(a_ps[0:4, :], sel[:, a, :], prod[:, a, :], start=(a == 0), stop=(a == 1))
                last.then_inc(den_in_psum, 1)

            def scores(it, g, j, Y, tiles):
                if 0 in tiles:
                    pe.wait_ge(rope_ready, Y + 1)
                    pe.wait_ge(sk_ready, Y + 1)
                    pe.wait_ge(den_ready, Y + 1)
                    nc.tensor.matmul(b_ps[0:SEG, 0:2], ident[:, 0:SEG], ident[:, 0:2], start=True, stop=True)
                for t in tiles:
                    for s in range(SPT):
                        tok = slice(t * P + s * SEG, t * P + (s + 1) * SEG)
                        for h in range(2):
                            d = slice(h * DH, (h + 1) * DH)
                            last = nc.tensor.matmul((a_ps, b_ps)[h][s * SEG:(s + 1) * SEG, t * SEG:(t + 1) * SEG], rope[d, 0, tok], rope[d, 1, tok], start=True, stop=True)
                if T - 1 in tiles:
                    last.then_inc(sc_in_psum, 1)

            def broadcast(it, g, j, Y):
                pe.wait_ge(rec_rows, 32 * (Y + 1))
                pe.wait_ge(sc_ready, Y + 1)
                pe.wait_ge(den_ready, Y + 1)
                nc.tensor.matmul(a_ps[:], selbc[:, 0, :], rec8[:], start=True, stop=True)
                nc.tensor.matmul(b_ps[:], selbc[:, 1, :], rec8[:], start=True, stop=True).then_inc(bc_ready, 1)

            def sdpa(g, t, Z):
                pe.wait_ge(pT_ready, Z + 1)
                after(pe, olo_ready, Z)
                if t == 0:
                    pe.wait_ge(norm_done, Z + T)
                for h in range(HU):
                    e = slice((h % 2) * DH, (h % 2 + 1) * DH)
                    last = nc.tensor.matmul(o_ps[e, h // 2, :], v[:, g, t, h * DH:(h + 1) * DH], pT[:, h, :], start=(h < 2), stop=False, skip_group_check=True)
                last.then_inc(sdpa_done, 1)

            def recall(g, t, s, U):
                w = t * SPT + s
                if w == 0:
                    return
                pe.wait_ge(mem_ready, U * NM + w)
                tok = slice(w * SEG, (w + 1) * SEG)
                q = slice(s * SEG, (s + 1) * SEG)
                if w < SEGS - 1:
                    after(pe, u_ready, U * NU + w - 1)
                    for j in range(PU):
                        last = nc.tensor.matmul(prev_ps[q, j * P:(j + 1) * P], skn[:, g, j, tok], mem[:, j, :], start=True, stop=True)
                    last.then_inc(prev_ready, 1)
                for j in range(PU):
                    last = nc.tensor.matmul(o_ps[:, j, q], mem[:, j, :], sqn[:, g, j, tok], start=False, stop=True, skip_group_check=True)
                if s == SPT - 1:
                    last.then_inc(o_ready, 1)

            def store(g, t, s, U, Z):
                w = t * SPT + s
                q = slice(s * SEG, (s + 1) * SEG)
                if w < SEGS - 1:
                    if w:
                        pe.wait_ge(u_ready, U * NU + w)
                    after(pe, mem_ready, U * NM + w)
                    for j in range(PU):
                        e = slice(j * P, (j + 1) * P)
                        last = nc.tensor.matmul(d_ps[:, j, :], sk[q, g, t, e], u[q, e] if w else v[q, g, t, e], start=True, stop=True)
                    last.then_inc(d_ready, 1)

            def project_out(g, t, Z):
                pe.wait_ge(olo_ready, Z + 1)
                after(pe, acc_done, Z)
                for j in range(PU):
                    last = three(nc, y_ps[:, 0:D], (o_hi[:, j], o_lo[:, j]), [w[:, g * PU + j] for w in wo], j == 0, j == PU - 1)
                last.then_inc(y_ready, 1)

            x_transposes(0)
            for j in range(PU):
                for f in (project, values, keys, denominators):
                    f(0, 0, j, j)
                scores(0, 0, j, j, range(T))
                broadcast(0, 0, j, j)

            def body(it):
                for g, t, Z, nxt in slots(it):
                    U = it * GROUPS + g
                    do = lambda f, *a: nxt and f(*nxt, *a)
                    if g == 1 and t == 0 and nxt:
                        x_transposes(it + 1)
                    do(project)
                    sdpa(g, t, Z)
                    recall(g, t, 0, U)
                    do(values)
                    store(g, t, 0, U, Z)
                    if t:
                        project_out(g, t - 1, Z - 1)
                    elif g:
                        project_out(0, T - 1, Z - 1)
                    elif not first_step(it):
                        project_out(1, T - 1, Z - 1)
                    recall(g, t, 1, U)
                    do(keys)
                    store(g, t, 1, U, Z)
                    do(denominators)
                    recall(g, t, 2, U)
                    do(scores, range(T // 2))
                    store(g, t, 2, U, Z)
                    do(scores, range(T // 2, T))
                    recall(g, t, 3, U)
                    store(g, t, 3, U, Z)
                    do(broadcast)
                if last_step(it):
                    project_out(1, T - 1, Z)

            units(pe, body)

    nc.clear_and_free_semaphores(sems)
    nc.all_engine_barrier()


H1 = 16
DH1 = D // H1
PAIRS1 = H1 // 2
NS = T * H1 // 2
KB = 2 * P
STATE = 64
DFF = 4 * D
MF = DFF // P
LAG_T, LAG_P = 3, 5
ROWS = 32
OC = H1 * ROWS // P


def attn1_phase(nc, x, out, wqk_d, wvg_d, bw_d, cw_d, wo_d, w1_d, w2_d, spread_d, cols_d, rows_d, b1_d, a_d, window_d, half_d, ident_d):
    x_v = x.rearrange("(n t p) d -> n p t d", t=T, p=P)
    out_v = out.rearrange("(n t p) d -> n p t d", t=T, p=P)
    with ExitStack() as ctx:
        def sb(nm, shape, dt=F32, c=ctx):
            return c.enter_context(nc.sbuf_tensor(f"c_{nm}", shape, dt))

        def ps(nm, shape):
            return ctx.enter_context(nc.psum_tensor(f"c_{nm}", shape, F32))

        def sem(nm):
            return ctx.enter_context(nc.semaphore(f"c_{nm}"))

        def halves(nm, shape):
            return [sb(f"{nm}_{h}", shape, F32R) for h in ("hi", "lo")]

        wqk = halves("wqk", [P, DC, 2 * D])
        wvg = halves("wvg", [P, DC, 2 * D])
        bw = halves("bw", [P, DC, P])
        cw = halves("cw", [P, D])
        wo = halves("wo", [P, OC, D])
        w1 = halves("w1", [P, DC, DFF])
        w2 = halves("w2", [P, MF, D])
        spread = sb("spread", [P, 4, 4, P], F32R)
        loaded = sem("loaded")
        hi_split = sem("hi_split")
        lo_split = sem("lo_split")

        with ExitStack() as c1:
            block = c1.enter_context(nc.Block())
            parts = []
            for n, (w, src) in enumerate(((wqk, wqk_d), (wvg, wvg_d), (bw, bw_d), (cw, cw_d), (wo, wo_d), (w1, w1_d), (w2, w2_d))):
                hi, lo = [h[:] if len(h.shape) == 2 else h[:].rearrange("p c i -> p (c i)") for h in w]
                parts.append((hi, lo, sb(f"raw{n}", [P, src.shape[1]], c=c1), src))

            spread_raw = sb("spread_raw", [P, 16 * P], c=c1)

            @block.sync
            def _(sp):
                sp.dma_start(spread_raw[:], spread_d).then_inc(loaded, 16)
                for hi, lo, raw, src in parts:
                    sp.dma_start(raw[:], src).then_inc(loaded, 16)

            @block.scalar
            def _(act):
                act.wait_ge(loaded, 16 * (len(parts) + 1))
                nc.scalar.copy(spread[:].rearrange("p a b m -> p (a b m)"), spread_raw[:])
                for hi, lo, raw, src in parts:
                    nc.scalar.copy(hi, raw[:]).then_inc(hi_split, 1)

            @block.vector
            def _(dve):
                for n, (hi, lo, raw, src) in enumerate(parts):
                    dve.wait_ge(hi_split, n + 1)
                    nc.vector.tensor_tensor(lo, raw[:], hi.bitcast(F32), ALU.subtract).then_inc(lo_split, 1)

        cols = sb("cols", [P, 12])
        rows = sb("rows", [P, 4, D])
        b1 = sb("b1", [P, MF])
        a = sb("a", [P, 1])
        half = sb("half", [P, T])
        eps = sb("eps", [P, T])
        ident = sb("ident", [P, P])
        identb = sb("identb", [P, P], BF16)
        window = sb("window", [P, KB])
        maskb = sb("maskb", [P, 2, KB], BF16)
        carrier = sb("carrier", [P, 1])
        table = sb("table", [P, 1])
        ln1_g, ln1_b, bq, bk, ln2_g, ln2_b = (cols[:, n * 2:n * 2 + 2] for n in range(6))

        x_in = sb("x_in", [P, T, D])
        y = sb("y", [P, T, D])
        xb = sb("xb", [P, T, D])
        stats = sb("stats", [P, T, 6])
        mv = sb("mv", [P, T, 2])
        lnt = sb("lnt", [P, 5, T])
        hT = sb("hT", [P, DC, SEQ])
        hT_hl = halves("hT", [P, DC, SEQ])
        qk_hl = [halves(n, [P, DC, SEQ]) for n in ("q", "k")]
        q4 = sb("q4", [P, PAIRS1, SEQ], F32R)
        k4 = sb("k4", [P, PAIRS1, SEQ], F32R)
        v = sb("v", [P, T, H1, ROWS])
        gate = sb("gate", [P, T, D])
        state = sb("state", [P, SEQ])
        state_hl = sb("state_hl", [P, SEQ], F32R)
        nmax = sb("nmax", [P, 4, 2])
        prob = sb("prob", [P, 4, 2, KB])
        pT = sb("pT", [P, 2, 2, 2, P])
        psum = sb("psum", [P, 4, 2])
        inv = sb("inv", [P, 4, 2])
        aoT_hl = halves("aoT", [P, OC, P])
        mixed = sb("mixed", [P, 2, D])
        t1 = sb("t1", [P, D])
        x1 = y
        res = sb("res", [P, T, D])
        stats2 = sb("stats2", [P, T, 6])
        mv2 = sb("mv2", [P, T, 2])
        lnt2 = sb("lnt2", [P, 2, T])
        h2T = hT
        h2T_hl = halves("h2T", [P, DC, SEQ])
        ff = sb("ff", [P, 2, SEQ])
        hn = ff[:].rearrange("p a (b d) -> p (a b) d", d=D)
        ff_hl = halves("ff", [P, 2, SEQ])

        s_ps = ps("s_ps", [P, 2, 2, KB])
        t_ps = ps("t_ps", [P, 2, 2, 2, P])
        o_ps = ps("o_ps", [P, 512])
        ab_ps = ps("ab_ps", [P, 2, SEQ])
        c_ps = ps("c_ps", [P, 2, D])
        oT = [bank.rearrange("p (g q) -> p g q", q=P) for bank in (o_ps[:], ab_ps[:, 0]) * 2]
        y_ps = s_ps[:].rearrange("p s h k -> p (s h) k")

        const_in = sem("const_in")
        const_ready = sem("const_ready")
        x_loaded = sem("x_loaded")
        var_ready = sem("var_ready")
        rstd_ready = sem("rstd_ready")
        hn_ready = sem("hn_ready")
        hT_in_psum = sem("hT_in_psum")
        hT_ready = sem("hT_ready")
        hhi_ready = sem("hhi_ready")
        hlo_ready = sem("hlo_ready")
        q_in_psum = sem("q_in_psum")
        qhi_ready = sem("qhi_ready")
        qlo_ready = sem("qlo_ready")
        q4_in_psum = sem("q4_in_psum")
        q4_ready = sem("q4_ready")
        k4_in_psum = sem("k4_in_psum")
        k4_ready = sem("k4_ready")
        vg_in_psum = sem("vg_in_psum")
        vg_ready = sem("vg_ready")
        gate_ready = sem("gate_ready")
        in_in_psum = sem("in_in_psum")
        state_ready = sem("state_ready")
        statehi_ready = sem("statehi_ready")
        statelo_ready = sem("statelo_ready")
        s_ready = sem("s_ready")
        max_ready = sem("max_ready")
        exp_ready = sem("exp_ready")
        t_ready = sem("t_ready")
        pT_ready = sem("pT_ready")
        pv_done = sem("pv_done")
        inv_ready = sem("inv_ready")
        norm_ready = sem("norm_ready")
        aohi_ready = sem("aohi_ready")
        aolo_ready = sem("aolo_ready")
        mix_in_psum = sem("mix_in_psum")
        mix_copied = sem("mix_copied")
        gate_done = sem("gate_done")
        x1_done = sem("x1_done")
        res_ready = sem("res_ready")
        xb_ready = sem("xb_ready")
        var2_ready = sem("var2_ready")
        rstd2_ready = sem("rstd2_ready")
        h2n_ready = sem("h2n_ready")
        h2T_in_psum = sem("h2T_in_psum")
        h2T_ready = sem("h2T_ready")
        h2hi_ready = sem("h2hi_ready")
        h2lo_ready = sem("h2lo_ready")
        ff_in_psum = sem("ff_in_psum")
        ff_ready = sem("ff_ready")
        ffhi_ready = sem("ffhi_ready")
        fflo_ready = sem("fflo_ready")
        y_in_psum = sem("y_in_psum")
        result_ready = sem("result_ready")
        stored = sem("stored")
        dve_order = sem("dve_order")
        pool_order = sem("pool_order")
        CONSTS = 7

        block = ctx.enter_context(nc.Block())

        def bodies(eng, body):
            body(0)
            with eng.Fori(1, NSEQ - 1) as it:
                body(it)
            body(NSEQ - 1)

        def keys_of(i):
            return slice(0 if i else P, KB)

        def head_of(j, h):
            return 4 * (j // 2) + 2 * h + j % 2

        def blocks_of(i):
            return range(0 if i else 1, 2)

        @block.sync
        def _(sp):
            for dst, src in ((cols, cols_d), (rows, rows_d), (b1, b1_d), (a, a_d), (half, half_d), (ident, ident_d), (window, window_d)):
                sp.dma_start(dst[:], src).then_inc(const_in, 16)
            sp.dma_start(x_in[:], x_v[0]).then_inc(x_loaded, 16)

            def load(it):
                sp.wait_ge(hn_ready, it)
                sp.wait_ge(xb_ready, it)
                sp.dma_start(x_in[:], sequence(x_v, it)).then_inc(x_loaded, 16)

            def body(it):
                if not last_step(it):
                    load(it + 1)
                sp.wait_ge(result_ready, (it + 1) * T)
                sp.dma_start(sequence(out_v, it), res[:]).then_inc(stored, 16)

            bodies(sp, body)
            sp.wait_ge(stored, 16 * NSEQ)

        @block.gpsimd
        def _(pool):
            order = Order(pool, pool_order)
            link = order.link
            pool.wait_ge(const_in, 16 * CONSTS)
            order.link(nc.gpsimd.memset(eps[:], EPS))

            def inverse_deviations(it):
                pool.wait_ge(var_ready, it + 1)
                order.link(nc.gpsimd.tensor_tensor(lnt[:, 0], mv[:, :, 1], eps[:], ALU.add))
                order.link(nc.gpsimd.tensor_tensor(lnt[:, 1], lnt[:, 0], half[:], ALU.pow))
                order.link(nc.gpsimd.tensor_tensor(lnt[:, 2], lnt[:, 1], lnt[:, 1], ALU.mult))
                order.link(nc.gpsimd.tensor_tensor(lnt[:, 0], lnt[:, 2], mv[:, :, 1], ALU.mult))
                order.link(nc.gpsimd.tensor_tensor(lnt[:, 2], lnt[:, 0], eps[:], ALU.add))
                order.link(nc.gpsimd.tensor_tensor(lnt[:, 3], lnt[:, 2], half[:], ALU.pow))
                nc.gpsimd.tensor_tensor(lnt[:, 4], lnt[:, 1], lnt[:, 3], ALU.mult).then_inc(rstd_ready, 1)

            def inverse_deviation2(it):
                pool.wait_ge(var2_ready, it + 1)
                order.link(nc.gpsimd.tensor_tensor(lnt2[:, 0], mv2[:, :, 1], eps[:], ALU.add))
                nc.gpsimd.tensor_tensor(lnt2[:, 1], lnt2[:, 0], half[:], ALU.pow).then_inc(rstd2_ready, 1)

            def residuals(it):
                after(pool, h2T_in_psum, it * DC)
                for t in range(T):
                    last = nc.gpsimd.tensor_tensor(xb[:, t], x_in[:, t], rows[:, 3], ALU.add)
                for t in range(T):
                    last = nc.gpsimd.tensor_scalar(y[:, t], x_in[:, t], mv[:, t, 0:1], lnt[:, 1, t:t + 1], ALU.subtract, ALU.mult)
                last.then_inc(xb_ready, 1)

            def add_bias(it, t):
                if t == 0:
                    pool.wait_ge(gate_done, it + 1)
                link(nc.gpsimd.tensor_tensor(t1[:], gate[:, t], rows[:, 2], ALU.mult))
                link(nc.gpsimd.tensor_tensor(y[:, t], y[:, t], t1[:], ALU.add))

            def normalise(it, n):
                i = n // PAIRS1
                pool.wait_ge(inv_ready, it * NS + n + 1)
                p = prob[:, n % 4, :, keys_of(i)]
                nc.gpsimd.tensor_tensor(p, p, inv[:, n % 4].unsqueeze(2).to_broadcast([P, 2, KB])[:, :, keys_of(i)], ALU.mult).then_inc(norm_ready, 1)

            def mix(it, t):
                pool.wait_ge(mix_copied, it * T + t + 1)
                if t == 0:
                    after(pool, stored, it * 16)
                    after(pool, h2T_in_psum, it * DC)
                link(nc.gpsimd.tensor_tensor(t1[:], mixed[:, 1], mixed[:, 0], ALU.subtract))
                link(nc.gpsimd.tensor_tensor(t1[:], gate[:, t], t1[:], ALU.mult))
                link(nc.gpsimd.tensor_tensor(t1[:], t1[:], mixed[:, 0], ALU.add))

            def mix_end(it, t):
                nc.gpsimd.tensor_tensor(x1[:, t], t1[:], y[:, t], ALU.add).then_inc(x1_done, 1)
                pool.wait_ge(x1_done, it * T + t + 1)
                nc.gpsimd.tensor_tensor(res[:, t], x1[:, t], xb[:, t], ALU.add).then_inc(res_ready, 1)

            inverse_deviations(0)
            residuals(0)

            def body(it):
                order.step(it)
                for n in range(NS):
                    normalise(it, n)
                    if n in (4, 7, 10, 13):
                        add_bias(it, (n - 4) // 3)
                    if n in (18, 26):
                        mix(it, (n - 18) // 8)
                    if n in (20, 28):
                        mix_end(it, (n - 20) // 8)
                    if n == 16 and not last_step(it):
                        inverse_deviations(it + 1)
                for t in (2, 3):
                    mix(it, t)
                    mix_end(it, t)
                inverse_deviation2(it)
                if not last_step(it):
                    residuals(it + 1)

            bodies(pool, body)

        @block.scalar
        def _(act):
            act.wait_ge(const_in, 16 * CONSTS)
            act.wait_ge(const_ready, 1)

            def h_hi(it, c):
                act.wait_ge(hT_ready, it * DC + c + 1)
                after(act, in_in_psum, it)
                nc.scalar.copy(hT_hl[0][:, c], hT[:, c]).then_inc(hhi_ready, 1)

            def qk_hi(it, a, m):
                act.wait_ge(q_in_psum, (it * 2 + a) * DC + 2 - m)
                after(act, k4_in_psum, it * PAIRS1)
                nc.scalar.activation(qk_hl[a][0][:, m], ab_ps[:, m], ACT.Identity, bias=(bq, bk)[a][:, m:m + 1]).then_inc(qhi_ready, 1)

            def q4_copy(it, j):
                act.wait_ge(q4_in_psum, it * PAIRS1 + j + 1)
                after(act, s_ready, it * NS)
                nc.scalar.copy(q4[:, j], ab_ps[:, 0]).then_inc(q4_ready, 1)

            def gates(it):
                act.wait_ge(vg_ready, (it + 1) * T)
                nc.scalar.activation(gate[:], gate[:], ACT.Tanh, scale=0.5).then_inc(gate_ready, 1)

            def state_hi(it):
                act.wait_ge(state_ready, it + 1)
                after(act, mix_in_psum, it * T)
                nc.scalar.copy(state_hl[:], state[:]).then_inc(statehi_ready, 1)

            def exp(it, n):
                i = n // PAIRS1
                G = it * NS + n
                act.wait_ge(max_ready, G + 1)
                after(act, t_ready, G - 3)
                for h in range(2):
                    last = nc.scalar.activation(prob[:, n % 4, h, keys_of(i)], s_ps[:, n % 2, h, keys_of(i)], ACT.Exp, bias=nmax[:, n % 4, h:h + 1],
                                                accum_out=psum[:, n % 4, h:h + 1])
                last.then_inc(exp_ready, 1)

            def pT_copy(it, n):
                i = n // PAIRS1
                b = blocks_of(i)
                G = it * NS + n
                act.wait_ge(t_ready, G + 1)
                after(act, pv_done, G - 1)
                nc.scalar.copy(pT[:, n % 2, :, b[0]:2], t_ps[:, n % 2, :, b[0]:2]).then_inc(pT_ready, 1)

            def mix_copy(it, t):
                act.wait_ge(mix_in_psum, it * T + t + 1)
                after(act, x1_done, it * T + t)
                nc.scalar.copy(mixed[:], c_ps[:]).then_inc(mix_copied, 1)

            def ao_hi(it, t):
                act.wait_ge(pv_done, it * NS + (t + 1) * PAIRS1)
                after(act, mix_in_psum, it * T + t)
                nc.scalar.copy(aoT_hl[0][:], oT[t]).then_inc(aohi_ready, 1)

            def h2_hi(it, c):
                act.wait_ge(h2T_ready, it * DC + c + 1)
                after(act, ff_in_psum, it * MF)
                nc.scalar.copy(h2T_hl[0][:, c], h2T[:, c]).then_inc(h2hi_ready, 1)

            def gelu(it, m):
                act.wait_ge(ff_in_psum, it * MF + m + 1)
                after(act, fflo_ready, it * MF + m - 1)
                if m == 0 and not last_step(it):
                    act.wait_ge(hT_in_psum, (it + 2) * DC)
                nc.scalar.activation(ff[:, m % 2], ab_ps[:, m % 2], ACT.Gelu, bias=b1[:, m:m + 1]).then_inc(ff_ready, 1)

            def ff_hi(it, m):
                act.wait_ge(ff_ready, it * MF + m + 1)
                after(act, y_in_psum, it * MF + m - 1)
                nc.scalar.copy(ff_hl[0][:, m % 2], ff[:, m % 2]).then_inc(ffhi_ready, 1)

            def projections(it):
                for a, m in ((0, 0), (1, 1), (1, 0)):
                    qk_hi(it, a, m)

            for c in range(DC):
                h_hi(0, c)
            qk_hi(0, 0, 1)
            projections(0)

            def body(it):
                gates(it)
                nc.scalar.activation(table[:], b1[:, 0:1], ACT.Exp)
                q4_copy(it, 0)
                q4_copy(it, 1)
                for n in range(NS + LAG_T):
                    if n + 2 < PAIRS1:
                        q4_copy(it, n + 2)
                    if n < NS:
                        exp(it, n)
                    if n >= LAG_T:
                        pT_copy(it, n - LAG_T)
                    if n in (13, 21, 29):
                        ao_hi(it, (n - 13) // 8)
                    if n == 10:
                        state_hi(it)
                    if n in (18, 26, 34):
                        mix_copy(it, (n - 18) // 8)
                    if n in (29, 32) and not last_step(it):
                        h_hi(it + 1, (n - 29) // 3)
                ao_hi(it, T - 1)
                if not last_step(it):
                    qk_hi(it + 1, 0, 1)
                mix_copy(it, T - 1)
                if not last_step(it):
                    projections(it + 1)
                nc.scalar.activation(table[:], b1[:, 0:1], ACT.Gelu)
                for c in range(DC):
                    h2_hi(it, c)
                for m in range(MF):
                    gelu(it, m)
                    ff_hi(it, m)

            bodies(act, body)

        @block.vector
        def _(dve):
            order = Order(dve, dve_order)
            link = order.link
            nc.vector.memset(v[:].rearrange("p t h e -> p (t h e)"), 0.0)
            dve.wait_ge(const_in, 16 * CONSTS)
            nc.vector.tensor_copy(identb[:], ident[:])
            nc.vector.tensor_copy(maskb[:], window[:].unsqueeze(1).to_broadcast([P, 2, KB])).then_inc(const_ready, 1)

            def norm(it):
                dve.wait_ge(x_loaded, 16 * (it + 1))
                after(dve, xb_ready, it)
                for t in range(T):
                    last = nc.vector.bn_stats(stats[:, t], x_in[:, t])
                link(last)
                nc.vector.memset(carrier[:], 0.0)
                for t in range(T):
                    last = nc.vector.bn_aggr(mv[:, t], stats[:, t])
                last.then_inc(var_ready, 1)

            def hn_of(it):
                dve.wait_ge(rstd_ready, it + 1)
                after(dve, hT_in_psum, it * DC)
                for t in range(T):
                    last = nc.vector.tensor_scalar(hn[:, t], x_in[:, t], mv[:, t, 0:1], lnt[:, 4, t:t + 1], ALU.subtract, ALU.mult)
                last.then_inc(hn_ready, 1)

            def affine(it, c, src, dst, g, b, waits, done):
                dve.wait_ge(waits, it * DC + c + 1)
                nc.vector.tensor_scalar(dst[:, c], src, g[:, c:c + 1], b[:, c:c + 1], ALU.mult, ALU.add).then_inc(done, 1)

            def h_affine(it, c):
                affine(it, c, ab_ps[:, 1], hT, ln1_g, ln1_b, hT_in_psum, hT_ready)

            def h_lo(it, c):
                dve.wait_ge(hhi_ready, it * DC + c + 1)
                nc.vector.tensor_tensor(hT_hl[1][:, c], hT[:, c], hT_hl[0][:, c].bitcast(F32), ALU.subtract).then_inc(hlo_ready, 1)

            def qk_lo(it, a, m):
                dve.wait_ge(qhi_ready, (it * 2 + a) * DC + 2 - m)
                nc.vector.scalar_tensor_tensor(qk_hl[a][1][:, m], ab_ps[:, m], (bq, bk)[a][:, m:m + 1], qk_hl[a][0][:, m].bitcast(F32), ALU.add, ALU.subtract).then_inc(qlo_ready, 1)

            def values_gates(it, t):
                dve.wait_ge(vg_in_psum, it * T + t + 1)
                after(dve, pv_done, it * NS)
                after(dve, x1_done, it * T)
                heads = lambda ap: ap.rearrange("p (h e) -> p h e", e=DH1)
                nc.vector.tensor_tensor(v[:, t, :, 0:DH1], heads(ab_ps[:, t % 2, 0:D]), heads(rows[:, 0]), ALU.add)
                nc.vector.tensor_tensor(gate[:, t], ab_ps[:, t % 2, D:2 * D], rows[:, 1], ALU.add).then_inc(vg_ready, 1)

            def k4_copy(it, j):
                dve.wait_ge(k4_in_psum, it * PAIRS1 + j + 1)
                after(dve, s_ready, it * NS)
                nc.vector.tensor_copy(k4[:, j], ab_ps[:, 1]).then_inc(k4_ready, 1)

            def scan(it):
                dve.wait_ge(in_in_psum, it + 1)
                after(dve, statelo_ready, it)
                nc.vector.tensor_tensor_scan(state[:], a[:].to_broadcast([P, SEQ]), c_ps[:].rearrange("p a d -> p (a d)"), 0.0, ALU.mult, ALU.add).then_inc(state_ready, 1)

            def state_lo(it):
                dve.wait_ge(statehi_ready, it + 1)
                up = slice(STATE, P)
                nc.vector.tensor_tensor(state_hl[up], state[up], state_hl[up].bitcast(F32), ALU.subtract).then_inc(statelo_ready, 1)

            def maxima(it, n):
                i = n // (H1 // 2)
                G = it * NS + n
                dve.wait_ge(s_ready, G + 1)
                after(dve, exp_ready, G - 3)
                nc.vector.tensor_reduce(nmax[:, n % 4], s_ps[:, n % 2, :, keys_of(i)], AX.X, ALU.max, negate=True).then_inc(max_ready, 1)

            def inverse_sums(it, n):
                dve.wait_ge(exp_ready, it * NS + n + 1)
                after(dve, norm_ready, it * NS + n - 3)
                nc.vector.reciprocal(inv[:, n % 4], psum[:, n % 4]).then_inc(inv_ready, 1)

            def ao_lo(it, t):
                dve.wait_ge(aohi_ready, it * T + t + 1)
                nc.vector.tensor_tensor(aoT_hl[1][:], oT[t], aoT_hl[0][:].bitcast(F32), ALU.subtract).then_inc(aolo_ready, 1)

            def stats2_of(it, t):
                dve.wait_ge(x1_done, it * T + t + 1)
                last = nc.vector.bn_stats(stats2[:, t], x1[:, t])
                if t == T - 1:
                    link(last)

            def gate_scale(it):
                dve.wait_ge(gate_ready, it + 1)
                nc.vector.tensor_scalar(gate[:], gate[:], 1.0, 0.5, ALU.add, ALU.mult).then_inc(gate_done, 1)

            def norm2(it):
                nc.vector.memset(carrier[:], 0.0)
                for t in range(T):
                    last = nc.vector.bn_aggr(mv2[:, t], stats2[:, t])
                last.then_inc(var2_ready, 1)

            def h2n_of(it):
                dve.wait_ge(rstd2_ready, it + 1)
                dve.wait_ge(res_ready, (it + 1) * T)
                for t in range(T):
                    last = nc.vector.tensor_scalar(x1[:, t], x1[:, t], mv2[:, t, 0:1], lnt2[:, 1, t:t + 1], ALU.subtract, ALU.mult)
                last.then_inc(h2n_ready, 1)

            def h2_lo(it, c):
                dve.wait_ge(h2hi_ready, it * DC + c + 1)
                nc.vector.tensor_tensor(h2T_hl[1][:, c], h2T[:, c], h2T_hl[0][:, c].bitcast(F32), ALU.subtract).then_inc(h2lo_ready, 1)

            def ff_lo(it, m):
                dve.wait_ge(ffhi_ready, it * MF + m + 1)
                nc.vector.tensor_tensor(ff_hl[1][:, m % 2], ff[:, m % 2], ff_hl[0][:, m % 2].bitcast(F32), ALU.subtract).then_inc(fflo_ready, 1)

            def result_of(it, t):
                if t == 0:
                    dve.wait_ge(y_in_psum, (it + 1) * MF)
                    dve.wait_ge(res_ready, (it + 1) * T)
                nc.vector.tensor_tensor(res[:, t], y_ps[:, t], res[:, t], ALU.add).then_inc(result_ready, 1)

            tab = [t_ps[:, c].rearrange("p h b q -> p (h b q)") for c in range(DC)]

            def projections(it, part):
                if part == 0:
                    for a, m in ((0, 0), (1, 1), (1, 0)):
                        qk_lo(it, a, m)
                    values_gates(it, 0)
                    values_gates(it, 1)
                else:
                    values_gates(it, 2)
                    values_gates(it, 3)
                    scan(it)

            norm(0)
            hn_of(0)
            for c in range(DC):
                h_affine(0, c)
            for c in range(DC):
                h_lo(0, c)
            qk_lo(0, 0, 1)
            projections(0, 0)
            projections(0, 1)

            def body(it):
                order.step(it)
                k4_copy(it, 0)
                k4_copy(it, 1)
                for n in range(NS + 1):
                    if n + 2 < PAIRS1:
                        k4_copy(it, n + 2)
                    if n < NS:
                        maxima(it, n)
                    if n:
                        inverse_sums(it, n - 1)
                    if n == 11:
                        state_lo(it)
                    if n == 6:
                        gate_scale(it)
                    if n in (15, 23, 31):
                        ao_lo(it, (n - 15) // 8)
                    if n in (22, 30):
                        stats2_of(it, (n - 22) // 8)
                    if not last_step(it):
                        if n == 12:
                            norm(it + 1)
                        if n == 20:
                            hn_of(it + 1)
                        if n in (28, 31):
                            h_affine(it + 1, (n - 28) // 3)
                        if n in (30, 32):
                            h_lo(it + 1, (n - 30) // 2)
                ao_lo(it, T - 1)
                if not last_step(it):
                    qk_lo(it + 1, 0, 1)
                stats2_of(it, T - 2)
                if not last_step(it):
                    projections(it + 1, 0)
                stats2_of(it, T - 1)
                norm2(it)
                h2n_of(it)
                if not last_step(it):
                    projections(it + 1, 1)
                for c in range(DC):
                    affine(it, c, tab[c], h2T, ln2_g, ln2_b, h2T_in_psum, h2T_ready)
                for c in range(DC):
                    h2_lo(it, c)
                for m in range(MF):
                    ff_lo(it, m)
                for t in range(T):
                    result_of(it, t)

            bodies(dve, body)

        @block.tensor
        def _(pe):
            pe.wait_ge(const_in, 16 * CONSTS)
            pe.wait_ge(const_ready, 1)
            pe.wait_ge(lo_split, 7)

            def transpose_chunk(src, dst, c):
                for t in range(T):
                    last = nc.tensor.transpose(dst[:, t * P:(t + 1) * P], src[:, t, c * P:(c + 1) * P], ident[:])
                return last

            tab = [t_ps[:, c].rearrange("p h b q -> p (h b q)") for c in range(DC)]

            def h_transposes(it, c):
                if c == 0:
                    pe.wait_ge(hn_ready, it + 1)
                    after(pe, k4_ready, it * PAIRS1)
                else:
                    pe.wait_ge(hT_ready, it * DC + c)
                transpose_chunk(hn, ab_ps[:, 1], c).then_inc(hT_in_psum, 1)

            def feature_major(w, cols_, x_hl, out_):
                for c in range(DC):
                    last = three(nc, out_, [h[:, c, cols_] for h in w], [h[:, c] for h in x_hl], c == 0, c == DC - 1)
                return last

            def queries_keys(it, a, m):
                if a:
                    pe.wait_ge(qlo_ready, it * 2 * DC + (2 - m))
                elif m:
                    pe.wait_ge(hlo_ready, (it + 1) * DC)
                else:
                    after(pe, aolo_ready, it * T)
                feature_major(wqk, slice(a * D + m * P, a * D + (m + 1) * P), hT_hl, ab_ps[:, m]).then_inc(q_in_psum, 1)

            def spread_qk(it, j):
                c, jj = divmod(j, PAIRS1 // 2)
                if j == 0:
                    pe.wait_ge(vg_ready, (it + 1) * T)
                    after(pe, ff_ready, it * MF)
                for a, (full, free) in enumerate(((q4_in_psum, q4_ready), (k4_in_psum, k4_ready))):
                    if j:
                        pe.wait_ge(free, it * PAIRS1 + j)
                    for half_ in range(2):
                        last = nc.tensor.matmul(ab_ps[:, a], spread[:, jj, 2 * a + half_], qk_hl[a][half_][:, c], start=(half_ == 0), stop=(half_ == 1))
                    last.then_inc(full, 1)

            def values_gates(it, t):
                if t < 2:
                    pe.wait_ge(qlo_ready, (it * 2 + 1) * DC + 2 - t)
                else:
                    pe.wait_ge(vg_ready, it * T + t - 1)
                tok = slice(t * P, (t + 1) * P)
                for c in range(DC):
                    last = three(nc, ab_ps[:, t % 2], [h[:, c, tok] for h in hT_hl], [w[:, c] for w in wvg], c == 0, c == DC - 1)
                last.then_inc(vg_in_psum, 1)

            def state_input(it):
                after(pe, mix_copied, it * T)
                feature_major(bw, slice(0, P), hT_hl, c_ps[:].rearrange("p a d -> p (a d)")).then_inc(in_in_psum, 1)

            def scores(it, n):
                i, j = divmod(n, PAIRS1)
                G = it * NS + n
                if n < PAIRS1:
                    pe.wait_ge(q4_ready, it * PAIRS1 + 2 * (n // 2) + 2)
                    pe.wait_ge(k4_ready, it * PAIRS1 + 2 * (n // 2) + 2)
                if n == 0:
                    after(pe, result_ready, it * T)
                after(pe, exp_ready, G - 1)
                keys_ = slice(max(i - 1, 0) * P, (i + 1) * P)
                nc.tensor.matmul(s_ps[:, n % 2, :, keys_of(i)], identb[:], maskb[:, :, keys_of(i)], start=True, stop=False, skip_group_check=True)
                r4 = slice(j % 2 * 4 * DH1, (j % 2 + 1) * 4 * DH1)
                for h in range(2):
                    slot = 2 * (j // 2) + h
                    last = nc.tensor.matmul(s_ps[:, n % 2, h, keys_of(i)], q4[r4, slot, i * P:(i + 1) * P], k4[r4, slot, keys_], start=False, stop=(h == 1), skip_group_check=True)
                last.then_inc(s_ready, 1)

            def transposes(it, n):
                i = n // PAIRS1
                G = it * NS + n
                pe.wait_ge(norm_ready, G + 1)
                after(pe, pT_ready, G - 1)
                if n == 0:
                    after(pe, h2T_ready, it * DC)
                for h in range(2):
                    for b in blocks_of(i):
                        last = nc.tensor.transpose(t_ps[:, n % 2, h, b], prob[:, n % 4, h, b * P:(b + 1) * P], ident[:])
                last.then_inc(t_ready, 1)

            def values(it, n):
                i, j = divmod(n, H1 // 2)
                G = it * NS + n
                pe.wait_ge(pT_ready, G + 1)
                if n == 0:
                    pe.wait_ge(vg_ready, (it + 1) * T)
                if j == 0:
                    if i == 1:
                        pe.wait_ge(q4_ready, (it + 1) * PAIRS1)
                    else:
                        after(pe, aolo_ready, it * T + i - 1)
                for h in range(2):
                    g, quarter = divmod(head_of(j, h), P // ROWS)
                    for b in blocks_of(i):
                        last = nc.tensor.matmul(oT[i][quarter * ROWS:(quarter + 1) * ROWS, g], v[:, i - 1 + b, head_of(j, h)], pT[:, n % 2, h, b], start=(b == blocks_of(i)[0]), stop=(b == 1))
                last.then_inc(pv_done, 1)

            def mix(it, t):
                pe.wait_ge(aolo_ready, it * T + t + 1)
                if t:
                    pe.wait_ge(mix_copied, it * T + t)
                else:
                    pe.wait_ge(statelo_ready, it + 1)
                tok = slice(t * P, (t + 1) * P)
                nc.tensor.matmul(c_ps[:, 0], state_hl[:, tok], cw[0][:], start=True, stop=False)
                nc.tensor.matmul(c_ps[:, 0], state_hl[0:STATE, tok], cw[1][0:STATE], start=False, stop=True)
                for c in range(OC):
                    last = three(nc, c_ps[:, 1], [h[:, c] for h in aoT_hl], [w[:, c] for w in wo], c == 0, c == OC - 1)
                last.then_inc(mix_in_psum, 1)

            def h2_transposes(it):
                pe.wait_ge(h2n_ready, it + 1)
                pe.wait_ge(pT_ready, (it + 1) * NS)
                for c in range(DC):
                    transpose_chunk(x1, tab[c], c).then_inc(h2T_in_psum, 1)

            def mlp1(it, m):
                if m == 0:
                    pe.wait_ge(h2lo_ready, (it + 1) * DC)
                if m < 2:
                    pe.wait_ge(vg_ready, (it + 2) * T if not last_step(it) else NSEQ * T)
                else:
                    pe.wait_ge(ff_ready, it * MF + m - 1)
                feature_major(w1, slice(m * P, (m + 1) * P), h2T_hl, ab_ps[:, m % 2]).then_inc(ff_in_psum, 1)

            def mlp2(it, m):
                pe.wait_ge(fflo_ready, it * MF + m + 1)
                if m == 0:
                    pe.wait_ge(exp_ready, (it + 1) * NS)
                for t in range(T):
                    tok = slice(t * P, (t + 1) * P)
                    last = three(nc, y_ps[:, t], [h[:, m % 2, tok] for h in ff_hl], [w[:, m] for w in w2], m == 0 and t % 2 == 0, m == MF - 1 and t % 2 == 1, skip_group_check=True)
                last.then_inc(y_in_psum, 1)

            for c in range(DC):
                h_transposes(0, c)
            for a, m in ((0, 1), (0, 0), (1, 1), (1, 0)):
                queries_keys(0, a, m)
            for t in range(T):
                values_gates(0, t)
            state_input(0)

            def body(it):
                spread_qk(it, 0)
                spread_qk(it, 1)
                for n in range(NS + LAG_P):
                    if n + 2 < PAIRS1:
                        spread_qk(it, n + 2)
                    if n < NS:
                        scores(it, n)
                    if LAG_T <= n < NS + LAG_T:
                        transposes(it, n - LAG_T)
                    if n >= LAG_P:
                        values(it, n - LAG_P)
                    if n in (17, 25, 33):
                        mix(it, (n - 17) // 8)
                    if n in (27, 30) and not last_step(it):
                        h_transposes(it + 1, (n - 27) // 3)
                if not last_step(it):
                    queries_keys(it + 1, 0, 1)
                mix(it, T - 1)
                if not last_step(it):
                    queries_keys(it + 1, 0, 0)
                    queries_keys(it + 1, 1, 1)
                    queries_keys(it + 1, 1, 0)
                    values_gates(it + 1, 0)
                    values_gates(it + 1, 1)
                    values_gates(it + 1, 2)
                h2_transposes(it)
                if not last_step(it):
                    values_gates(it + 1, 3)
                    state_input(it + 1)
                mlp1(it, 0)
                mlp1(it, 1)
                for m in range(MF):
                    mlp2(it, m)
                    if m + 2 < MF:
                        mlp1(it, m + 2)

            bodies(pe, body)


def network(nc, x, attn0, ffn0, attn1, ffn1, out):
    between = [nc.dram_tensor(f"after_{name}", [NSEQ * SEQ, D], F32, kind="Internal").ap() for name in ("attn0", "ffn0", "attn1")]
    attn0_phase(nc, x, between[0], **attn0)
    moe_phase(nc, "b", between[0], between[1], shared=True, **ffn0)
    attn1_phase(nc, between[1], between[2], **attn1)
    moe_phase(nc, "d", between[2], out, shared=False, bias_d=None, **ffn1)




def by_chunks(w):
    import numpy as np
    return np.reshape(w, (DC, P, -1)).transpose(1, 0, 2).reshape(P, -1)


def experts_by_chunks(w):
    import numpy as np
    return np.reshape(w, (w.shape[0], DC, P, P)).transpose(2, 0, 1, 3)


def common_tables():
    import numpy as np
    return dict(half_d=np.full((P, T), -0.5, np.float32), ident_d=np.eye(P, dtype=np.float32))


def attn0_layout(w_qkv, w_out, ln_g, ln_b, mem_beta):
    import numpy as np
    f32 = np.float32
    inner = HEADS * DH
    evens_first = np.concatenate([np.arange(0, DH, 2), np.arange(1, DH, 2)])
    qk = w_qkv[:, :2 * inner].reshape(DC, P, 2, PAIRS, 2, DH)[..., evens_first].transpose(1, 2, 3, 0, 4, 5).reshape(P, -1)
    beta = mem_beta.reshape(PAIRS, 2)
    freqs = (f32(10000.0) ** (-np.arange(0, DH, 2, dtype=f32) / f32(DH))).astype(f32)
    angles = (np.arange(SEQ, dtype=f32)[None, :] * freqs[:, None]).astype(f32)
    sines = np.sin(angles).astype(f32)
    part = np.arange(P)
    head = part // DH
    sel = np.zeros((P, 2, 4), f32)
    selbc = np.zeros((8, 2, P), f32)
    for a in range(2):
        sel[part, a, 2 * a + head] = 1
        for half in range(2):
            selbc[4 * half + 2 * a + head, a, part] = 1
    return dict(
        wqk_d=qk, wv_d=by_chunks(w_qkv[:, 2 * inner:]), wo_d=w_out.reshape(PAIRS, P, D).transpose(1, 0, 2).reshape(P, -1),
        lng_d=ln_g.reshape(DC, P).T, lnb_d=ln_b.reshape(DC, P).T,
        beta_rows_d=np.repeat(beta.T, SEQ // 16, axis=0), beta_heads_d=np.broadcast_to(beta.reshape(1, HEADS), (P, HEADS)),
        cos_d=np.tile(np.cos(angles), (4, 1)).astype(f32), sin_d=np.concatenate([-sines, sines, -sines, sines]),
        mask_d=np.where(np.arange(SEG)[None, :] <= part[:, None] % SEG, 0, -1e30).astype(f32),
        sel_d=sel, selbc_d=selbc.reshape(8, -1), eps4_d=np.array([[1e-6], [1e-6], [0], [0]], f32), **common_tables())


def ffn0_layout(gate_w, correction_bias, Wg, Wu, Wd, Wg_s, Wu_s, Wd_s):
    import numpy as np
    E = gate_w.shape[0]
    wg, wu, wd = (np.concatenate([s[None], w]) for s, w in ((Wg_s, Wg), (Wu_s, Wu), (Wd_s, Wd)))
    return dict(wg_d=experts_by_chunks(wg), wu_d=experts_by_chunks(wu), wd_d=wd.transpose(1, 0, 2),
                bias_d=np.broadcast_to(correction_bias, (P, E)), **router_layout(gate_w), **common_tables())


def ffn1_layout(gate_w, w_gate, w_up, w_down):
    wg, wu, wd = (w.transpose(0, 2, 1) for w in (w_gate, w_up, w_down))
    return dict(wg_d=experts_by_chunks(wg), wu_d=experts_by_chunks(wu), wd_d=wd.transpose(1, 0, 2), **router_layout(gate_w), **common_tables())


def router_layout(gate_w):
    import numpy as np
    E = gate_w.shape[0]
    lower = np.arange(E)[None, :] < np.arange(E)[:, None]
    return dict(gate_d=by_chunks(gate_w.T).reshape(P, DC, E), lower_d=np.broadcast_to(lower.astype(np.float32), (P, E, E)))


def attn1_layout(ln1_g, ln1_b, WQ, bQ, WK, bK, WV, bV, WO, bO, Wg, bg, A, Bw, Cw, ln2_g, ln2_b, W1, b1, W2, b2):
    import numpy as np
    f32 = np.float32
    by_feature = lambda a: a.reshape(DC, P).T
    spread = np.zeros((P, 4, 4, P), f32)
    p = np.arange(P)
    quarter, s, d = p // (2 * DH1), p // DH1 % 2, p % DH1
    for r in range(4):
        m = s * 4 * DH1 + r * DH1 + d
        spread[p, quarter, r % 2, m] = DH1 ** -0.5
        spread[p, quarter, 2 + r // 2, m] = 1
    wo = np.pad(WO.reshape(H1, DH1, D), ((0, 0), (0, ROWS - DH1), (0, 0)))
    q, k = np.arange(P)[:, None], np.arange(P)[None, :]
    window = np.concatenate([np.where(k > q, 0, -1e30), np.where(k <= q, 0, -1e30)], 1).astype(f32)
    return dict(
        wqk_d=by_chunks(np.concatenate([WQ, WK], 1)), wvg_d=by_chunks(np.concatenate([WV, Wg], 1)),
        bw_d=by_chunks(np.concatenate([Bw, Bw], 1)), cw_d=np.concatenate([Cw, Cw]), wo_d=wo.reshape(OC, P, D).transpose(1, 0, 2).reshape(P, -1), spread_d=spread.reshape(P, -1), w1_d=by_chunks(W1),
        w2_d=W2.reshape(MF, P, D).transpose(1, 0, 2).reshape(P, -1),
        cols_d=np.concatenate([by_feature(ln1_g), by_feature(ln1_b), by_feature(bQ), by_feature(bK), by_feature(ln2_g), by_feature(ln2_b)], 1),
        rows_d=np.broadcast_to(np.stack([bV, bg, bO, b2]), (P, 4, D)), b1_d=b1.reshape(MF, P).T, a_d=np.concatenate([A, A])[:, None],
        window_d=window, **common_tables())


def kernel(**inputs):
    import numpy as np
    import concourse.bacc as bacc
    from concourse.bass_utils import run_bass_kernel_spmd

    arrays = {name: np.asarray(a) for name, a in inputs.items()}

    def of(prefix):
        return {name[len(prefix):]: a for name, a in arrays.items() if name.startswith(prefix)}

    x = arrays.pop("L0_attn_x")
    layouts = dict(attn0=attn0_layout(**of("L0_attn_")), ffn0=ffn0_layout(**of("L0_ffn_")),
                   attn1=attn1_layout(**of("L1_attn_")), ffn1=ffn1_layout(**of("L1_ffn_")))

    nc = bacc.Bacc("TRN2", target_bir_lowering=False, num_devices=1)
    feeds = {}

    def feed(name, a):
        feeds[name] = np.ascontiguousarray(a)
        return nc.dram_tensor(name, feeds[name].shape, mybir.dt.from_np(feeds[name].dtype), kind="ExternalInput").ap()

    x_d = feed("x", x.reshape(NSEQ * SEQ, D))
    args = {block: {name: feed(f"{block}_{name}", a) for name, a in layout.items()} for block, layout in layouts.items()}
    out = nc.dram_tensor("out_0_dram", (NSEQ * SEQ, D), F32, kind="ExternalOutput").ap()
    network(nc, x_d, out=out, **args)
    result = run_bass_kernel_spmd(nc, [feeds], core_ids=[0])
    return result.results[0]["out_0_dram"].reshape(x.shape)
```
